# Optimizing a Trainium2 kernel written in Bass

```python
import numpy as np
import jax
import jax.numpy as jnp

def _softmax(x, axis=-1):
    return jax.nn.softmax(x, axis=axis)

def _gelu(x):
    return jax.nn.gelu(x, approximate=True)

def _silu(x):
    return jax.nn.silu(x)

def _sigmoid(x):
    return jax.nn.sigmoid(x)

def _layernorm(x, axis=-1, eps=1e-05):
    m = jnp.mean(x, axis=axis, keepdims=True)
    v = jnp.var(x, axis=axis, keepdims=True)
    return (x - m) / jnp.sqrt(v + eps)

def _scatter_add(tgt, idx, src, axis=0):
    return tgt.at[idx].add(src)

def _segment_sum(src, seg, n):
    return jax.ops.segment_sum(src, seg, n)
kernel_name = 'mk_lm_tower_d1_tok_ids1024_r4_fa41df'

def setup_inputs(seed: int=0):
    np.random.seed(seed)
    _w = jnp.asarray

    def _rec_inputs():
        import jax
        import jax.numpy as jnp
        _rk = jax.random.key(seed)
        x = jax.random.randint(jax.random.fold_in(_rk, 1), (16, 256), 0, 31993, jnp.int32)
        return x
    x = _rec_inputs()

    def _L0_tok_setup():
        import jax, jax.numpy as jnp
        import numpy as np
        V, D, B, L = (8000, 256, 4, 512)

        def _make_pe(max_len, d_model):
            pos = np.arange(max_len, dtype=np.float32)[:, None]
            wk = np.exp(np.arange(0, d_model, 2, dtype=np.float32) * -(np.log(10000.0) / d_model))
            pe = np.zeros((max_len, d_model), dtype=np.float32)
            pe[:, 0::2] = np.sin(pos * wk)
            pe[:, 1::2] = np.cos(pos * wk)
            return jnp.asarray(pe)
        key = jax.random.key(seed)
        k0, k1, k2, k3, k4 = jax.random.split(key, 5)
        tokens = jax.random.randint(k0, (B, L), 0, V)
        emb = jax.random.normal(k1, (V, D), dtype=jnp.float32) * 0.02
        emb = emb.at[0].set(0.0)
        w_q = jax.random.normal(k2, (D, D), dtype=jnp.float32) * 0.02
        w_k = jax.random.normal(k3, (D, D), dtype=jnp.float32) * 0.02
        w_v = jax.random.normal(k4, (D, D), dtype=jnp.float32) * 0.02
        return {'tokens': tokens, 'emb': emb, 'w_q': w_q, 'w_k': w_k, 'w_v': w_v, 'pos_enc': _make_pe(L, D)}
    _L0_tok_all = _L0_tok_setup()
    _L0_tok_in = {k: v for k, v in _L0_tok_all.items() if k in ('emb', 'w_q', 'w_k', 'w_v', 'pos_enc')}
    del _L0_tok_all

    def _L0_attn_setup():
        import jax, jax.numpy as jnp
        import numpy as np
        D_MODEL = 256
        D_STATE = 128
        D_CONV = 4
        EXPAND = 2
        HEADDIM = 64
        D_INNER = EXPAND * D_MODEL
        NHEADS = D_INNER // HEADDIM
        CONV_CH = D_INNER + 2 * D_STATE
        D_IN_PROJ = 2 * D_INNER + 2 * D_STATE + NHEADS
        CHUNK = 128

        def segsum(a):
            T = a.shape[-1]
            a_rep = jnp.broadcast_to(a[..., :, None], a.shape + (T,))
            a_masked = jnp.where(jnp.tril(jnp.ones((T, T), bool), -1), a_rep, 0.0)
            seg = jnp.cumsum(a_masked, axis=-2)
            return jnp.where(jnp.tril(jnp.ones((T, T), bool), 0), seg, -jnp.inf)

        def _ssd(X, a, Bm, Cm):
            b, l, h, p = X.shape
            c = l // CHUNK
            Xc = X.reshape(b, c, CHUNK, h, p)
            Bc = Bm.reshape(b, c, CHUNK, -1)
            Cc = Cm.reshape(b, c, CHUNK, -1)
            ac = a.reshape(b, c, CHUNK, h).transpose(0, 3, 1, 2)
            a_cs = jnp.cumsum(ac, axis=-1)
            Lm = jnp.exp(segsum(ac))
            Y_diag = jnp.einsum('bcln,bcsn,bhcls,bcshp->bclhp', Cc, Bc, Lm, Xc)
            decay_states = jnp.exp(a_cs[..., -1:] - a_cs)
            states = jnp.einsum('bcln,bhcl,bclhp->bchpn', Bc, decay_states, Xc)
            states = jnp.concatenate([jnp.zeros_like(states[:, :1]), states], axis=1)
            a_chunk = jnp.pad(a_cs[..., -1], ((0, 0), (0, 0), (1, 0)))
            decay_chunk = jnp.exp(segsum(a_chunk))
            prev_states = jnp.einsum('bhzc,bchpn->bzhpn', decay_chunk, states)[:, :-1]
            Y_off = jnp.einsum('bcln,bchpn,bhcl->bclhp', Cc, prev_states, jnp.exp(a_cs))
            return (Y_diag + Y_off).reshape(b, l, h, p)
        key = jax.random.key(seed)
        ks = jax.random.split(key, 8)
        B, L = (4, 512)
        return {'x': jax.random.normal(ks[0], (B, L, D_MODEL), jnp.float32), 'ln_w': jnp.ones((D_MODEL,), jnp.float32), 'ln_b': jnp.zeros((D_MODEL,), jnp.float32), 'in_proj_w': jax.random.normal(ks[1], (D_IN_PROJ, D_MODEL), jnp.float32) * 0.02, 'conv_w': jax.random.normal(ks[2], (CONV_CH, D_CONV), jnp.float32) * 0.2, 'conv_b': jnp.zeros((CONV_CH,), jnp.float32), 'dt_bias': jax.random.normal(ks[3], (NHEADS,), jnp.float32) * 0.5, 'A_log': jax.random.uniform(ks[4], (NHEADS,), jnp.float32, 0.0, 1.5), 'D': jax.random.normal(ks[5], (NHEADS,), jnp.float32) * 0.1 + 1.0, 'norm_w': jnp.ones((D_INNER,), jnp.float32), 'out_proj_w': jax.random.normal(ks[6], (D_MODEL, D_INNER), jnp.float32) * 0.02}
    _L0_attn_all = _L0_attn_setup()
    _L0_attn_in = {k: v for k, v in _L0_attn_all.items() if k in ('ln_w', 'ln_b', 'in_proj_w', 'conv_w', 'conv_b', 'dt_bias', 'A_log', 'D', 'norm_w', 'out_proj_w')}
    del _L0_attn_all

    def _L0_ffn_setup():
        import jax, jax.numpy as jnp
        import numpy as np
        TOP_K = 2
        CAPACITY_FACTOR = 1.0
        key = jax.random.key(seed)
        ks = jax.random.split(key, 4)
        sl, bs, hs, ffn, E = (512, 8, 256, 1024, 8)
        x = jax.random.normal(ks[0], (sl, bs, hs), dtype=jnp.float32)
        w_router = jax.random.normal(ks[1], (hs, E), dtype=jnp.float32) * 0.02
        w1 = jax.random.normal(ks[2], (E, hs, ffn), dtype=jnp.float32) * 0.02
        w2 = jax.random.normal(ks[3], (E, ffn, hs), dtype=jnp.float32) * 0.02
        bias = jnp.zeros((1, 1, hs), dtype=jnp.float32)
        return {'x': x, 'w_router': w_router, 'w1': w1, 'w2': w2, 'bias': bias}
    _L0_ffn_all = _L0_ffn_setup()
    _L0_ffn_in = {k: v for k, v in _L0_ffn_all.items() if k in ('w_router', 'w1', 'w2', 'bias')}
    del _L0_ffn_all
    return {'x': x, 'L0_tok_emb': _L0_tok_in['emb'], 'L0_tok_w_q': _L0_tok_in['w_q'], 'L0_tok_w_k': _L0_tok_in['w_k'], 'L0_tok_w_v': _L0_tok_in['w_v'], 'L0_tok_pos_enc': _L0_tok_in['pos_enc'], 'L0_attn_ln_w': _L0_attn_in['ln_w'], 'L0_attn_ln_b': _L0_attn_in['ln_b'], 'L0_attn_in_proj_w': _L0_attn_in['in_proj_w'], 'L0_attn_conv_w': _L0_attn_in['conv_w'], 'L0_attn_conv_b': _L0_attn_in['conv_b'], 'L0_attn_dt_bias': _L0_attn_in['dt_bias'], 'L0_attn_A_log': _L0_attn_in['A_log'], 'L0_attn_D': _L0_attn_in['D'], 'L0_attn_norm_w': _L0_attn_in['norm_w'], 'L0_attn_out_proj_w': _L0_attn_in['out_proj_w'], 'L0_ffn_w_router': _L0_ffn_in['w_router'], 'L0_ffn_w1': _L0_ffn_in['w1'], 'L0_ffn_w2': _L0_ffn_in['w2'], 'L0_ffn_bias': _L0_ffn_in['bias']}

def reference(x, L0_tok_emb, L0_tok_w_q, L0_tok_w_k, L0_tok_w_v, L0_tok_pos_enc, L0_attn_ln_w, L0_attn_ln_b, L0_attn_in_proj_w, L0_attn_conv_w, L0_attn_conv_b, L0_attn_dt_bias, L0_attn_A_log, L0_attn_D, L0_attn_norm_w, L0_attn_out_proj_w, L0_ffn_w_router, L0_ffn_w1, L0_ffn_w2, L0_ffn_bias):
    import jax
    import jax.numpy as jnp

    def _L0_tok_ref(tokens, emb, w_q, w_k, w_v, pos_enc):
        import jax, jax.numpy as jnp
        import numpy as np
        V, D, B, L = (8000, 256, 4, 512)

        def _make_pe(max_len, d_model):
            pos = np.arange(max_len, dtype=np.float32)[:, None]
            wk = np.exp(np.arange(0, d_model, 2, dtype=np.float32) * -(np.log(10000.0) / d_model))
            pe = np.zeros((max_len, d_model), dtype=np.float32)
            pe[:, 0::2] = np.sin(pos * wk)
            pe[:, 1::2] = np.cos(pos * wk)
            return jnp.asarray(pe)
        d_model = emb.shape[1]
        x = emb[tokens] * jnp.sqrt(jnp.float32(d_model)) + pos_enc[:tokens.shape[1], :]
        q = jnp.einsum('bld,de->ble', x, w_q)
        k = jnp.einsum('bld,de->ble', x, w_k)
        v = jnp.einsum('bld,de->ble', x, w_v)
        qk = jnp.einsum('bqd,bkd->bqk', q, k) / jnp.sqrt(jnp.float32(d_model))
        s_qk = jax.nn.softmax(qk, axis=1)
        return jnp.einsum('bqk,bkd->bqd', s_qk, v)

    def _L0_attn_ref(x, ln_w, ln_b, in_proj_w, conv_w, conv_b, dt_bias, A_log, D, norm_w, out_proj_w):
        import jax, jax.numpy as jnp
        import numpy as np
        D_MODEL = 256
        D_STATE = 128
        D_CONV = 4
        EXPAND = 2
        HEADDIM = 64
        D_INNER = EXPAND * D_MODEL
        NHEADS = D_INNER // HEADDIM
        CONV_CH = D_INNER + 2 * D_STATE
        D_IN_PROJ = 2 * D_INNER + 2 * D_STATE + NHEADS
        CHUNK = 128

        def segsum(a):
            T = a.shape[-1]
            a_rep = jnp.broadcast_to(a[..., :, None], a.shape + (T,))
            a_masked = jnp.where(jnp.tril(jnp.ones((T, T), bool), -1), a_rep, 0.0)
            seg = jnp.cumsum(a_masked, axis=-2)
            return jnp.where(jnp.tril(jnp.ones((T, T), bool), 0), seg, -jnp.inf)

        def _ssd(X, a, Bm, Cm):
            b, l, h, p = X.shape
            c = l // CHUNK
            Xc = X.reshape(b, c, CHUNK, h, p)
            Bc = Bm.reshape(b, c, CHUNK, -1)
            Cc = Cm.reshape(b, c, CHUNK, -1)
            ac = a.reshape(b, c, CHUNK, h).transpose(0, 3, 1, 2)
            a_cs = jnp.cumsum(ac, axis=-1)
            Lm = jnp.exp(segsum(ac))
            Y_diag = jnp.einsum('bcln,bcsn,bhcls,bcshp->bclhp', Cc, Bc, Lm, Xc)
            decay_states = jnp.exp(a_cs[..., -1:] - a_cs)
            states = jnp.einsum('bcln,bhcl,bclhp->bchpn', Bc, decay_states, Xc)
            states = jnp.concatenate([jnp.zeros_like(states[:, :1]), states], axis=1)
            a_chunk = jnp.pad(a_cs[..., -1], ((0, 0), (0, 0), (1, 0)))
            decay_chunk = jnp.exp(segsum(a_chunk))
            prev_states = jnp.einsum('bhzc,bchpn->bzhpn', decay_chunk, states)[:, :-1]
            Y_off = jnp.einsum('bcln,bchpn,bhcl->bclhp', Cc, prev_states, jnp.exp(a_cs))
            return (Y_diag + Y_off).reshape(b, l, h, p)
        B, L, _ = x.shape
        mu = x.mean(-1, keepdims=True)
        var = ((x - mu) ** 2).mean(-1, keepdims=True)
        h = (x - mu) / jnp.sqrt(var + 1e-05) * ln_w + ln_b
        zxbcdt = h @ in_proj_w.T
        z = zxbcdt[..., :D_INNER]
        xBC = zxbcdt[..., D_INNER:D_INNER + CONV_CH]
        dt = jax.nn.softplus(zxbcdt[..., -NHEADS:] + dt_bias)
        xp = jnp.pad(xBC, ((0, 0), (D_CONV - 1, 0), (0, 0)))
        conv = sum((xp[:, k:k + L, :] * conv_w[:, k] for k in range(D_CONV))) + conv_b
        xBC = jax.nn.silu(conv)
        xs = xBC[..., :D_INNER].reshape(B, L, NHEADS, HEADDIM)
        Bm = xBC[..., D_INNER:D_INNER + D_STATE]
        Cm = xBC[..., D_INNER + D_STATE:]
        A = -jnp.exp(A_log)
        Y = _ssd(xs * dt[..., None], dt * A, Bm, Cm)
        Y = Y + D[None, None, :, None] * xs
        y = Y.reshape(B, L, D_INNER)
        y = y * jax.nn.silu(z)
        y = y * jax.lax.rsqrt(jnp.mean(y * y, -1, keepdims=True) + 1e-05) * norm_w
        out = y @ out_proj_w.T
        return out + x

    def _L0_ffn_ref(x, w_router, w1, w2, bias):
        import jax, jax.numpy as jnp
        import numpy as np
        TOP_K = 2
        CAPACITY_FACTOR = 1.0
        sl, bs, hs = x.shape
        E = w_router.shape[1]
        xf = x.reshape(-1, hs)
        T = xf.shape[0]
        capacity = int(CAPACITY_FACTOR * TOP_K * T / E)
        scores = jax.nn.softmax(xf @ w_router, axis=-1)
        expert_weights, top_experts = jax.lax.top_k(scores, TOP_K)
        flat_e = top_experts.reshape(-1)
        flat_w = expert_weights.reshape(-1)
        N = flat_e.shape[0]
        order = jnp.argsort(flat_e, stable=True)
        bin_ids = flat_e[order]
        tpe = jnp.zeros((E,), jnp.int32).at[flat_e].add(1)
        starts = jnp.cumsum(tpe) - tpe
        offsets = jnp.arange(N) - starts[bin_ids]
        valid = offsets < capacity
        slot = jnp.where(valid, bin_ids * capacity + offsets, E * capacity)
        src = order // TOP_K
        xb = jnp.zeros((E * capacity + 1, hs), x.dtype).at[slot].set(xf[src])
        xb = xb[:-1].reshape(E, capacity, hs)
        h = jax.nn.gelu(jnp.einsum('ech,ehf->ecf', xb, w1))
        y = jnp.einsum('ecf,efh->ech', h, w2).reshape(E * capacity, hs)
        yv = jnp.where(valid[:, None], y[jnp.minimum(slot, E * capacity - 1)], 0.0)
        out = jnp.zeros((T, hs), x.dtype).at[src].add(flat_w[order][:, None] * yv)
        return out.reshape(sl, bs, hs) + bias
    h = _L0_tok_ref(x, L0_tok_emb, L0_tok_w_q, L0_tok_w_k, L0_tok_w_v, L0_tok_pos_enc)
    h = h + _L0_attn_ref(_layernorm(h, axis=-1), L0_attn_ln_w, L0_attn_ln_b, L0_attn_in_proj_w, L0_attn_conv_w, L0_attn_conv_b, L0_attn_dt_bias, L0_attn_A_log, L0_attn_D, L0_attn_norm_w, L0_attn_out_proj_w)
    h = h + _L0_ffn_ref(_layernorm(h, axis=-1), L0_ffn_w_router, L0_ffn_w1, L0_ffn_w2, L0_ffn_bias)
    return h

_drawn_inputs = setup_inputs


def setup_inputs(seed=0):
    import zlib

    import numpy as np

    out = dict(_drawn_inputs(seed))
    spreads = {'L0_attn_ln_w': (1.0, 0.2),
     'L0_attn_ln_b': (0.0, 0.1),
     'L0_attn_conv_b': (0.0, 0.1),
     'L0_attn_norm_w': (1.0, 0.2),
     'L0_ffn_bias': (0.0, 0.1)}
    factors = {'L0_tok_w_q': 7.272,
     'L0_tok_w_k': 5.748,
     'L0_attn_dt_bias': 6.209,
     'L0_attn_A_log': 6.495,
     'L0_ffn_w_router': 5.575,
     'L0_ffn_w1': 4.735,
     'L0_ffn_w2': 4.807}
    for name, (base, spread) in spreads.items():
        noise = np.random.default_rng([zlib.crc32(name.encode()), seed]).standard_normal(out[name].shape)
        drawn = base * np.exp(spread * noise) if base else spread * noise
        out[name] = jnp.asarray(drawn.astype(out[name].dtype))
    for name, factor in factors.items():
        out[name] = (out[name] * factor).astype(out[name].dtype)
    return out
```

```python
import concourse.bass as bass
from concourse import mybir
from contextlib import ExitStack

F32 = mybir.dt.float32
F32R = mybir.dt.float32r
BF16 = mybir.dt.bfloat16
I32 = mybir.dt.int32
U32 = mybir.dt.uint32
ALU = mybir.AluOpType
ACT = mybir.ActivationFunctionType
AX = mybir.AxisListType

P = 128
EPS = 1e-5
LOG_TERMS = [1.0 / (2 * n + 1) for n in range(7, 0, -1)]


class Signal:

    def __init__(self, sem, steps=1, credit=0):
        self.sem, self.steps, self.credit = sem, steps, credit

    def __getitem__(self, p):
        return self.sem

    def now(self, r, p, step=None):
        step = self.steps if step is None else step
        return r * (2 * self.steps) + (self.credit - 2 * self.steps + 2 * (step - 1) + p + 1)

    def before(self, r, p):
        assert self.credit == 2 * self.steps
        return r * (2 * self.steps) + (p - 1)


class DmaSignal:

    def __init__(self, sems, per_turn, credit=0):
        self.sems, self.per_turn, self.credit = sems, per_turn, credit

    def __getitem__(self, p):
        return self.sems[p]

    def now(self, r, p):
        return r * self.per_turn + self.credit

    def before(self, r, p):
        assert self.credit == self.per_turn
        return r * self.per_turn


class Chain:

    def __init__(self, eng, sem, per_turn):
        self.eng, self.sem, self.per_turn, self.count, self.r = eng, sem, per_turn, 0, None

    def mark(self, ins):
        self.count += 1
        ins.then_inc(self.sem, 1)
        return self.count

    def wait(self, count=None):
        self.eng.wait_ge(self.sem, self.value(self.count if count is None else count))

    def value(self, count):
        return count if self.r is None else self.r * self.per_turn + (count - self.per_turn)

    def close(self):
        assert self.count == self.per_turn, self.count


def hold(eng, sem, value):
    eng.wait_ge(sem, value)
    eng.sem_inc(hold.counts[eng.engine], 1)


def lm_block(nc, tokens, emb, w_qT, w_kT, w_v, pos_enc, ln_w, ln_b, in_wT, conv_w, conv_b, dt_bias, A_log,
             D_skip, norm_w, out_wT, w_router, w1, w2, bias, out, slots_dram):
    N_TILES = tokens.shape[1]
    T = N_TILES * P
    VOCAB, DM = emb.shape
    KD = DM // P
    L = 2 * P
    NB = T // L
    PAIRS = NB // 2
    DI = out_wT.shape[0]
    NH = dt_bias.shape[1]
    HD = DI // NH
    KI = DI // P
    NS = P
    CC = DI + 2 * NS
    MC = CC // P
    TAPS = conv_w.shape[2]
    NE = w_router.shape[2]
    FF = w1.shape[1]
    KF = FF // P
    CAP = 2 * T // NE
    NSLOT = NE * CAP
    JS = CAP // P
    GW = 4 * P
    NG = CAP // GW
    ROW = slots_dram.shape[1]
    C_W0, C_E0, C_TOK = DM, DM + 2, DM + 3
    assert (L, KD, MC, NS, TAPS) == (256, 2, 6, 128, 4) and NH * P == 1024 and NE == 8 and HD * NH == 4 * P

    DVE_LINKS, MOE_LINKS, N_LOADS = 115, 6, 16

    with ExitStack() as ctx:
        def sb(name, shape, dt=F32, c=ctx):
            return c.enter_context(nc.sbuf_tensor(name, shape, dt))

        def sem(name):
            return ctx.enter_context(nc.semaphore(name))

        def signal(name, steps=1, credit=0):
            return Signal(sem(name), steps, credit)

        def dma_signal(name, per_turn, credit=0):
            return DmaSignal([sem(f"{name}{p}") for p in range(2)], per_turn, credit)

        ident = sb("ident", [P, P])
        w_raw = sb("w_raw", [P, 2, KD * FF])
        zero_row = sb("zero_row", [P, ROW])
        tok_iota = sb("tok_iota", [P, 4], I32)

        first = ExitStack()
        fb = lambda name, shape, dt=F32: sb(name, shape, dt, first)
        tri = fb("tri", [P, P])
        below = fb("below", [P, P])
        before_b = fb("before_b", [P, P], BF16)
        ones_b = fb("ones_b", [P, P], BF16)
        neg_half = fb("neg_half", [P, 4])
        e_iota = fb("e_iota", [P, NE])
        tok_all = fb("tok_all", [P, N_TILES + 4], I32)
        tok_neg = fb("tok_neg", [P, N_TILES], I32)
        wqk_in = fb("wqk_in", [P, 2, KD, DM])
        wqk = fb("wqk", [P, KD, DM])
        wv = fb("wv", [P, KD, DM])
        w_in = fb("w_in", [P, KD, in_wT.shape[1]])
        w_out = fb("w_out", [P, KI, DM])
        pos = fb("pos", [P, KD, DM])
        lnw = fb("lnw", [P, KD])
        lnb = fb("lnb", [P, KD])
        cw = fb("cw", [P, MC, TAPS])
        cb = fb("cb", [P, MC])
        nw = fb("nw", [P, KI])
        dtb = fb("dtb", [P, NH])
        alog = fb("alog", [P, NH])
        neg_a = fb("neg_a", [P, NH])
        dskip = fb("dskip", [P, NH])
        wr = fb("wr", [P, KD, NE])
        bias_b = fb("bias_b", [P, DM])
        oh_sum = fb("oh_sum", [P, NE], BF16)

        def pair(name, shape, dt=F32):
            return [fb(f"{name}{p}", shape, dt) for p in range(2)]

        idx = pair("idx", [P, KD], I32)
        xg = pair("xg", [P, KD, DM])
        x = pair("x", [P, KD, DM])
        xT = pair("xT", [P, KD, L])
        tT = pair("tT", [P, KD, L])
        probs = pair("probs", [P, KD, L])
        v = pair("v", [P, KD, DM])
        hn = pair("hn", [P, KD, DM])
        hu = pair("hu", [P, KD, DM])
        hT = pair("hT", [P, KD, L])
        xc = pair("xc", [P, MC, L])
        th = pair("th", [P, 3, 2 * L])
        sz = pair("sz", [P, KD, DI])
        xs = pair("xs", [P, KD, DI])
        xdt = pair("xdt", [P, KD, DI])
        seg = pair("seg", [P, KD, NH, P])
        gm = pair("gm", [P, KD, P])
        bs = pair("bs", [P, NS])
        xdec = pair("xdec", [P, DI])
        st = pair("st", [P, DI])
        y = pair("y", [P, KD, DI])
        yT = pair("yT", [P, KD, KI, P])
        h2 = pair("h2", [P, KD, DM])
        hb = pair("hb", [P, KD, DM])
        rows = pair("rows", [P, KD, ROW])
        v2T = pair("v2T", [P, KD, L])
        nmax = pair("nmax", [P, KD]); rsum = pair("rsum", [P, KD]); rinv = pair("rinv", [P, KD])
        stats = pair("stats", [P, KD, 6]); mv = pair("mv", [P, KD, 2])
        lnv = pair("lnv", [P, 2, KD]); lnr = pair("lnr", [P, 2, KD])
        hu_s = pair("hu_s", [P, KD]); hu_b = pair("hu_b", [P, KD])
        dty = pair("dty", [P, KD, NH]); dtn = pair("dtn", [P, KD, NH]); dtw = pair("dtw", [P, KD, NH])
        dts = pair("dts", [P, KD, NH]); dtq = pair("dtq", [P, KD, NH]); dtp = pair("dtp", [P, KD, NH])
        dt_ = pair("dt_", [P, KD, NH]); a_ = pair("a_", [P, KD, NH])
        ea = pair("ea", [P, NH]); edec = pair("edec", [P, NH])
        ss = pair("ss", [P, KD]); msq = pair("msq", [P, KD]); rms = pair("rms", [P, KD])
        stats2 = pair("stats2", [P, KD, 6]); mv2 = pair("mv2", [P, KD, 2])
        lv2 = pair("lv2", [P, KD]); lr2 = pair("lr2", [P, KD])
        lmax = pair("lmax", [P, KD]); lg = pair("lg", [P, KD, NE]); le = pair("le", [P, KD, NE])
        lsum = pair("lsum", [P, KD]); linv = pair("linv", [P, KD]); pr = pair("pr", [P, KD, NE])
        top = pair("top", [P, KD, 8]); topi = pair("topi", [P, KD, 8], U32); topf = pair("topf", [P, KD, 2])
        oh = pair("oh", [P, KD, 2, NE]); ohs = pair("ohs", [P, KD, NE], BF16); ohp = pair("ohp", [P, KD, 2, NE])
        offs = pair("offs", [P, 2 * KD]); valid = pair("valid", [P, 2 * KD])
        sl = pair("sl", [P, 2 * KD]); slot = pair("slot", [P, 2 * KD], I32)
        first.close()

        second = ExitStack()
        eb = lambda name, shape, dt=F32: sb(name, shape, dt, second)
        w_hi = [eb(f"w_hi{q}", [P, 2, KD * FF], F32R) for q in range(2)]
        w_lo = [eb(f"w_lo{q}", [P, 2, KD * FF], F32R) for q in range(2)]
        xe = [eb(f"xe{q}", [P, JS, ROW]) for q in range(2)]
        xe_hi = [eb(f"xe_hi{g}", [P, KD, GW], F32R) for g in range(2)]
        xe_lo = [eb(f"xe_lo{g}", [P, KD, GW], F32R) for g in range(2)]
        hf = [eb(f"hf{g}", [P, GW]) for g in range(2)]
        h_hi = eb("h_hi", [P, KF, GW], F32R)
        h_lo = eb("h_lo", [P, KF, GW], F32R)
        ye = [eb(f"ye{q}", [P, JS, DM]) for q in range(2)]
        e_now = eb("e_now", [P, 1])
        is_first = [eb(f"is_first{q}", [P, JS]) for q in range(2)]
        wd = [eb(f"wd{q}", [P, JS]) for q in range(2)]
        w_slot = [eb(f"w_slot{q}", [P, JS]) for q in range(2)]
        tok_slot = [eb(f"tok_slot{q}", [P, JS], I32) for q in range(2)]
        second.close()

        bank = [[ctx.enter_context(nc.psum_tensor(f"bank{p}{i}", [P, 512], F32)) for i in range(4)]
                for p in range(2)]

        s_consts = sem("s_consts")
        s_tok = sem("s_tok")
        hold.counts = {nc.vector.engine: sem("dve_held"), nc.gpsimd.engine: sem("pool_held")}
        s_clamped = sem("s_clamped")
        s_masks = sem("s_masks")
        s_mask0 = sem("s_mask0")
        s_prep = sem("s_prep")
        s_nega = sem("s_nega")
        s_wqk = sem("s_wqk")
        s_template = sem("s_template")
        s_fill = sem("s_fill")
        s_dump = sem("s_dump")
        idx_ready = signal("idx_ready", 1, 2)
        gathered = dma_signal("gathered", 16 * KD, 16 * KD)
        x_ready = signal("x_ready", 1, 2)
        xT_psum = signal("xT_psum"); xT_ready = signal("xT_ready")
        tT_psum = signal("tT_psum"); v_psum = signal("v_psum"); tT_ready = signal("tT_ready")
        st_psum = signal("st_psum"); nmax_ready = signal("nmax_ready"); probs_ready = signal("probs_ready")
        v_ready = signal("v_ready"); o_psum = signal("o_psum")
        lnv_ready = signal("lnv_ready"); lnr_ready = signal("lnr_ready")
        hn_ready = signal("hn_ready"); hu_coef = signal("hu_coef"); hu_ready = signal("hu_ready")
        hnT_psum = signal("hnT_psum"); hT_ready = signal("hT_ready")
        dt_psum = signal("dt_psum"); xbc_psum = signal("xbc_psum", 3); tap_ready = signal("tap_ready", 3)
        conv_done = signal("conv_done", 3); th_ready = signal("th_ready", 3); xc_ready = signal("xc_ready", 3)
        dtn_ready = signal("dtn_ready"); dtw_ready = signal("dtw_ready"); a_ready = signal("a_ready")
        seg_in = signal("seg_in", 2)
        z_psum = signal("z_psum", 2); tz_ready = signal("tz_ready", 2); sz_ready = signal("sz_ready", 2)
        btg_psum = signal("btg_psum"); bs_ready = signal("bs_ready"); gm_ready = signal("gm_ready")
        xs_psum = signal("xs_psum", 2); xs_ready = signal("xs_ready", 2); xdt_ready = signal("xdt_ready", 2)
        seg_psum = signal("seg_psum", 4); decay_ready = signal("decay_ready", 4)
        edec_ready = signal("edec_ready"); xdec_ready = signal("xdec_ready")
        m_ready = signal("m_ready", 2); skip_ready = signal("skip_ready", 2)
        state_psum = signal("state_psum"); st_ready = signal("st_ready")
        yd_psum = signal("yd_psum", 2); yo_psum = signal("yo_psum")
        y_ready = signal("y_ready", 2); ss_ready = signal("ss_ready")
        yT_psum = signal("yT_psum", 2); yT_ready = signal("yT_ready", 2)
        msq_ready = signal("msq_ready"); rms_ready = signal("rms_ready")
        out_psum = signal("out_psum"); h2_ready = signal("h2_ready", 1, 2)
        lv2_ready = signal("lv2_ready"); lr2_ready = signal("lr2_ready")
        v2_ready = signal("v2_ready"); hb_ready = signal("hb_ready")
        hb_stored = dma_signal("hb_stored", 16, 16)
        v2T_psum = signal("v2T_psum"); v2T_ready = signal("v2T_ready", 1, 2)
        logit_psum = signal("logit_psum"); lg_ready = signal("lg_ready", 1, 2); le_ready = signal("le_ready")
        ohs_ready = signal("ohs_ready"); pos_psum = signal("pos_psum"); slot_ready = signal("slot_ready", 1, 2)
        scattered = dma_signal("scattered", 64)
        rows_free = signal("rows_free", 1, 2)
        chain_sem = sem("dve_chain")
        moe_chain_sem = sem("dve_moe_chain")
        pool_chain = sem("pool_chain")
        part_done = sem("part_done")
        w_loaded = sem("w_loaded")
        w_split = sem("w_split")
        xe_loaded = dma_signal("xe_loaded", 16)
        slot_info = sem("slot_info")
        xeT_psum = sem("xeT_psum")
        x_half = sem("x_half")
        xe_split = sem("xe_split")
        h_psum = sem("h_psum")
        hf_ready = sem("hf_ready")
        hhi_ready = sem("hhi_ready")
        hlo_ready = sem("hlo_ready")
        y_psum = sem("y_psum")
        ye_ready = sem("ye_ready")
        added = sem("added")
        expert_added = sem("expert_added")
        H_BANKS, Y0 = 4, 4 * NG

        def bc(ap, shape):
            return ap.to_broadcast(shape)

        GROUPS = (2, 0, 1)
        XBC_BANK, Z_BANK, SEG_BANK = (2, 3, 0), (2, 0), (1, 3, 0, 2)
        XS_BANK, YD_BANK, YT_BANK = (2, 1), (1, 0), (3, 1)
        PER_TURN = 2 * NG * KF
        h_bank = bank[0]
        x_bank = bank[1][0:2]
        y_bank = bank[1][2:4]

        block = ctx.enter_context(nc.Block())

        @block.sync
        def _(sp):
            sp.dma_start(tok_all[:, 0:N_TILES], tokens).then_inc(s_tok, 16)
            loads = [
                (wqk_in[:, 0, :, :], w_qT.rearrange("(k p) n -> p k n", p=P)),
                (wqk_in[:, 1, :, :], w_kT.rearrange("(k p) n -> p k n", p=P)),
                (pos[:, :, :], pos_enc.rearrange("(k p) n -> p k n", p=P)),
                (wv[:, :, :], w_v.rearrange("(k p) n -> p k n", p=P)),
                (w_in[:, :, :], in_wT.rearrange("(k p) n -> p k n", p=P)),
                (w_out[:, :, :], out_wT.rearrange("(k p) n -> p k n", p=P)),
                (lnw[:, :], ln_w), (lnb[:, :], ln_b), (cw[:, :, :], conv_w), (cb[:, :], conv_b),
                (nw[:, :], norm_w), (wr[:, :, :], w_router),
                (dtb[:, :], bc(dt_bias, [P, NH])), (alog[:, :], bc(A_log, [P, NH])),
                (dskip[:, :], bc(D_skip, [P, NH])), (bias_b[:, :], bc(bias, [P, DM])),
            ]
            assert len(loads) == N_LOADS
            for dst, src in loads:
                sp.dma_start(dst, src).then_inc(s_consts, 16)
            sp.wait_ge(s_template, 1)
            sp.dma_start(slots_dram.rearrange("(n p) c -> p n c", p=P),
                         zero_row[:, :].unsqueeze(1).to_broadcast([P, NSLOT // P, ROW])).then_inc(s_fill, 16)
            sp.dma_start(out[T:T + P, :], zero_row[:, 0:DM]).then_inc(s_dump, 16)
            sp.dma_start(w_raw[:, 0, :].rearrange("p (k f) -> p k f", k=KD),
                         w1[0:DM, :].rearrange("(k p) f -> p k f", p=P)).then_inc(w_loaded, 16)
            sp.dma_start(w_raw[:, 1, :].rearrange("p (k f) -> p k f", k=KF),
                         w2[0:FF, :].rearrange("(k p) f -> p k f", p=P)).then_inc(w_loaded, 16)
            with sp.Fori(1, PAIRS + 1) as r:
                for p in range(2):
                    sp.wait_ge(hb_ready[p], hb_ready.now(r, p))
                    sp.dma_start(out[bass.ds(r * (2 * L) + (p * L - 2 * L), L), :]
                                 .rearrange("(k p) n -> p k n", p=P), hb[p][:, :, :]).then_inc(hb_stored[p], 16)
            for p in range(2):
                sp.wait_ge(scattered[p], 64 * PAIRS)
                sp.wait_ge(hb_stored[p], 16 * (PAIRS + 1))
            sp.wait_ge(s_dump, 16)

            sp.wait_ge(part_done, 4)

            def load_weights(e):
                sp.wait_ge(w_split, e * 2)
                sp.dma_start(w_raw[:, 0, :].rearrange("p (k f) -> p k f", k=KD),
                             w1[bass.ds(e * DM, DM), :].rearrange("(k p) f -> p k f", p=P)).then_inc(w_loaded, 16)
                sp.dma_start(w_raw[:, 1, :].rearrange("p (k f) -> p k f", k=KF),
                             w2[bass.ds(e * FF, FF), :].rearrange("(k p) f -> p k f", p=P)).then_inc(w_loaded, 16)

            def load_slots(e, q):
                sp.dma_start(xe[q][:, :, :], slots_dram[bass.ds(e * CAP, CAP), :]
                             .rearrange("(j p) c -> p j c", p=P)).then_inc(xe_loaded[q], 16)

            for q in range(2):
                load_slots(q, q)
            with sp.Fori(1, NE // 2) as r:
                for q in range(2):
                    e = r * 2 + (q - 1)
                    load_weights(e)
                    sp.wait_ge(xeT_psum, e * NG)
                    sp.wait_ge(slot_info, e)
                    load_slots(e + 1, q)
            load_weights(NE - 1)
            sp.wait_ge(added, 16 * NE * JS)
            sp.wait_ge(expert_added, 2 + NE)

        @block.gpsimd
        def _(pool):
            g = nc.gpsimd
            g.memset(zero_row[:, :], 0.0)
            for m, val in ((ident, 0.0), (tri, 1.0), (below, 1.0), (before_b, 1.0), (ones_b, 1.0)):
                g.memset(m[:, :], val)
            g.memset(neg_half[:, :], -0.5)
            g.memset(oh_sum[:, :], 0.0)
            g.memset(tok_all[:, N_TILES:], 0).then_inc(s_mask0, 1)
            pool.wait_ge(s_mask0, 1)
            g.affine_select(out=ident[:, :], in_=ident[:, :], compare_op=ALU.not_equal, fill=1.0, base=0,
                            pattern=[[-1, P]], channel_multiplier=1)
            g.affine_select(out=tri[:, :], in_=tri[:, :], compare_op=ALU.is_ge, fill=0.0, base=0,
                            pattern=[[1, P]], channel_multiplier=-1)
            g.affine_select(out=below[:, :], in_=below[:, :], compare_op=ALU.is_gt, fill=0.0, base=0,
                            pattern=[[-1, P]], channel_multiplier=1)
            g.affine_select(out=before_b[:, :], in_=before_b[:, :], compare_op=ALU.is_gt, fill=0.0, base=0,
                            pattern=[[1, P]], channel_multiplier=-1)
            g.iota(e_iota[:, :], pattern=[[1, NE]], base=0, channel_multiplier=0,
                   allow_small_or_imprecise_dtypes=True)
            g.iota(tok_iota[:, :], pattern=[[P, 4]], base=0, channel_multiplier=1).then_inc(s_masks, 1)
            g.iota(zero_row[:, C_TOK:C_TOK + 1].bitcast(I32), pattern=[[0, 1]], base=T,
                   channel_multiplier=1).then_inc(s_template, 1)

            def take_tokens(p, col):
                g.tensor_copy(idx[p][:, :], tok_all[:, bass.ds(col, KD)]).then_inc(idx_ready[p], 1)

            def gather(p):
                for c in range(KD):
                    g.indirect_dma_start(xg[p][:, c, :], None, emb,
                                         bass.IndirectOffsetOnAxis(ap=idx[p][:, c:c + 1], axis=0))\
                        .then_inc(gathered[p], 16)

            pool.wait_ge(s_clamped, 1)
            for p in range(2):
                take_tokens(p, KD * p)
            for p in range(2):
                pool.wait_ge(idx_ready[p], p + 1)
                gather(p)
            for p in range(2):
                pool.sem_inc(hb_stored[p], hb_stored.credit)
            pool.sem_inc(rows_free.sem, rows_free.credit)
            pool.wait_ge(s_masks, 1)
            pool.wait_ge(s_consts, 16 * N_LOADS)
            pool.wait_ge(s_fill, 16)
            with g.Fori(1, PAIRS + 1) as r:
                for p in range(2):
                    hold(pool, x_ready[p], x_ready.before(r, p))
                    hold(pool, gathered[p], gathered.before(r, p))
                    take_tokens(p, r * (2 * KD) + KD * p)
                for p in range(2):
                    hold(pool, idx_ready[p], idx_ready.now(r, p))
                    gather(p)
                for p in range(2):
                    pool.wait_ge(lnv_ready[p], lnv_ready.now(r, p))
                    g.tensor_tensor(lnr[p][:, :, :].rearrange("p a c -> p (a c)"),
                                    lnv[p][:, :, :].rearrange("p a c -> p (a c)"),
                                    neg_half[:, :], ALU.pow).then_inc(lnr_ready[p], 1)
                for c in range(KD):
                    for p in range(2):
                        pool.wait_ge(a_ready[p], a_ready.now(r, p))
                        g.tensor_tensor(seg[p][:, c, :, :], bc(tri[:, :].unsqueeze(1), [P, NH, P]),
                                        bc(a_[p][:, c, :].unsqueeze(2), [P, NH, P]), ALU.mult)\
                            .then_inc(seg_in[p], 1)
                for p in range(2):
                    pool.wait_ge(edec_ready[p], edec_ready.now(r, p))
                    pool.wait_ge(xdt_ready[p], xdt_ready.now(r, p, 1))
                    g.tensor_tensor(xdec[p][:, :].rearrange("p (h d) -> p h d", h=NH),
                                    xdt[p][:, 0, :].rearrange("p (h d) -> p h d", h=NH),
                                    bc(edec[p][:, :].unsqueeze(2), [P, NH, HD]), ALU.mult)\
                        .then_inc(xdec_ready[p], 1)
                for c in range(KD):
                    for p in range(2):
                        pool.wait_ge(xs_ready[p], xs_ready.now(r, p, c + 1))
                        g.tensor_tensor(xs[p][:, c, :].rearrange("p (h d) -> p h d", h=NH),
                                        xs[p][:, c, :].rearrange("p (h d) -> p h d", h=NH),
                                        bc(dskip[:, :].unsqueeze(2), [P, NH, HD]), ALU.mult)\
                            .then_inc(skip_ready[p], 1)
                for p in range(2):
                    pool.wait_ge(msq_ready[p], msq_ready.now(r, p))
                    g.tensor_tensor(rms[p][:, :], msq[p][:, :], neg_half[:, 0:KD], ALU.pow).then_inc(rms_ready[p], 1)
                for p in range(2):
                    pool.wait_ge(lv2_ready[p], lv2_ready.now(r, p))
                    g.tensor_tensor(lr2[p][:, :], lv2[p][:, :], neg_half[:, 0:KD], ALU.pow).then_inc(lr2_ready[p], 1)
                for p in range(2):
                    pool.wait_ge(hb_stored[p], hb_stored.before(r, p))
                    pool.wait_ge(h2_ready[p], h2_ready.now(r, p))
                    g.tensor_tensor(hb[p][:, :, :], h2[p][:, :, :], bc(bias_b[:, :].unsqueeze(1), [P, KD, DM]),
                                    ALU.add).then_inc(hb_ready[p], 1)
                for p in range(2):
                    hold(pool, slot_ready[p], slot_ready.now(r, p))
                    for c in range(KD):
                        for k in range(2):
                            g.indirect_dma_start(
                                slots_dram, bass.IndirectOffsetOnAxis(ap=slot[p][:, 2 * c + k:2 * c + k + 1], axis=0),
                                rows[p][:, c, :], None, bounds_check=NSLOT - 1, oob_is_err=False)\
                                .then_inc(scattered[p], 16)
                for p in range(2):
                    pool.wait_ge(scattered[p], scattered.now(r, p))
                    pool.sem_inc(rows_free[p], 1)
            for p in range(2):
                pool.wait_ge(gathered[p], gathered.credit * (PAIRS + 1))

            pool.drain().then_inc(part_done, 1)

            pool.wait_ge(part_done, 4)
            pool.sem_inc(expert_added, 2)

            def split_weights(n, q):
                hold(pool, w_loaded, n * 32)
                hold(pool, y_psum, n * (2 * NG))
                g.tensor_copy(w_hi[q][:, :, :], w_raw[:, :, :]).then_inc(w_split, 1)
                pool.wait_ge(w_split, n * 2 - 1)
                g.tensor_tensor(w_lo[q][:, :, :], w_raw[:, :, :], w_hi[q][:, :, :].bitcast(F32), ALU.subtract)\
                    .then_inc(w_split, 1)

            def add_results(n, q):
                for j in range(JS):
                    if j % 2 == 0:
                        hold(pool, ye_ready, n * (JS // 2) + (2 + j // 2 + 1 - JS // 2))
                    g.indirect_dma_start(out, bass.IndirectOffsetOnAxis(ap=tok_slot[q][:, j:j + 1], axis=0),
                                         ye[q][:, j, :], None, compute_op=ALU.add).then_inc(added, 16)
                    hold(pool, added, n * (16 * JS) + (16 * j + 16 - 16 * JS))
                pool.sem_inc(expert_added, 1)

            split_weights(1, 0)
            with g.Fori(1, NE // 2) as r:
                for q in range(2):
                    split_weights(r * 2 + q, 1 - q)
                    add_results(r * 2 + (q - 1), q)
            split_weights(NE, 1)
            add_results(NE - 1, 0)
            add_results(NE, 1)

        @block.scalar
        def _(act):
            sc = nc.scalar
            act.wait_ge(s_consts, 16 * N_LOADS)
            sc.activation(neg_a[:, :], alog[:, :], ACT.Exp).then_inc(s_nega, 1)
            act.wait_ge(s_wqk, 1)
            sc.activation(wqk[:, :, :].rearrange("p k n -> p (k n)"), bank[0][0][:, :], ACT.Copy,
                          scale=float(DM) ** -0.5).then_inc(s_wqk, 1)

            def copy(dst, src, signal_, func=ACT.Copy, **kw):
                sc.activation(dst, src, func, **kw).then_inc(signal_, 1)

            def flat(t):
                return t.rearrange("p a b -> p (a b)")

            act.sem_inc(v2T_ready.sem, v2T_ready.credit)
            with sc.Fori(1, PAIRS + 1) as r:
                for p in range(2):
                    act.wait_ge(xT_psum[p], xT_psum.now(r, p))
                    copy(flat(xT[p][:, :, :]), bank[p][0][:, :], xT_ready[p])
                for p in range(2):
                    act.wait_ge(tT_psum[p], tT_psum.now(r, p))
                    copy(flat(tT[p][:, :, :]), bank[p][1][:, :], tT_ready[p])
                for p in range(2):
                    act.wait_ge(nmax_ready[p], nmax_ready.now(r, p))
                    for c in range(KD):
                        ins = sc.activation(probs[p][:, c, :], bank[p][3][:, c * L:(c + 1) * L], ACT.Exp,
                                            bias=nmax[p][:, c:c + 1], accum_out=rsum[p][:, c:c + 1])
                    ins.then_inc(probs_ready[p], 1)
                for p in range(2):
                    act.wait_ge(hu_coef[p], hu_coef.now(r, p))
                    act.wait_ge(hn_ready[p], hn_ready.now(r, p))
                    for c in range(KD):
                        ins = sc.activation(hu[p][:, c, :], bank[p][0][:, c * DM:(c + 1) * DM], ACT.Identity,
                                            scale=hu_s[p][:, c:c + 1], bias=hu_b[p][:, c:c + 1])
                    ins.then_inc(hu_ready[p], 1)
                for p in range(2):
                    act.wait_ge(hnT_psum[p], hnT_psum.now(r, p))
                    for k in range(KD):
                        ins = sc.activation(hT[p][:, k, :], bank[p][1][:, k * L:(k + 1) * L], ACT.Identity,
                                            scale=lnw[:, k:k + 1], bias=lnb[:, k:k + 1])
                    ins.then_inc(hT_ready[p], 1)
                for p in range(2):
                    act.wait_ge(dtn_ready[p], dtn_ready.now(r, p))
                    copy(flat(dtw[p][:, :, :]), flat(dtn[p][:, :, :]), dtw_ready[p], ACT.Exp)

                def last_tap(p, i):
                    j = GROUPS[i]
                    act.wait_ge(xbc_psum[p], xbc_psum.now(r, p, i + 1))
                    for h in range(2):
                        m = 2 * j + h
                        ins = sc.activation(xc[p][:, m, :], bank[p][XBC_BANK[i]][:, h * L:(h + 1) * L], ACT.Identity,
                                            scale=cw[:, m, TAPS - 1:TAPS], bias=cb[:, m:m + 1])
                    ins.then_inc(tap_ready[p], 1)

                def tanh_conv(p, i):
                    j = GROUPS[i]
                    act.wait_ge(conv_done[p], conv_done.now(r, p, i + 1))
                    copy(th[p][:, j, :], flat(xc[p][:, 2 * j:2 * j + 2, :]), th_ready[p], ACT.Tanh)

                def tanh_z(p, c):
                    act.wait_ge(z_psum[p], z_psum.now(r, p, c + 1))
                    copy(sz[p][:, c, :], bank[p][Z_BANK[c]][:, :], tz_ready[p], ACT.Tanh)

                def decay(p, i):
                    act.wait_ge(seg_psum[p], seg_psum.now(r, p, i + 1))
                    c, half = i // 2, i % 2
                    copy(seg[p][:, c, 4 * half:4 * half + 4, :].rearrange("p h l -> p (h l)"),
                         bank[p][SEG_BANK[i]][:, :], decay_ready[p], ACT.Exp)

                def x_rows(p, c):
                    act.wait_ge(xs_psum[p], xs_psum.now(r, p, c + 1))
                    copy(xs[p][:, c, :], bank[p][XS_BANK[c]][:, :], xs_ready[p])

                for i in range(3):
                    for p in range(2):
                        last_tap(p, i)
                for i in range(3):
                    for p in range(2):
                        tanh_conv(p, i)
                    if i == 0:
                        for p in range(2):
                            tanh_z(p, 0)
                for p in range(2):
                    act.wait_ge(btg_psum[p], btg_psum.now(r, p))
                    sc.activation(bs[p][:, :], bank[p][3][:, 0:NS], ACT.Copy)
                    copy(ea[p][:, :], bank[p][3][:, 3 * P:3 * P + NH], bs_ready[p], ACT.Exp)
                for p in range(2):
                    decay(p, 0)
                for p in range(2):
                    tanh_z(p, 1)
                for p in range(2):
                    x_rows(p, 0)
                for p in range(2):
                    decay(p, 1)
                    act.wait_ge(decay_ready[p], decay_ready.now(r, p, 2))
                    copy(edec[p][:, :], seg[p][:, 0, :, P - 1], edec_ready[p])
                for p in range(2):
                    x_rows(p, 1)
                for i in (2, 3):
                    for p in range(2):
                        decay(p, i)
                for p in range(2):
                    act.wait_ge(state_psum[p], state_psum.now(r, p))
                    copy(st[p][:, :], bank[p][3][:, :], st_ready[p])
                for p in range(2):
                    act.wait_ge(y_ready[p], y_ready.now(r, p))
                    for c in range(KD):
                        ins = sc.activation(th[p][:, c, :], y[p][:, c, :], ACT.Square,
                                            accum_out=ss[p][:, c:c + 1])
                    ins.then_inc(ss_ready[p], 1)
                for c in range(KD):
                    for p in range(2):
                        act.wait_ge(yT_psum[p], yT_psum.now(r, p, c + 1))
                        copy(flat(yT[p][:, c, :, :]), bank[p][YT_BANK[c]][:, :], yT_ready[p])
                for p in range(2):
                    act.wait_ge(v2T_psum[p], v2T_psum.now(r, p))
                    copy(flat(v2T[p][:, :, :]), bank[p][2][:, :], v2T_ready[p])
                for p in range(2):
                    act.wait_ge(lg_ready[p], lg_ready.now(r, p))
                    copy(flat(le[p][:, :, :]), flat(lg[p][:, :, :]), le_ready[p], ACT.Exp)
            act.drain().then_inc(part_done, 1)

            act.wait_ge(part_done, 4)
            act.sem_inc(hhi_ready, H_BANKS)
            with sc.Fori(1, NE // 2 + 1) as r:
                for g in range(2 * NG):
                    for m in range(KF):
                        i = KF * g + m
                        act.wait_ge(h_psum, r * PER_TURN + (i + 1 - PER_TURN))
                        act.wait_ge(hlo_ready, r * PER_TURN + (i + 1 - PER_TURN))
                        sc.activation(hf[m % 2][:, :], h_bank[i % H_BANKS][:, :], ACT.Gelu_apprx_tanh)\
                            .then_inc(hf_ready, 1)
                        sc.activation(h_hi[:, m, :], h_bank[i % H_BANKS][:, :], ACT.Gelu_apprx_tanh)\
                            .then_inc(hhi_ready, 1)

        @block.vector
        def _(dve):
            vc = nc.vector

            def flat(t):
                return t.rearrange("p a b -> p (a b)")

            def heads(t):
                return t.rearrange("p (h d) -> p h d", h=NH)

            prep = Chain(dve, s_prep, 0)
            dve.wait_ge(s_tok, 16)
            prep.mark(vc.tensor_scalar(tok_neg[:, :], tok_all[:, 0:N_TILES], 0.0, float(VOCAB), ALU.is_lt, ALU.mult))
            prep.wait()
            prep.mark(vc.tensor_tensor(tok_neg[:, :], tok_neg[:, :], tok_all[:, 0:N_TILES], ALU.add))
            prep.wait()
            vc.tensor_scalar(tok_all[:, 0:N_TILES], tok_neg[:, :], 0.0, float(VOCAB - 1), ALU.max, ALU.min)\
                .then_inc(s_clamped, 1)
            dve.wait_ge(s_consts, 16 * N_LOADS)
            vc.tensor_scalar(cw[:, :, :], cw[:, :, :], 0.5, None, ALU.mult)
            vc.tensor_scalar(cb[:, :], cb[:, :], 0.5, None, ALU.mult)
            vc.tensor_scalar(w_in[:, :, 0:DI], w_in[:, :, 0:DI], 0.5, None, ALU.mult)
            for k in range(KI):
                vc.tensor_scalar(w_out[:, k, :], w_out[:, k, :], nw[:, k:k + 1], None, ALU.mult)
            dve.wait_ge(s_nega, 1)
            prep.mark(vc.tensor_scalar(neg_a[:, :], neg_a[:, :], -1.0, None, ALU.mult))
            prep.wait()

            def embed(p):
                vc.scalar_tensor_tensor(out=flat(x[p][:, :, :]), in0=flat(xg[p][:, :, :]), scalar=float(DM) ** 0.5,
                                        in1=flat(pos[:, :, :]), op0=ALU.mult, op1=ALU.add).then_inc(x_ready[p], 1)

            for sig in (h2_ready, lg_ready, slot_ready):
                dve.sem_inc(sig.sem, sig.credit)
            for p in range(2):
                dve.wait_ge(gathered[p], gathered.credit)
                embed(p)

            with vc.Fori(1, PAIRS + 1) as r:
                ch = Chain(dve, chain_sem, DVE_LINKS)
                ch.r = r

                def norm_stats(p, src, st6, mean_var):
                    for c in range(KD):
                        last = ch.mark(vc.bn_stats(st6[:, c, :], src[:, c, :]))
                    hold(dve, ch.sem, ch.value(last))
                    for c in range(KD):
                        last = ch.mark(vc.bn_aggr(mean_var[:, c, :], st6[:, c, :]))
                    ch.wait()

                def query_max(p):
                    dve.wait_ge(st_psum[p], st_psum.now(r, p))
                    vc.tensor_reduce(nmax[p][:, :], bank[p][3][:, :].rearrange("p (c q) -> p c q", c=KD), AX.X,
                                     ALU.max, negate=True).then_inc(nmax_ready[p], 1)

                def scale_v(p):
                    dve.wait_ge(probs_ready[p], probs_ready.now(r, p))
                    ch.mark(vc.reciprocal(rinv[p][:, :], rsum[p][:, :]))
                    ch.wait()
                    dve.wait_ge(v_psum[p], v_psum.now(r, p))
                    vc.tensor_tensor(v[p][:, :, :], bank[p][2][:, :].rearrange("p (c d) -> p c d", c=KD),
                                     bc(rinv[p][:, :].unsqueeze(2), [P, KD, DM]), ALU.mult).then_inc(v_ready[p], 1)

                def norm_1(p):
                    dve.wait_ge(o_psum[p], o_psum.now(r, p))
                    norm_stats(p, bank[p][0][:, :].rearrange("p (c d) -> p c d", c=KD), stats[p], mv[p])
                    vc.tensor_scalar(lnv[p][:, 0, :], mv[p][:, :, 1], EPS, None, ALU.add)
                    vc.tensor_scalar(lnv[p][:, 1, :], mv[p][:, :, 1], 1.0 + EPS, EPS * EPS, ALU.mult, ALU.add)\
                        .then_inc(lnv_ready[p], 1)

                def apply_norm_1(p):
                    dve.wait_ge(lnr_ready[p], lnr_ready.now(r, p))
                    for c in range(KD):
                        ins = vc.tensor_scalar(hn[p][:, c, :], bank[p][0][:, c * DM:(c + 1) * DM],
                                               mv[p][:, c, 0:1], lnr[p][:, 1, c:c + 1], ALU.subtract, ALU.mult)
                    ins.then_inc(hn_ready[p], 1)
                    vc.tensor_scalar(hu_s[p][:, :], lnr[p][:, 0, :], 1.0, None, ALU.add)
                    vc.scalar_tensor_tensor(out=hu_b[p][:, :], in0=mv[p][:, :, 0], scalar=-1.0, in1=lnr[p][:, 0, :],
                                            op0=ALU.mult, op1=ALU.mult).then_inc(hu_coef[p], 1)

                def dt_in(p):
                    dve.wait_ge(dt_psum[p], dt_psum.now(r, p))
                    ch.mark(vc.tensor_tensor(dty[p][:, :, :], bank[p][1][:, 0:KD * NH].rearrange("p (c h) -> p c h", c=KD),
                                             bc(dtb[:, :].unsqueeze(1), [P, KD, NH]), ALU.add))
                    ch.wait()
                    vc.scalar_tensor_tensor(out=dtn[p][:, :, :], in0=dty[p][:, :, :], scalar=-1.0, in1=dty[p][:, :, :],
                                            op0=ALU.mult, op1=ALU.min).then_inc(dtn_ready[p], 1)

                def softplus(ps):
                    def each(make):
                        for p in ps:
                            ch.mark(make(p))
                        ch.wait()
                    for p in ps:
                        dve.wait_ge(dtw_ready[p], dtw_ready.now(r, p))
                    f = lambda t, p: flat(t[p][:, :, :])
                    each(lambda p: vc.tensor_scalar(f(dtq, p), f(dtw, p), 2.0, None, ALU.add))
                    each(lambda p: vc.reciprocal(f(dtq, p), f(dtq, p)))
                    each(lambda p: vc.tensor_tensor(f(dts, p), f(dtw, p), f(dtq, p), ALU.mult))
                    each(lambda p: vc.tensor_tensor(f(dtq, p), f(dts, p), f(dts, p), ALU.mult))
                    each(lambda p: vc.tensor_scalar(f(dtp, p), f(dtq, p), LOG_TERMS[0], None, ALU.mult))
                    for term in LOG_TERMS[1:]:
                        each(lambda p: vc.scalar_tensor_tensor(out=f(dtp, p), in0=f(dtp, p), scalar=term, in1=f(dtq, p),
                                                               op0=ALU.add, op1=ALU.mult))
                    each(lambda p: vc.scalar_tensor_tensor(out=f(dtp, p), in0=f(dtp, p), scalar=1.0, in1=f(dts, p),
                                                           op0=ALU.add, op1=ALU.mult))
                    each(lambda p: vc.tensor_scalar(f(dtp, p), f(dtp, p), 2.0, None, ALU.mult))
                    each(lambda p: vc.scalar_tensor_tensor(out=f(dt_, p), in0=f(dty, p), scalar=0.0, in1=f(dtp, p),
                                                           op0=ALU.max, op1=ALU.add))
                    for p in ps:
                        vc.tensor_tensor(a_[p][:, :, :], dt_[p][:, :, :], bc(neg_a[:, :].unsqueeze(1), [P, KD, NH]),
                                         ALU.mult).then_inc(a_ready[p], 1)

                def conv(p, i):
                    j = GROUPS[i]
                    dve.wait_ge(tap_ready[p], tap_ready.now(r, p, i + 1))
                    done = [None, None]
                    for back in range(1, TAPS):
                        for h in range(2):
                            m = 2 * j + h
                            if done[h]:
                                ch.wait(done[h])
                            ins = vc.scalar_tensor_tensor(
                                out=xc[p][:, m, back:], in0=bank[p][XBC_BANK[i]][:, h * L:(h + 1) * L - back],
                                scalar=cw[:, m, TAPS - 1 - back:TAPS - back], in1=xc[p][:, m, back:],
                                op0=ALU.mult, op1=ALU.add)
                            if back < TAPS - 1:
                                done[h] = ch.mark(ins)
                    ins.then_inc(conv_done[p], 1)

                def gate_conv(p, i):
                    j = GROUPS[i]
                    dve.wait_ge(th_ready[p], th_ready.now(r, p, i + 1))
                    both = flat(xc[p][:, 2 * j:2 * j + 2, :])
                    vc.scalar_tensor_tensor(out=both, in0=th[p][:, j, :], scalar=1.0, in1=both,
                                            op0=ALU.add, op1=ALU.mult).then_inc(xc_ready[p], 1)

                def gate_z(p, c):
                    dve.wait_ge(tz_ready[p], tz_ready.now(r, p, c + 1))
                    vc.scalar_tensor_tensor(out=sz[p][:, c, :], in0=sz[p][:, c, :], scalar=1.0,
                                            in1=bank[p][Z_BANK[c]][:, :], op0=ALU.add, op1=ALU.mult)\
                        .then_inc(sz_ready[p], 1)

                def mask_scores(p):
                    dve.wait_ge(bs_ready[p], bs_ready.now(r, p))
                    vc.tensor_tensor(gm[p][:, :, :], bank[p][3][:, P:3 * P].rearrange("p (c l) -> p c l", c=KD),
                                     bc(tri[:, :].unsqueeze(1), [P, KD, P]), ALU.mult).then_inc(gm_ready[p], 1)

                def times_dt(p, c):
                    dve.wait_ge(xs_ready[p], xs_ready.now(r, p, c + 1))
                    vc.tensor_tensor(heads(xdt[p][:, c, :]), heads(bank[p][XS_BANK[c]][:, :]),
                                     bc(dt_[p][:, c, :].unsqueeze(2), [P, NH, HD]), ALU.mult).then_inc(xdt_ready[p], 1)

                def decay_scores(p, c):
                    dve.wait_ge(decay_ready[p], decay_ready.now(r, p, 2 * c + 2))
                    dve.wait_ge(edec_ready[p], edec_ready.now(r, p))
                    dve.wait_ge(gm_ready[p], gm_ready.now(r, p))
                    vc.tensor_tensor(seg[p][:, c, :, :], seg[p][:, c, :, :], bc(gm[p][:, c, :].unsqueeze(1), [P, NH, P]),
                                     ALU.mult).then_inc(m_ready[p], 1)

                def gated_y(p, c):
                    if c == 0:
                        dve.wait_ge(yd_psum[p], yd_psum.now(r, p, 1))
                        dve.wait_ge(skip_ready[p], skip_ready.now(r, p, 1))
                        ch.mark(vc.tensor_tensor(y[p][:, 0, :], bank[p][YD_BANK[0]][:, :], xs[p][:, 0, :], ALU.add))
                        ch.wait()
                    else:
                        dve.wait_ge(yo_psum[p], yo_psum.now(r, p))
                        ch.mark(vc.tensor_tensor(heads(y[p][:, 1, :]), heads(bank[p][2][:, :]),
                                                 bc(ea[p][:, :].unsqueeze(2), [P, NH, HD]), ALU.mult))
                        ch.wait()
                        dve.wait_ge(skip_ready[p], skip_ready.now(r, p, 2))
                        ch.mark(vc.tensor_tensor(y[p][:, 1, :], y[p][:, 1, :], xs[p][:, 1, :], ALU.add))
                        ch.wait()
                        ch.mark(vc.tensor_tensor(y[p][:, 1, :], bank[p][YD_BANK[1]][:, :], y[p][:, 1, :], ALU.add))
                        ch.wait()
                    vc.tensor_tensor(y[p][:, c, :], y[p][:, c, :], sz[p][:, c, :], ALU.mult).then_inc(y_ready[p], 1)

                def mean_square(p):
                    dve.wait_ge(ss_ready[p], ss_ready.now(r, p))
                    vc.tensor_scalar(msq[p][:, :], ss[p][:, :], 1.0 / DI, EPS, ALU.mult, ALU.add)\
                        .then_inc(msq_ready[p], 1)

                def residual(p):
                    dve.wait_ge(out_psum[p], out_psum.now(r, p))
                    dve.wait_ge(rms_ready[p], rms_ready.now(r, p))
                    dve.wait_ge(hu_ready[p], hu_ready.now(r, p))
                    for c in range(KD):
                        ins = vc.scalar_tensor_tensor(out=h2[p][:, c, :], in0=bank[p][0][:, c * DM:(c + 1) * DM],
                                                      scalar=rms[p][:, c:c + 1], in1=hu[p][:, c, :],
                                                      op0=ALU.mult, op1=ALU.add)
                    ins.then_inc(h2_ready[p], 1)
                    hold(dve, h2_ready[p], h2_ready.now(r, p))
                    norm_stats(p, h2[p], stats2[p], mv2[p])
                    vc.tensor_scalar(lv2[p][:, :], mv2[p][:, :, 1], EPS, None, ALU.add).then_inc(lv2_ready[p], 1)

                def norm_2(p):
                    dve.wait_ge(lr2_ready[p], lr2_ready.now(r, p))
                    dve.wait_ge(rows_free[p], rows_free.before(r, p))
                    for c in range(KD):
                        ins = vc.tensor_scalar(rows[p][:, c, 0:DM], h2[p][:, c, :], mv2[p][:, c, 0:1],
                                               lr2[p][:, c:c + 1], ALU.subtract, ALU.mult)
                    ins.then_inc(v2_ready[p], 1)

                def router_in(p):
                    dve.wait_ge(logit_psum[p], logit_psum.now(r, p))
                    logits = bank[p][3][:, 0:KD * NE].rearrange("p (c e) -> p c e", c=KD)
                    ch.mark(vc.tensor_reduce(lmax[p][:, :], logits, AX.X, ALU.max, negate=True))
                    ch.wait()
                    vc.tensor_tensor(lg[p][:, :, :], logits, bc(lmax[p][:, :].unsqueeze(2), [P, KD, NE]), ALU.add)\
                        .then_inc(lg_ready[p], 1)

                def router_top(p):
                    dve.wait_ge(le_ready[p], le_ready.now(r, p))
                    ch.mark(vc.tensor_reduce(lsum[p][:, :], le[p][:, :, :], AX.X, ALU.add))
                    ch.wait()
                    ch.mark(vc.reciprocal(linv[p][:, :], lsum[p][:, :]))
                    ch.wait()
                    last = ch.mark(vc.tensor_tensor(pr[p][:, :, :], le[p][:, :, :],
                                                    bc(linv[p][:, :].unsqueeze(2), [P, KD, NE]), ALU.mult))
                    hold(dve, ch.sem, ch.value(last))
                    for c in range(KD):
                        last = ch.mark(vc.max(top[p][:, c, :], pr[p][:, c, :]))
                    hold(dve, ch.sem, ch.value(last))
                    for c in range(KD):
                        ch.mark(vc.max_index(topi[p][:, c, :], top[p][:, c, :], pr[p][:, c, :]))
                    ch.wait()
                    ch.mark(vc.tensor_copy(topf[p][:, :, :], topi[p][:, :, 0:2]))
                    ch.wait()
                    ch.mark(vc.tensor_tensor(oh[p][:, :, :, :].rearrange("p c k e -> p (c k) e"),
                                             bc(e_iota[:, :].unsqueeze(1), [P, 2 * KD, NE]),
                                             bc(flat(topf[p][:, :, :]).unsqueeze(2), [P, 2 * KD, NE]), ALU.is_equal))
                    ch.wait()
                    vc.tensor_tensor(ohs[p][:, :, :], oh[p][:, :, 0, :], oh[p][:, :, 1, :], ALU.add)\
                        .then_inc(ohs_ready[p], 1)
                    vc.tensor_copy(rows[p][:, :, C_W0:C_W0 + 2], top[p][:, :, 0:2])
                    vc.tensor_copy(rows[p][:, :, C_E0], topf[p][:, :, 0])
                    ch.mark(vc.tensor_copy(rows[p][:, :, C_TOK].bitcast(I32), tok_iota[:, KD * p:KD * p + KD]))

                def slots_of(p):
                    dve.wait_ge(pos_psum[p], pos_psum.now(r, p))
                    dve.wait_ge(slot_ready[p], slot_ready.before(r, p))
                    ch.mark(vc.tensor_tensor(ohp[p][:, :, :, :], oh[p][:, :, :, :],
                                             bc(bank[p][1][:, 0:KD * NE].rearrange("p (c e) -> p c e", c=KD).unsqueeze(2),
                                                [P, KD, 2, NE]), ALU.mult))
                    ch.wait()
                    ch.mark(vc.tensor_reduce(offs[p][:, :], ohp[p][:, :, :, :].rearrange("p c k e -> p (c k) e"),
                                             AX.X, ALU.add))
                    ch.wait()
                    vc.scalar_tensor_tensor(out=sl[p][:, :], in0=flat(topf[p][:, :, :]), scalar=float(CAP),
                                            in1=offs[p][:, :], op0=ALU.mult, op1=ALU.add)
                    ch.mark(vc.tensor_scalar(valid[p][:, :], offs[p][:, :], float(CAP), None, ALU.is_lt))
                    ch.wait()
                    ch.mark(vc.scalar_tensor_tensor(out=sl[p][:, :], in0=sl[p][:, :], scalar=-float(NSLOT),
                                                    in1=valid[p][:, :], op0=ALU.add, op1=ALU.mult))
                    ch.wait()
                    vc.tensor_scalar(slot[p][:, :], sl[p][:, :], float(NSLOT), None, ALU.add).then_inc(slot_ready[p], 1)

                def count_choices():
                    for p in range(2):
                        for c in range(KD):
                            ch.mark(vc.tensor_tensor(oh_sum[:, :], oh_sum[:, :], ohs[p][:, c, :], ALU.add))
                            ch.wait()
                    ch.mark(vc.tensor_scalar(tok_iota[:, :], tok_iota[:, :], float(2 * L), None, ALU.add))
                    ch.wait()

                def both(step, *args):
                    for p in range(2):
                        step(p, *args)

                both(query_max); both(scale_v); both(norm_1); both(apply_norm_1)
                both(dt_in); both(conv, 0); softplus((0, 1)); both(conv, 1); both(conv, 2)
                both(gate_conv, 0); both(gate_z, 0); both(gate_conv, 1); both(gate_conv, 2)
                both(mask_scores); both(gate_z, 1); both(times_dt, 0); both(decay_scores, 0)
                both(times_dt, 1); both(decay_scores, 1)
                both(gated_y, 0); both(gated_y, 1); both(mean_square); both(residual)
                for p in range(2):
                    dve.wait_ge(gathered[p], gathered.now(r, p))
                    embed(p)
                both(norm_2); both(router_in); both(router_top); both(slots_of)
                count_choices()
                ch.close()
            dve.drain().then_inc(part_done, 1)

            dve.wait_ge(part_done, 4)
            dve.sem_inc(xe_split, 1)
            dve.sem_inc(hlo_ready, 2)
            dve.sem_inc(ye_ready, 2)
            prep.mark(vc.memset(e_now[:, :], 0.0))
            prep.wait()
            with vc.Fori(1, NE // 2 + 1) as r:
                ch = Chain(dve, moe_chain_sem, MOE_LINKS)
                ch.r = r

                def slot_infos(q):
                    dve.wait_ge(xe_loaded[q], xe_loaded.now(r, q))
                    dve.wait_ge(expert_added, r * 2 + (q - 1))
                    vc.tensor_tensor(wd[q][:, :], xe[q][:, :, C_W0], xe[q][:, :, C_W0 + 1], ALU.subtract)
                    ch.mark(vc.tensor_scalar(is_first[q][:, :], xe[q][:, :, C_E0], e_now[:, :], None, ALU.is_equal))
                    ch.wait()
                    ch.mark(vc.tensor_tensor(wd[q][:, :], wd[q][:, :], is_first[q][:, :], ALU.mult))
                    ch.wait()
                    vc.tensor_tensor(w_slot[q][:, :], wd[q][:, :], xe[q][:, :, C_W0 + 1], ALU.add)
                    vc.tensor_scalar(e_now[:, :], e_now[:, :], 1.0, None, ALU.add)
                    ch.mark(vc.tensor_copy(tok_slot[q][:, :], xe[q][:, :, C_TOK].bitcast(I32)))
                    hold(dve, ch.sem, ch.value(ch.count))
                    dve.sem_inc(slot_info, 1)

                def split_x(g):
                    dve.wait_ge(xeT_psum, r * (2 * NG) + (g + 1 - 2 * NG))
                    for k in range(KD):
                        vc.tensor_copy(xe_hi[g % 2][:, k, :], x_bank[k][:, :]).then_inc(x_half, 1)
                    for k in range(KD):
                        dve.wait_ge(x_half, r * (2 * NG * KD) + (g * KD + k + 1 - 2 * NG * KD))
                        ins = vc.tensor_tensor(xe_lo[g % 2][:, k, :], x_bank[k][:, :], xe_hi[g % 2][:, k, :].bitcast(F32),
                                               ALU.subtract)
                    ins.then_inc(xe_split, 1)

                def split_h(g):
                    for m in range(KF):
                        i = KF * g + m
                        dve.wait_ge(hhi_ready, r * PER_TURN + (H_BANKS + i + 1 - PER_TURN))
                        vc.tensor_tensor(h_lo[:, m, :], hf[m % 2][:, :], h_hi[:, m, :].bitcast(F32), ALU.subtract)\
                            .then_inc(hlo_ready, 1)

                def weigh(g):
                    q, half = g // NG, g % NG
                    for b in range(2):
                        j = 4 * half + 2 * b
                        dve.wait_ge(y_psum, r * (4 * NG) + (Y0 + 2 * g + b + 1 - 4 * NG))
                        vc.tensor_tensor(ye[q][:, j:j + 2, :], y_bank[b][:, :].rearrange("p (j d) -> p j d", j=2),
                                         bc(w_slot[q][:, j:j + 2].unsqueeze(2), [P, 2, DM]), ALU.mult)\
                            .then_inc(ye_ready, 1)

                slot_infos(0)
                split_x(0)
                for g in range(2 * NG):
                    split_h(g)
                    if g + 1 == NG:
                        slot_infos(1)
                    if g + 1 < 2 * NG:
                        split_x(g + 1)
                    weigh(g)
                ch.close()

        @block.tensor
        def _(pe):
            te = nc.tensor

            pe.wait_ge(s_consts, 16 * N_LOADS)
            pe.wait_ge(s_masks, 1)
            for m in range(KD):
                for k in range(KD):
                    ins = te.matmul(bank[0][0][:, m * DM:(m + 1) * DM], wqk_in[:, 0, k, m * P:(m + 1) * P],
                                    wqk_in[:, 1, k, :], start=(k == 0), stop=(k == KD - 1))
            ins.then_inc(s_wqk, 1)
            pe.wait_ge(s_wqk, 2)
            pe.wait_ge(s_prep, 3)

            def transposes(p, b, srcs):
                for n, src in enumerate(srcs):
                    ins = te.transpose(bank[p][b][:, n * P:(n + 1) * P], src, ident[:, :])
                return ins

            with te.Fori(1, PAIRS + 1) as r:
                def to_xT(p):
                    pe.wait_ge(x_ready[p], x_ready.before(r, p))
                    pe.wait_ge(h2_ready[p], h2_ready.before(r, p))
                    transposes(p, 0, [x[p][:, c, k * P:(k + 1) * P] for k in range(KD) for c in range(KD)])\
                        .then_inc(xT_psum[p], 1)

                def query_side(p):
                    pe.wait_ge(xT_ready[p], xT_ready.now(r, p))
                    pe.wait_ge(slot_ready[p], slot_ready.before(r, p))
                    for m in range(KD):
                        for k in range(KD):
                            ins = te.matmul(bank[p][1][:, m * L:(m + 1) * L], wqk[:, k, m * P:(m + 1) * P],
                                            xT[p][:, k, :], start=(k == 0), stop=(k == KD - 1))
                    ins.then_inc(tT_psum[p], 1)
                    pe.wait_ge(v2T_ready[p], v2T_ready.before(r, p))
                    for c in range(KD):
                        for k in range(KD):
                            ins = te.matmul(bank[p][2][:, c * DM:(c + 1) * DM], xT[p][:, k, c * P:(c + 1) * P],
                                            wv[:, k, :], start=(k == 0), stop=(k == KD - 1))
                    ins.then_inc(v_psum[p], 1)

                def scores(p):
                    pe.wait_ge(tT_ready[p], tT_ready.now(r, p))
                    pe.wait_ge(lg_ready[p], lg_ready.before(r, p))
                    for c in range(KD):
                        for k in range(KD):
                            ins = te.matmul(bank[p][3][:, c * L:(c + 1) * L], xT[p][:, k, c * P:(c + 1) * P],
                                            tT[p][:, k, :], start=(k == 0), stop=(k == KD - 1))
                    ins.then_inc(st_psum[p], 1)

                def attend(p):
                    pe.wait_ge(v_ready[p], v_ready.now(r, p))
                    for c in range(KD):
                        for k in range(KD):
                            ins = te.matmul(bank[p][0][:, c * DM:(c + 1) * DM], probs[p][:, k, c * P:(c + 1) * P],
                                            v[p][:, k, :], start=(k == 0), stop=(k == KD - 1))
                    ins.then_inc(o_psum[p], 1)

                def to_hT(p):
                    pe.wait_ge(hn_ready[p], hn_ready.now(r, p))
                    transposes(p, 1, [hn[p][:, c, k * P:(k + 1) * P] for k in range(KD) for c in range(KD)])\
                        .then_inc(hnT_psum[p], 1)

                def project_dt(p):
                    pe.wait_ge(hT_ready[p], hT_ready.now(r, p))
                    for c in range(KD):
                        for k in range(KD):
                            ins = te.matmul(bank[p][1][:, c * NH:(c + 1) * NH], hT[p][:, k, c * P:(c + 1) * P],
                                            w_in[:, k, DI + CC:DI + CC + NH], start=(k == 0), stop=(k == KD - 1))
                    ins.then_inc(dt_psum[p], 1)

                def project_channels(p, i):
                    if i == 2:
                        pe.wait_ge(hu_ready[p], hu_ready.now(r, p))
                    for h in range(2):
                        m = 2 * GROUPS[i] + h
                        for k in range(KD):
                            ins = te.matmul(bank[p][XBC_BANK[i]][:, h * L:(h + 1) * L],
                                            w_in[:, k, DI + m * P:DI + (m + 1) * P], hT[p][:, k, :],
                                            start=(k == 0), stop=(k == KD - 1))
                    ins.then_inc(xbc_psum[p], 1)

                def project_z(p, c):
                    pe.wait_ge(conv_done[p], conv_done.now(r, p, 1 if c == 0 else 3))
                    for k in range(KD):
                        ins = te.matmul(bank[p][Z_BANK[c]][:, :], hT[p][:, k, c * P:(c + 1) * P], w_in[:, k, 0:DI],
                                        start=(k == 0), stop=(k == KD - 1))
                    ins.then_inc(z_psum[p], 1)

                def state_inputs(p):
                    pe.wait_ge(xc_ready[p], xc_ready.now(r, p, 1))
                    pe.wait_ge(conv_done[p], conv_done.now(r, p, 2))
                    pe.wait_ge(a_ready[p], a_ready.now(r, p))
                    te.transpose(bank[p][3][:, 0:P], xc[p][:, KI, 0:P], ident[:, :])
                    for c in range(KD):
                        te.matmul(bank[p][3][:, (c + 1) * P:(c + 2) * P], xc[p][:, KI, c * P:(c + 1) * P],
                                  xc[p][:, KI + 1, c * P:(c + 1) * P], start=True, stop=True)
                    te.matmul(bank[p][3][:, 3 * P:3 * P + NH], tri[:, :], a_[p][:, 1, :], start=True, stop=True)\
                        .then_inc(btg_psum[p], 1)

                def segment_sums(p, i):
                    c, half = i // 2, i % 2
                    pe.wait_ge(seg_in[p], seg_in.now(r, p, c + 1))
                    if i == 1:
                        pe.wait_ge(bs_ready[p], bs_ready.now(r, p))
                        pe.wait_ge(gm_ready[p], gm_ready.now(r, p))
                    if i == 2:
                        pe.wait_ge(sz_ready[p], sz_ready.now(r, p, 2))
                    if i == 3:
                        pe.wait_ge(xs_ready[p], xs_ready.now(r, p, 1))
                        pe.wait_ge(xdt_ready[p], xdt_ready.now(r, p, 1))
                    te.matmul(bank[p][SEG_BANK[i]][:, :], below[:, :],
                              seg[p][:, c, 4 * half:4 * half + 4, :].rearrange("p h l -> p (h l)"),
                              start=True, stop=True).then_inc(seg_psum[p], 1)

                def x_to_rows(p, c):
                    if c == 0:
                        pe.wait_ge(sz_ready[p], sz_ready.now(r, p, 1))
                        pe.wait_ge(xc_ready[p], xc_ready.now(r, p))
                    else:
                        pe.wait_ge(decay_ready[p], decay_ready.now(r, p, 1))
                    transposes(p, XS_BANK[c], [xc[p][:, m, c * P:(c + 1) * P] for m in range(KI)])\
                        .then_inc(xs_psum[p], 1)

                def chunk_state(p):
                    pe.wait_ge(decay_ready[p], decay_ready.now(r, p, 2))
                    pe.wait_ge(bs_ready[p], bs_ready.now(r, p))
                    pe.wait_ge(xdec_ready[p], xdec_ready.now(r, p))
                    te.matmul(bank[p][3][:, :], bs[p][:, :], xdec[p][:, :], start=True, stop=True)\
                        .then_inc(state_psum[p], 1)

                def own_chunk(p, c):
                    pe.wait_ge(m_ready[p], m_ready.now(r, p, c + 1))
                    if c == 0:
                        pe.wait_ge(xs_ready[p], xs_ready.now(r, p, 2))
                        pe.wait_ge(xdt_ready[p], xdt_ready.now(r, p, 2))
                    for h in range(NH):
                        ins = te.matmul(bank[p][YD_BANK[c]][:, h * HD:(h + 1) * HD], seg[p][:, c, h, :],
                                        xdt[p][:, c, h * HD:(h + 1) * HD], start=True, stop=True)
                    ins.then_inc(yd_psum[p], 1)

                def from_state(p):
                    pe.wait_ge(st_ready[p], st_ready.now(r, p))
                    pe.wait_ge(decay_ready[p], decay_ready.now(r, p))
                    te.matmul(bank[p][2][:, :], xc[p][:, KI + 1, P:2 * P], st[p][:, :], start=True, stop=True)\
                        .then_inc(yo_psum[p], 1)

                def to_yT(p, c):
                    pe.wait_ge(y_ready[p], y_ready.now(r, p, c + 1))
                    transposes(p, YT_BANK[c], [y[p][:, c, k * P:(k + 1) * P] for k in range(KI)])\
                        .then_inc(yT_psum[p], 1)

                def project_out(p):
                    pe.wait_ge(yT_ready[p], yT_ready.now(r, p))
                    for c in range(KD):
                        for k in range(KI):
                            ins = te.matmul(bank[p][0][:, c * DM:(c + 1) * DM], yT[p][:, c, k, :], w_out[:, k, :],
                                            start=(k == 0), stop=(k == KI - 1))
                    ins.then_inc(out_psum[p], 1)

                def to_v2T(p):
                    pe.wait_ge(v2_ready[p], v2_ready.now(r, p))
                    transposes(p, 2, [rows[p][:, c, k * P:(k + 1) * P] for k in range(KD) for c in range(KD)])\
                        .then_inc(v2T_psum[p], 1)

                def route(p):
                    pe.wait_ge(v2T_ready[p], v2T_ready.now(r, p))
                    for c in range(KD):
                        for k in range(KD):
                            ins = te.matmul(bank[p][3][:, c * NE:(c + 1) * NE], v2T[p][:, k, c * P:(c + 1) * P],
                                            wr[:, k, :], start=(k == 0), stop=(k == KD - 1))
                    ins.then_inc(logit_psum[p], 1)

                def choices_before(p):
                    pe.wait_ge(ohs_ready[p], ohs_ready.now(r, p))
                    for c in range(KD):
                        dst = bank[p][1][:, c * NE:(c + 1) * NE]
                        te.matmul(dst, before_b[:, :], ohs[p][:, c, :], start=True, stop=False)
                        for pp in range(p + 1):
                            for cc in range(KD if pp < p else c):
                                te.matmul(dst, ones_b[:, :], ohs[pp][:, cc, :], start=False, stop=False)
                        ins = te.matmul(dst, ones_b[:, :], oh_sum[:, :], start=False, stop=True)
                    ins.then_inc(pos_psum[p], 1)

                def both(step, *args):
                    for p in range(2):
                        step(p, *args)

                both(to_xT); both(query_side); both(scores); both(attend); both(to_hT)
                both(project_dt)
                for i in range(3):
                    both(project_channels, i)
                both(project_z, 0); both(state_inputs); both(segment_sums, 0); both(project_z, 1)
                both(x_to_rows, 0); both(segment_sums, 1); both(x_to_rows, 1)
                both(segment_sums, 2); both(segment_sums, 3)
                both(chunk_state); both(own_chunk, 0); both(own_chunk, 1); both(from_state)
                both(to_yT, 0); both(to_yT, 1); both(project_out); both(to_v2T); both(route); both(choices_before)
            pe.drain().then_inc(part_done, 1)

            pe.wait_ge(part_done, 4)
            pe.sem_inc(y_psum, Y0)

            def three(out_, hi, lo, rhi, rlo, first_, last_):
                te.matmul(out_, hi, rhi, start=first_, stop=False)
                te.matmul(out_, hi, rlo, start=False, stop=False)
                return te.matmul(out_, lo, rhi, start=False, stop=last_)

            with te.Fori(1, NE // 2 + 1) as r:
                def turn_x(g):
                    q, half = g // NG, g % NG
                    if half == 0:
                        pe.wait_ge(xe_loaded[q], xe_loaded.now(r, q))
                    pe.wait_ge(xe_split, r * (2 * NG) + (1 + g - 2 * NG))
                    for k in range(KD):
                        for j in range(4):
                            ins = te.transpose(x_bank[k][:, j * P:(j + 1) * P],
                                               xe[q][:, 4 * half + j, k * P:(k + 1) * P], ident[:, :])
                    ins.then_inc(xeT_psum, 1)

                def first_product(g):
                    q = g // NG
                    pe.wait_ge(w_split, r * 4 + (2 * q - 2))
                    pe.wait_ge(xe_split, r * (2 * NG) + (2 + g - 2 * NG))
                    for m in range(KF):
                        i = KF * g + m
                        pe.wait_ge(hhi_ready, r * PER_TURN + (i + 1 - PER_TURN))
                        for k in range(KD):
                            at = slice(k * FF + m * P, k * FF + (m + 1) * P)
                            ins = three(h_bank[i % H_BANKS][:, :], w_hi[q][:, 0, at], w_lo[q][:, 0, at],
                                        xe_hi[g % 2][:, k, :], xe_lo[g % 2][:, k, :], k == 0, k == KD - 1)
                        ins.then_inc(h_psum, 1)

                def second_product(g):
                    q = g // NG
                    for b in range(2):
                        pe.wait_ge(ye_ready, r * (4 * NG) + (2 * g + b + 1 - 4 * NG))
                        for j in (2 * b, 2 * b + 1):
                            dst = y_bank[b][:, (j % 2) * DM:(j % 2 + 1) * DM]
                            for m in range(KF):
                                if j == 0:
                                    pe.wait_ge(hlo_ready, r * PER_TURN + (2 + KF * g + m + 1 - PER_TURN))
                                at = slice(m * DM, (m + 1) * DM)
                                ins = three(dst, h_hi[:, m, j * P:(j + 1) * P], h_lo[:, m, j * P:(j + 1) * P],
                                            w_hi[q][:, 1, at], w_lo[q][:, 1, at], m == 0, m == KF - 1)
                        ins.then_inc(y_psum, 1)

                turn_x(0)
                for g in range(2 * NG):
                    first_product(g)
                    if g + 1 < 2 * NG:
                        turn_x(g + 1)
                    second_product(g)


def kernel(x, L0_tok_emb, L0_tok_w_q, L0_tok_w_k, L0_tok_w_v, L0_tok_pos_enc, L0_attn_ln_w, L0_attn_ln_b,
           L0_attn_in_proj_w, L0_attn_conv_w, L0_attn_conv_b, L0_attn_dt_bias, L0_attn_A_log, L0_attn_D,
           L0_attn_norm_w, L0_attn_out_proj_w, L0_ffn_w_router, L0_ffn_w1, L0_ffn_w2, L0_ffn_bias):
    import numpy as np
    import concourse.bacc as bacc
    from concourse.bass_utils import run_bass_kernel_spmd

    A = np.asarray
    x = A(x)
    nb, length = x.shape
    tokens = nb * length
    dm = A(L0_tok_emb).shape[1]
    ne, _, ff = A(L0_ffn_w1).shape

    def by_lane(a):
        a = A(a)
        return np.moveaxis(a.reshape(-1, P, *a.shape[1:]), 1, 0)

    laid_out = {
        "tokens": by_lane(x.reshape(-1)),
        "emb": A(L0_tok_emb),
        "w_qT": A(L0_tok_w_q).T, "w_kT": A(L0_tok_w_k).T, "w_v": A(L0_tok_w_v),
        "pos_enc": A(L0_tok_pos_enc)[:length],
        "ln_w": by_lane(L0_attn_ln_w), "ln_b": by_lane(L0_attn_ln_b),
        "in_wT": A(L0_attn_in_proj_w).T,
        "conv_w": by_lane(L0_attn_conv_w), "conv_b": by_lane(L0_attn_conv_b),
        "dt_bias": A(L0_attn_dt_bias)[None], "A_log": A(L0_attn_A_log)[None], "D_skip": A(L0_attn_D)[None],
        "norm_w": by_lane(L0_attn_norm_w),
        "out_wT": A(L0_attn_out_proj_w).T,
        "w_router": by_lane(L0_ffn_w_router),
        "w1": A(L0_ffn_w1).reshape(ne * dm, ff), "w2": A(L0_ffn_w2).reshape(ne * ff, dm),
        "bias": A(L0_ffn_bias).reshape(1, dm),
    }
    nc = bacc.Bacc("TRN2", target_bir_lowering=False, num_devices=1)
    arrays, aps = {}, {}
    for name, a in laid_out.items():
        arrays[name] = np.ascontiguousarray(a)
        aps[name] = nc.dram_tensor(name, a.shape, mybir.dt.from_np(a.dtype), kind="ExternalInput").ap()
    aps["out"] = nc.dram_tensor("out", (tokens + P, dm), F32, kind="ExternalOutput").ap()
    aps["slots_dram"] = nc.dram_tensor("slots_dram", (2 * tokens, dm + 4), F32).ap()
    lm_block(nc, **aps)
    r = run_bass_kernel_spmd(nc, [arrays], core_ids=[0])
    return r.results[0]["out"][:tokens].reshape(nb, length, dm)
```

```python
import concourse.bass as bass
from concourse import mybir
from contextlib import ExitStack

F32 = mybir.dt.float32
F32R = mybir.dt.float32r
BF16 = mybir.dt.bfloat16
I32 = mybir.dt.int32
U32 = mybir.dt.uint32
ALU = mybir.AluOpType
ACT = mybir.ActivationFunctionType
AX = mybir.AxisListType

P = 128
EPS = 1e-5
LOG_TERMS = [1.0 / (2 * n + 1) for n in range(7, 0, -1)]


class Turn:

    def __init__(self, reg, shift=0):
        self.reg, self.shift = reg, shift

    def value(self, factor, rest):
        return self.reg * factor + (self.shift * factor + rest)


class Signal:

    def __init__(self, sem, steps=1, credit=0):
        self.sem, self.steps, self.credit = sem, steps, credit

    def __getitem__(self, p):
        return self.sem

    def now(self, r, p, step=None):
        step = self.steps if step is None else step
        return r.value(2 * self.steps, self.credit - 2 * self.steps + p * self.steps + step)

    def before(self, r, p):
        assert self.credit == 2 * self.steps
        return r.value(2 * self.steps, (p - 1) * self.steps)


class DmaSignal:

    def __init__(self, sems, per_turn, credit=0):
        self.sems, self.per_turn, self.credit = sems, per_turn, credit

    def __getitem__(self, p):
        return self.sems[p]

    def now(self, r, p):
        return r.value(self.per_turn, self.credit)

    def before(self, r, p):
        assert self.credit == self.per_turn
        return r.value(self.per_turn, 0)


class Chain:

    def __init__(self, eng, sem, links, r=None, p=0, times=2):
        self.eng, self.sem, self.links, self.count = eng, sem, links, 0
        self.r, self.p, self.times = r, p, times

    def mark(self, ins):
        self.count += 1
        ins.then_inc(self.sem, 1)
        return self.count

    def wait(self, count=None):
        self.eng.wait_ge(self.sem, self.value(self.count if count is None else count))

    def value(self, count):
        if self.r is None:
            return count
        return self.r.value(self.times * self.links, (self.p - self.times) * self.links + count)

    def close(self):
        assert self.count == self.links, self.count


def hold(eng, sem, value):
    eng.wait_ge(sem, value)
    eng.sem_inc(hold.counts[eng.engine], 1)


def run_batches(loop, half, turns):
    half(0, Turn(1), None, None)
    half(1, Turn(1), Turn(1), None)
    with loop(2, turns + 1) as reg:
        half(0, Turn(reg), Turn(reg, -1), Turn(reg, -1))
        half(1, Turn(reg), Turn(reg), Turn(reg, -1))
    half(0, None, Turn(turns), Turn(turns))
    half(1, None, None, Turn(turns))


def lm_block(nc, tokens, emb, w_qT, w_kT, w_v, pos_enc, ln_w, ln_b, in_wT, conv_w, conv_b, dt_bias, A_log,
             D_skip, norm_w, out_wT, w_router, w1, w2, bias, out, slots_dram):
    N_TILES = tokens.shape[1]
    T = N_TILES * P
    VOCAB, DM = emb.shape
    KD = DM // P
    L = 2 * P
    NB = T // L
    PAIRS = NB // 2
    DI = out_wT.shape[0]
    NH = dt_bias.shape[1]
    HD = DI // NH
    KI = DI // P
    NS = P
    CC = DI + 2 * NS
    MC = CC // P
    TAPS = conv_w.shape[2]
    NE = w_router.shape[2]
    FF = w1.shape[1]
    KF = FF // P
    CAP = 2 * T // NE
    NSLOT = NE * CAP
    JS = CAP // P
    GW = 4 * P
    NG = CAP // GW
    ROW = slots_dram.shape[1]
    C_W0, C_E0, C_TOK = DM, DM + 2, DM + 3
    assert (L, KD, MC, NS, TAPS) == (256, 2, 6, 128, 4) and NH * P == 1024 and NE == 8 and HD * NH == 4 * P

    FRONT_LINKS, BACK_LINKS, ROUTING_LINKS, MOE_LINKS, N_LOADS = 32, 8, 17, 6, 16

    with ExitStack() as ctx:
        def sb(name, shape, dt=F32, c=ctx):
            return c.enter_context(nc.sbuf_tensor(name, shape, dt))

        def sem(name):
            return ctx.enter_context(nc.semaphore(name))

        def signal(name, steps=1, credit=0):
            return Signal(sem(name), steps, credit)

        def dma_signal(name, per_turn, credit=0):
            return DmaSignal([sem(f"{name}{p}") for p in range(2)], per_turn, credit)

        ident = sb("ident", [P, P])
        w_raw = sb("w_raw", [P, 2, KD * FF])
        zero_row = sb("zero_row", [P, ROW])
        tok_iota = sb("tok_iota", [P, KD], I32)

        first = ExitStack()
        fb = lambda name, shape, dt=F32: sb(name, shape, dt, first)
        tri = fb("tri", [P, P])
        below = fb("below", [P, P])
        before_b = fb("before_b", [P, P], BF16)
        ones_b = fb("ones_b", [P, P], BF16)
        neg_half = fb("neg_half", [P, 4])
        e_iota = fb("e_iota", [P, NE])
        tok_all = fb("tok_all", [P, N_TILES + 4], I32)
        tok_neg = fb("tok_neg", [P, N_TILES], I32)
        wqk_in = fb("wqk_in", [P, 2, KD, DM])
        wqk = fb("wqk", [P, KD, DM])
        wv = fb("wv", [P, KD, DM])
        w_in = fb("w_in", [P, KD, in_wT.shape[1]])
        w_out = fb("w_out", [P, KI, DM])
        pos = fb("pos", [P, KD, DM])
        lnw = fb("lnw", [P, KD])
        lnb = fb("lnb", [P, KD])
        cw = fb("cw", [P, MC, TAPS])
        cb = fb("cb", [P, MC])
        nw = fb("nw", [P, KI])
        dtb = fb("dtb", [P, NH])
        alog = fb("alog", [P, NH])
        neg_a = fb("neg_a", [P, NH])
        dskip = fb("dskip", [P, NH])
        wr = fb("wr", [P, KD, NE])
        bias_b = fb("bias_b", [P, DM])
        oh_sum = fb("oh_sum", [P, NE], BF16)

        def pair(name, shape, dt=F32):
            return [fb(f"{name}{p}", shape, dt) for p in range(2)]

        idx = pair("idx", [P, KD], I32)
        xg = pair("xg", [P, KD, DM])
        x = pair("x", [P, KD, DM])
        xT = pair("xT", [P, KD, L])
        tT = pair("tT", [P, KD, L])
        probs = pair("probs", [P, KD, L])
        v = pair("v", [P, KD, DM])
        hn = pair("hn", [P, KD, DM])
        hu = pair("hu", [P, KD, DM])
        hT = pair("hT", [P, KD, L])
        xc = pair("xc", [P, MC, L])
        th = pair("th", [P, 3, 2 * L])
        sz = pair("sz", [P, KD, DI])
        xs = pair("xs", [P, KD, DI])
        xdt = pair("xdt", [P, KD, DI])
        seg = pair("seg", [P, KD, NH, P])
        gm = pair("gm", [P, KD, P])
        bs = pair("bs", [P, NS])
        xdec = pair("xdec", [P, DI])
        st = pair("st", [P, DI])
        y = pair("y", [P, KD, DI])
        yT = pair("yT", [P, KD, KI, P])
        h2 = pair("h2", [P, KD, DM])
        hb = pair("hb", [P, KD, DM])
        rows = pair("rows", [P, KD, ROW])
        v2T = pair("v2T", [P, KD, L])
        nmax = pair("nmax", [P, KD]); rsum = pair("rsum", [P, KD]); rinv = pair("rinv", [P, KD])
        stats = pair("stats", [P, KD, 6]); mv = pair("mv", [P, KD, 2])
        lnv = pair("lnv", [P, 2, KD]); lnr = pair("lnr", [P, 2, KD])
        hu_s = pair("hu_s", [P, KD]); hu_b = pair("hu_b", [P, KD])
        dty = pair("dty", [P, KD, NH]); dtn = pair("dtn", [P, KD, NH]); dtw = pair("dtw", [P, KD, NH])
        dts = pair("dts", [P, KD, NH]); dtq = pair("dtq", [P, KD, NH]); dtp = pair("dtp", [P, KD, NH])
        dt_ = pair("dt_", [P, KD, NH]); a_ = pair("a_", [P, KD, NH])
        ea = pair("ea", [P, NH]); edec = pair("edec", [P, NH])
        ss = pair("ss", [P, KD]); msq = pair("msq", [P, KD]); rms = pair("rms", [P, KD])
        stats2 = pair("stats2", [P, KD, 6]); mv2 = pair("mv2", [P, KD, 2])
        lv2 = pair("lv2", [P, KD]); lr2 = pair("lr2", [P, KD])
        lmax = pair("lmax", [P, KD]); lg = pair("lg", [P, KD, NE]); le = pair("le", [P, KD, NE])
        lsum = pair("lsum", [P, KD]); linv = pair("linv", [P, KD]); pr = pair("pr", [P, KD, NE])
        top = pair("top", [P, KD, 8]); topi = pair("topi", [P, KD, 8], U32); topf = pair("topf", [P, KD, 2])
        oh = pair("oh", [P, KD, 2, NE]); ohs = pair("ohs", [P, KD, NE], BF16); ohp = pair("ohp", [P, KD, 2, NE])
        offs = pair("offs", [P, 2 * KD]); valid = pair("valid", [P, 2 * KD])
        sl = pair("sl", [P, 2 * KD]); slot = pair("slot", [P, 2 * KD], I32)
        first.close()

        second = ExitStack()
        eb = lambda name, shape, dt=F32: sb(name, shape, dt, second)
        w_hi = [eb(f"w_hi{q}", [P, 2, KD * FF], F32R) for q in range(2)]
        w_lo = [eb(f"w_lo{q}", [P, 2, KD * FF], F32R) for q in range(2)]
        xe = [eb(f"xe{q}", [P, JS, ROW]) for q in range(2)]
        xe_hi = [eb(f"xe_hi{g}", [P, KD, GW], F32R) for g in range(2)]
        xe_lo = [eb(f"xe_lo{g}", [P, KD, GW], F32R) for g in range(2)]
        hf = [eb(f"hf{g}", [P, GW]) for g in range(2)]
        h_hi = eb("h_hi", [P, KF, GW], F32R)
        h_lo = eb("h_lo", [P, KF, GW], F32R)
        ye = [eb(f"ye{q}", [P, JS, DM]) for q in range(2)]
        e_now = eb("e_now", [P, 1])
        is_first = [eb(f"is_first{q}", [P, JS]) for q in range(2)]
        wd = [eb(f"wd{q}", [P, JS]) for q in range(2)]
        w_slot = [eb(f"w_slot{q}", [P, JS]) for q in range(2)]
        tok_slot = [eb(f"tok_slot{q}", [P, JS], I32) for q in range(2)]
        second.close()

        bank = [[ctx.enter_context(nc.psum_tensor(f"bank{p}{i}", [P, 512], F32)) for i in range(4)]
                for p in range(2)]

        s_consts = sem("s_consts")
        s_tok = sem("s_tok")
        hold.counts = {nc.vector.engine: sem("dve_held"), nc.gpsimd.engine: sem("pool_held")}
        s_clamped = sem("s_clamped")
        s_masks = sem("s_masks")
        s_mask0 = sem("s_mask0")
        s_prep = sem("s_prep")
        s_nega = sem("s_nega")
        s_wqk = sem("s_wqk")
        s_template = sem("s_template")
        s_fill = sem("s_fill")
        s_dump = sem("s_dump")
        idx_ready = signal("idx_ready", 1, 2)
        gathered = dma_signal("gathered", 16 * KD, 16 * KD)
        x_ready = signal("x_ready", 1, 2)
        xT_psum = signal("xT_psum"); xT_ready = signal("xT_ready")
        tT_psum = signal("tT_psum"); v_psum = signal("v_psum"); tT_ready = signal("tT_ready")
        st_psum = signal("st_psum"); nmax_ready = signal("nmax_ready"); probs_ready = signal("probs_ready")
        v_ready = signal("v_ready"); o_psum = signal("o_psum")
        lnv_ready = signal("lnv_ready"); lnr_ready = signal("lnr_ready")
        hn_ready = signal("hn_ready"); hu_coef = signal("hu_coef"); hu_ready = signal("hu_ready")
        hnT_psum = signal("hnT_psum"); hT_ready = signal("hT_ready")
        dt_psum = signal("dt_psum"); xbc_psum = signal("xbc_psum", 3); tap_ready = signal("tap_ready", 3)
        conv_done = signal("conv_done", 3); th_ready = signal("th_ready", 3); xc_ready = signal("xc_ready", 3)
        dtn_ready = signal("dtn_ready"); dtw_ready = signal("dtw_ready"); a_ready = signal("a_ready")
        seg_in = signal("seg_in", 2)
        z_psum = signal("z_psum", 2); tz_ready = signal("tz_ready", 2); sz_ready = signal("sz_ready", 2)
        btg_psum = signal("btg_psum"); bs_ready = signal("bs_ready"); gm_ready = signal("gm_ready")
        xs_psum = signal("xs_psum", 2); xs_ready = signal("xs_ready", 2); xdt_ready = signal("xdt_ready", 2)
        seg_psum = signal("seg_psum", 4); decay_ready = signal("decay_ready", 4)
        edec_ready = signal("edec_ready"); xdec_ready = signal("xdec_ready")
        m_ready = signal("m_ready", 2); skip_ready = signal("skip_ready", 2)
        state_psum = signal("state_psum"); st_ready = signal("st_ready")
        yd_psum = signal("yd_psum", 2); yo_psum = signal("yo_psum")
        y_ready = signal("y_ready", 2); ss_ready = signal("ss_ready")
        yT_psum = signal("yT_psum", 2); yT_ready = signal("yT_ready", 2)
        msq_ready = signal("msq_ready"); rms_ready = signal("rms_ready")
        out_psum = signal("out_psum"); h2_ready = signal("h2_ready", 1, 2)
        lv2_ready = signal("lv2_ready"); lr2_ready = signal("lr2_ready")
        v2_ready = signal("v2_ready"); hb_ready = signal("hb_ready")
        hb_stored = dma_signal("hb_stored", 16, 16)
        v2T_psum = signal("v2T_psum"); v2T_ready = signal("v2T_ready")
        logit_psum = signal("logit_psum"); lg_ready = signal("lg_ready"); le_ready = signal("le_ready")
        ohs_ready = signal("ohs_ready"); pos_psum = signal("pos_psum"); pos_taken = signal("pos_taken", 1, 2); slot_ready = signal("slot_ready", 1, 2)
        scattered = dma_signal("scattered", 64)
        rows_free = signal("rows_free", 1, 2)
        front_chain = sem("front_chain"); back_chain = sem("back_chain"); routing_chain = sem("routing_chain")
        moe_chain_sem = sem("dve_moe_chain")
        part_done = sem("part_done")
        w_loaded = sem("w_loaded")
        w_split = sem("w_split")
        xe_loaded = dma_signal("xe_loaded", 16)
        slot_info = sem("slot_info")
        xeT_psum = sem("xeT_psum")
        x_half = sem("x_half")
        xe_split = sem("xe_split")
        h_psum = sem("h_psum")
        hf_ready = sem("hf_ready")
        hhi_ready = sem("hhi_ready")
        hlo_ready = sem("hlo_ready")
        y_psum = sem("y_psum")
        ye_ready = sem("ye_ready")
        added = sem("added")
        expert_added = sem("expert_added")
        H_BANKS, Y0 = 4, 4 * NG

        def bc(ap, shape):
            return ap.to_broadcast(shape)

        GROUPS = (2, 0, 1)
        XBC_BANK, Z_BANK, SEG_BANK = (2, 3, 0), (2, 0), (1, 3, 0, 2)
        XS_BANK, YD_BANK, YT_BANK = (2, 1), (1, 0), (3, 1)
        PER_TURN = 2 * NG * KF
        h_bank = bank[0]
        x_bank = bank[1][0:2]
        y_bank = bank[1][2:4]

        block = ctx.enter_context(nc.Block())

        @block.sync
        def _(sp):
            sp.dma_start(tok_all[:, 0:N_TILES], tokens).then_inc(s_tok, 16)
            loads = [
                (wqk_in[:, 0, :, :], w_qT.rearrange("(k p) n -> p k n", p=P)),
                (wqk_in[:, 1, :, :], w_kT.rearrange("(k p) n -> p k n", p=P)),
                (pos[:, :, :], pos_enc.rearrange("(k p) n -> p k n", p=P)),
                (wv[:, :, :], w_v.rearrange("(k p) n -> p k n", p=P)),
                (w_in[:, :, :], in_wT.rearrange("(k p) n -> p k n", p=P)),
                (w_out[:, :, :], out_wT.rearrange("(k p) n -> p k n", p=P)),
                (lnw[:, :], ln_w), (lnb[:, :], ln_b), (cw[:, :, :], conv_w), (cb[:, :], conv_b),
                (nw[:, :], norm_w), (wr[:, :, :], w_router),
                (dtb[:, :], bc(dt_bias, [P, NH])), (alog[:, :], bc(A_log, [P, NH])),
                (dskip[:, :], bc(D_skip, [P, NH])), (bias_b[:, :], bc(bias, [P, DM])),
            ]
            assert len(loads) == N_LOADS
            for dst, src in loads:
                sp.dma_start(dst, src).then_inc(s_consts, 16)
            sp.wait_ge(s_template, 1)
            sp.dma_start(slots_dram.rearrange("(n p) c -> p n c", p=P),
                         zero_row[:, :].unsqueeze(1).to_broadcast([P, NSLOT // P, ROW])).then_inc(s_fill, 16)
            sp.dma_start(out[T:T + P, :], zero_row[:, 0:DM]).then_inc(s_dump, 16)
            sp.dma_start(w_raw[:, 0, :].rearrange("p (k f) -> p k f", k=KD),
                         w1[0:DM, :].rearrange("(k p) f -> p k f", p=P)).then_inc(w_loaded, 16)
            sp.dma_start(w_raw[:, 1, :].rearrange("p (k f) -> p k f", k=KF),
                         w2[0:FF, :].rearrange("(k p) f -> p k f", p=P)).then_inc(w_loaded, 16)
            with sp.Fori(1, PAIRS + 1) as reg:
                r = Turn(reg)
                for p in range(2):
                    sp.wait_ge(hb_ready[p], hb_ready.now(r, p))
                    sp.dma_start(out[bass.ds(r.value(2 * L, p * L - 2 * L), L), :]
                                 .rearrange("(k p) n -> p k n", p=P), hb[p][:, :, :]).then_inc(hb_stored[p], 16)
            for p in range(2):
                sp.wait_ge(scattered[p], 64 * PAIRS)
                sp.wait_ge(hb_stored[p], 16 * (PAIRS + 1))
            sp.wait_ge(s_dump, 16)

            sp.wait_ge(part_done, 4)

            def load_weights(e):
                sp.wait_ge(w_split, e * 2)
                sp.dma_start(w_raw[:, 0, :].rearrange("p (k f) -> p k f", k=KD),
                             w1[bass.ds(e * DM, DM), :].rearrange("(k p) f -> p k f", p=P)).then_inc(w_loaded, 16)
                sp.dma_start(w_raw[:, 1, :].rearrange("p (k f) -> p k f", k=KF),
                             w2[bass.ds(e * FF, FF), :].rearrange("(k p) f -> p k f", p=P)).then_inc(w_loaded, 16)

            def load_slots(e, q):
                sp.dma_start(xe[q][:, :, :], slots_dram[bass.ds(e * CAP, CAP), :]
                             .rearrange("(j p) c -> p j c", p=P)).then_inc(xe_loaded[q], 16)

            for q in range(2):
                load_slots(q, q)
            with sp.Fori(1, NE // 2) as r:
                for q in range(2):
                    e = r * 2 + (q - 1)
                    load_weights(e)
                    sp.wait_ge(xeT_psum, e * NG)
                    sp.wait_ge(slot_info, e)
                    load_slots(e + 1, q)
            load_weights(NE - 1)
            sp.wait_ge(added, 16 * NE * JS)
            sp.wait_ge(expert_added, 2 + NE)

        @block.gpsimd
        def _(pool):
            g = nc.gpsimd
            g.memset(zero_row[:, :], 0.0)
            for m, val in ((ident, 0.0), (tri, 1.0), (below, 1.0), (before_b, 1.0), (ones_b, 1.0)):
                g.memset(m[:, :], val)
            g.memset(neg_half[:, :], -0.5)
            g.memset(oh_sum[:, :], 0.0)
            g.memset(tok_all[:, N_TILES:], 0).then_inc(s_mask0, 1)
            pool.wait_ge(s_mask0, 1)
            g.affine_select(out=ident[:, :], in_=ident[:, :], compare_op=ALU.not_equal, fill=1.0, base=0,
                            pattern=[[-1, P]], channel_multiplier=1)
            g.affine_select(out=tri[:, :], in_=tri[:, :], compare_op=ALU.is_ge, fill=0.0, base=0,
                            pattern=[[1, P]], channel_multiplier=-1)
            g.affine_select(out=below[:, :], in_=below[:, :], compare_op=ALU.is_gt, fill=0.0, base=0,
                            pattern=[[-1, P]], channel_multiplier=1)
            g.affine_select(out=before_b[:, :], in_=before_b[:, :], compare_op=ALU.is_gt, fill=0.0, base=0,
                            pattern=[[1, P]], channel_multiplier=-1)
            g.iota(e_iota[:, :], pattern=[[1, NE]], base=0, channel_multiplier=0,
                   allow_small_or_imprecise_dtypes=True)
            g.iota(tok_iota[:, :], pattern=[[P, KD]], base=0, channel_multiplier=1).then_inc(s_masks, 1)
            g.iota(zero_row[:, C_TOK:C_TOK + 1].bitcast(I32), pattern=[[0, 1]], base=T,
                   channel_multiplier=1).then_inc(s_template, 1)

            def take_tokens(p, col):
                g.tensor_copy(idx[p][:, :], tok_all[:, bass.ds(col, KD)]).then_inc(idx_ready[p], 1)

            def gather(p):
                for c in range(KD):
                    g.indirect_dma_start(xg[p][:, c, :], None, emb,
                                         bass.IndirectOffsetOnAxis(ap=idx[p][:, c:c + 1], axis=0))\
                        .then_inc(gathered[p], 16)

            pool.wait_ge(s_clamped, 1)
            for p in range(2):
                take_tokens(p, KD * p)
            for p in range(2):
                pool.wait_ge(idx_ready[p], p + 1)
                gather(p)
            for p in range(2):
                pool.sem_inc(hb_stored[p], hb_stored.credit)
            pool.sem_inc(rows_free.sem, rows_free.credit)
            pool.wait_ge(s_masks, 1)
            pool.wait_ge(s_consts, 16 * N_LOADS)
            pool.wait_ge(s_fill, 16)
            def gather_next(r, p):
                hold(pool, x_ready[p], x_ready.before(r, p))
                hold(pool, gathered[p], gathered.before(r, p))
                take_tokens(p, r.value(2 * KD, KD * p))
                hold(pool, idx_ready[p], idx_ready.now(r, p))
                gather(p)

            def norm_roots(r, p):
                pool.wait_ge(lnv_ready[p], lnv_ready.now(r, p))
                g.tensor_tensor(lnr[p][:, :, :].rearrange("p a c -> p (a c)"),
                                lnv[p][:, :, :].rearrange("p a c -> p (a c)"),
                                neg_half[:, :], ALU.pow).then_inc(lnr_ready[p], 1)

            def segment_inputs(r, p):
                pool.wait_ge(a_ready[p], a_ready.now(r, p))
                for c in range(KD):
                    g.tensor_tensor(seg[p][:, c, :, :], bc(tri[:, :].unsqueeze(1), [P, NH, P]),
                                    bc(a_[p][:, c, :].unsqueeze(2), [P, NH, P]), ALU.mult).then_inc(seg_in[p], 1)

            def decayed_x(r, p):
                pool.wait_ge(edec_ready[p], edec_ready.now(r, p))
                pool.wait_ge(xdt_ready[p], xdt_ready.now(r, p, 1))
                g.tensor_tensor(xdec[p][:, :].rearrange("p (h d) -> p h d", h=NH),
                                xdt[p][:, 0, :].rearrange("p (h d) -> p h d", h=NH),
                                bc(edec[p][:, :].unsqueeze(2), [P, NH, HD]), ALU.mult).then_inc(xdec_ready[p], 1)

            def skip_x(r, p, c):
                pool.wait_ge(xs_ready[p], xs_ready.now(r, p, c + 1))
                g.tensor_tensor(xs[p][:, c, :].rearrange("p (h d) -> p h d", h=NH),
                                xs[p][:, c, :].rearrange("p (h d) -> p h d", h=NH),
                                bc(dskip[:, :].unsqueeze(2), [P, NH, HD]), ALU.mult).then_inc(skip_ready[p], 1)

            def gated_root(r, p):
                pool.wait_ge(msq_ready[p], msq_ready.now(r, p))
                g.tensor_tensor(rms[p][:, :], msq[p][:, :], neg_half[:, 0:KD], ALU.pow).then_inc(rms_ready[p], 1)

            def second_root(r, p):
                pool.wait_ge(lv2_ready[p], lv2_ready.now(r, p))
                g.tensor_tensor(lr2[p][:, :], lv2[p][:, :], neg_half[:, 0:KD], ALU.pow).then_inc(lr2_ready[p], 1)

            def with_bias(r, p):
                pool.wait_ge(hb_stored[p], hb_stored.before(r, p))
                pool.wait_ge(h2_ready[p], h2_ready.now(r, p))
                g.tensor_tensor(hb[p][:, :, :], h2[p][:, :, :], bc(bias_b[:, :].unsqueeze(1), [P, KD, DM]),
                                ALU.add).then_inc(hb_ready[p], 1)

            def scatter_rows(t, p):
                hold(pool, slot_ready[p], slot_ready.now(t, p))
                for c in range(KD):
                    for k in range(2):
                        g.indirect_dma_start(
                            slots_dram, bass.IndirectOffsetOnAxis(ap=slot[p][:, 2 * c + k:2 * c + k + 1], axis=0),
                            rows[p][:, c, :], None, bounds_check=NSLOT - 1, oob_is_err=False)\
                            .then_inc(scattered[p], 16)

            def free_rows(t, p):
                pool.wait_ge(scattered[p], scattered.now(t, p))
                pool.sem_inc(rows_free[p], 1)

            def half(p, f, b, t):
                q = 1 - p
                if b:
                    decayed_x(b, q)
                    skip_x(b, q, 0)
                if f:
                    gather_next(f, p)
                if b:
                    skip_x(b, q, 1)
                if f:
                    norm_roots(f, p)
                if b:
                    gated_root(b, q)
                if t:
                    scatter_rows(t, p)
                if f:
                    segment_inputs(f, p)
                if b:
                    second_root(b, q)
                    with_bias(b, q)
                if t:
                    free_rows(t, p)

            run_batches(g.Fori, half, PAIRS)
            for p in range(2):
                pool.wait_ge(gathered[p], gathered.credit * (PAIRS + 1))

            pool.drain().then_inc(part_done, 1)

            pool.wait_ge(part_done, 4)
            pool.sem_inc(expert_added, 2)

            def split_weights(n, q):
                hold(pool, w_loaded, n * 32)
                hold(pool, y_psum, n * (2 * NG))
                g.tensor_copy(w_hi[q][:, :, :], w_raw[:, :, :]).then_inc(w_split, 1)
                pool.wait_ge(w_split, n * 2 - 1)
                g.tensor_tensor(w_lo[q][:, :, :], w_raw[:, :, :], w_hi[q][:, :, :].bitcast(F32), ALU.subtract)\
                    .then_inc(w_split, 1)

            def add_results(n, q):
                for j in range(JS):
                    if j % 2 == 0:
                        hold(pool, ye_ready, n * (JS // 2) + (2 + j // 2 + 1 - JS // 2))
                    g.indirect_dma_start(out, bass.IndirectOffsetOnAxis(ap=tok_slot[q][:, j:j + 1], axis=0),
                                         ye[q][:, j, :], None, compute_op=ALU.add).then_inc(added, 16)
                    hold(pool, added, n * (16 * JS) + (16 * j + 16 - 16 * JS))
                pool.sem_inc(expert_added, 1)

            split_weights(1, 0)
            with g.Fori(1, NE // 2) as r:
                for q in range(2):
                    split_weights(r * 2 + q, 1 - q)
                    add_results(r * 2 + (q - 1), q)
            split_weights(NE, 1)
            add_results(NE - 1, 0)
            add_results(NE, 1)

        @block.scalar
        def _(act):
            sc = nc.scalar
            act.wait_ge(s_consts, 16 * N_LOADS)
            sc.activation(neg_a[:, :], alog[:, :], ACT.Exp).then_inc(s_nega, 1)
            act.wait_ge(s_wqk, 1)
            sc.activation(wqk[:, :, :].rearrange("p k n -> p (k n)"), bank[0][0][:, :], ACT.Copy,
                          scale=float(DM) ** -0.5).then_inc(s_wqk, 1)

            def copy(dst, src, signal_, func=ACT.Copy, **kw):
                sc.activation(dst, src, func, **kw).then_inc(signal_, 1)

            def flat(t):
                return t.rearrange("p a b -> p (a b)")

            def transposed_x(r, p):
                act.wait_ge(xT_psum[p], xT_psum.now(r, p))
                copy(flat(xT[p][:, :, :]), bank[p][0][:, :], xT_ready[p])

            def query_side(r, p):
                act.wait_ge(tT_psum[p], tT_psum.now(r, p))
                copy(flat(tT[p][:, :, :]), bank[p][1][:, :], tT_ready[p])

            def score_exps(r, p):
                act.wait_ge(nmax_ready[p], nmax_ready.now(r, p))
                for c in range(KD):
                    ins = sc.activation(probs[p][:, c, :], bank[p][3][:, c * L:(c + 1) * L], ACT.Exp,
                                        bias=nmax[p][:, c:c + 1], accum_out=rsum[p][:, c:c + 1])
                ins.then_inc(probs_ready[p], 1)

            def residuals(r, p):
                act.wait_ge(hu_coef[p], hu_coef.now(r, p))
                act.wait_ge(hn_ready[p], hn_ready.now(r, p))
                for c in range(KD):
                    ins = sc.activation(hu[p][:, c, :], bank[p][0][:, c * DM:(c + 1) * DM], ACT.Identity,
                                        scale=hu_s[p][:, c:c + 1], bias=hu_b[p][:, c:c + 1])
                ins.then_inc(hu_ready[p], 1)

            def mixer_input(r, p):
                act.wait_ge(hnT_psum[p], hnT_psum.now(r, p))
                for k in range(KD):
                    ins = sc.activation(hT[p][:, k, :], bank[p][1][:, k * L:(k + 1) * L], ACT.Identity,
                                        scale=lnw[:, k:k + 1], bias=lnb[:, k:k + 1])
                ins.then_inc(hT_ready[p], 1)

            def dt_exp(r, p):
                act.wait_ge(dtn_ready[p], dtn_ready.now(r, p))
                copy(flat(dtw[p][:, :, :]), flat(dtn[p][:, :, :]), dtw_ready[p], ACT.Exp)

            def last_tap(r, p, i):
                j = GROUPS[i]
                act.wait_ge(xbc_psum[p], xbc_psum.now(r, p, i + 1))
                for h in range(2):
                    m = 2 * j + h
                    ins = sc.activation(xc[p][:, m, :], bank[p][XBC_BANK[i]][:, h * L:(h + 1) * L], ACT.Identity,
                                        scale=cw[:, m, TAPS - 1:TAPS], bias=cb[:, m:m + 1])
                ins.then_inc(tap_ready[p], 1)

            def tanh_conv(r, p, i):
                j = GROUPS[i]
                act.wait_ge(conv_done[p], conv_done.now(r, p, i + 1))
                copy(th[p][:, j, :], flat(xc[p][:, 2 * j:2 * j + 2, :]), th_ready[p], ACT.Tanh)

            def tanh_z(r, p, c):
                act.wait_ge(z_psum[p], z_psum.now(r, p, c + 1))
                copy(sz[p][:, c, :], bank[p][Z_BANK[c]][:, :], tz_ready[p], ACT.Tanh)

            def state_inputs(r, p):
                act.wait_ge(btg_psum[p], btg_psum.now(r, p))
                sc.activation(bs[p][:, :], bank[p][3][:, 0:NS], ACT.Copy)
                copy(ea[p][:, :], bank[p][3][:, 3 * P:3 * P + NH], bs_ready[p], ACT.Exp)

            def decay(r, p, i):
                act.wait_ge(seg_psum[p], seg_psum.now(r, p, i + 1))
                c, half_ = i // 2, i % 2
                copy(seg[p][:, c, 4 * half_:4 * half_ + 4, :].rearrange("p h l -> p (h l)"),
                     bank[p][SEG_BANK[i]][:, :], decay_ready[p], ACT.Exp)

            def end_decay(r, p):
                act.wait_ge(decay_ready[p], decay_ready.now(r, p, 2))
                copy(edec[p][:, :], seg[p][:, 0, :, P - 1], edec_ready[p])

            def x_rows(r, p, c):
                act.wait_ge(xs_psum[p], xs_psum.now(r, p, c + 1))
                copy(xs[p][:, c, :], bank[p][XS_BANK[c]][:, :], xs_ready[p])

            def state(r, p):
                act.wait_ge(state_psum[p], state_psum.now(r, p))
                copy(st[p][:, :], bank[p][3][:, :], st_ready[p])

            def squares(r, p):
                act.wait_ge(y_ready[p], y_ready.now(r, p))
                for c in range(KD):
                    ins = sc.activation(th[p][:, c, :], y[p][:, c, :], ACT.Square, accum_out=ss[p][:, c:c + 1])
                ins.then_inc(ss_ready[p], 1)

            def transposed_y(r, p, c):
                act.wait_ge(yT_psum[p], yT_psum.now(r, p, c + 1))
                copy(flat(yT[p][:, c, :, :]), bank[p][YT_BANK[c]][:, :], yT_ready[p])

            def transposed_rows(t, p):
                act.wait_ge(v2T_psum[p], v2T_psum.now(t, p))
                copy(flat(v2T[p][:, :, :]), bank[p][0][:, :], v2T_ready[p])

            def router_exp(t, p):
                act.wait_ge(lg_ready[p], lg_ready.now(t, p))
                copy(flat(le[p][:, :, :]), flat(lg[p][:, :, :]), le_ready[p], ACT.Exp)

            def half(p, f, b, t):
                q = 1 - p
                if f:
                    transposed_x(f, p)
                if b:
                    tanh_conv(b, q, 1); tanh_conv(b, q, 2)
                if f:
                    query_side(f, p)
                if b:
                    state_inputs(b, q)
                    decay(b, q, 0)
                    tanh_z(b, q, 1)
                    x_rows(b, q, 0)
                    decay(b, q, 1)
                    end_decay(b, q)
                if f:
                    score_exps(f, p)
                if b:
                    x_rows(b, q, 1)
                    decay(b, q, 2); decay(b, q, 3)
                if t:
                    transposed_rows(t, p)
                if b:
                    state(b, q)
                if f:
                    residuals(f, p)
                    mixer_input(f, p)
                if b:
                    transposed_y(b, q, 0)
                if t:
                    router_exp(t, p)
                if b:
                    squares(b, q)
                if f:
                    dt_exp(f, p)
                    last_tap(f, p, 0)
                if b:
                    transposed_y(b, q, 1)
                if f:
                    last_tap(f, p, 1)
                    last_tap(f, p, 2)
                    tanh_conv(f, p, 0); tanh_z(f, p, 0)

            run_batches(sc.Fori, half, PAIRS)
            act.drain().then_inc(part_done, 1)

            act.wait_ge(part_done, 4)
            act.sem_inc(hhi_ready, H_BANKS)
            with sc.Fori(1, NE // 2 + 1) as r:
                for g in range(2 * NG):
                    for m in range(KF):
                        i = KF * g + m
                        act.wait_ge(h_psum, r * PER_TURN + (i + 1 - PER_TURN))
                        act.wait_ge(hlo_ready, r * PER_TURN + (i + 1 - PER_TURN))
                        sc.activation(hf[m % 2][:, :], h_bank[i % H_BANKS][:, :], ACT.Gelu_apprx_tanh)\
                            .then_inc(hf_ready, 1)
                        sc.activation(h_hi[:, m, :], h_bank[i % H_BANKS][:, :], ACT.Gelu_apprx_tanh)\
                            .then_inc(hhi_ready, 1)

        @block.vector
        def _(dve):
            vc = nc.vector

            def flat(t):
                return t.rearrange("p a b -> p (a b)")

            def heads(t):
                return t.rearrange("p (h d) -> p h d", h=NH)

            prep = Chain(dve, s_prep, 0)
            dve.wait_ge(s_tok, 16)
            prep.mark(vc.tensor_scalar(tok_neg[:, :], tok_all[:, 0:N_TILES], 0.0, float(VOCAB), ALU.is_lt, ALU.mult))
            prep.wait()
            prep.mark(vc.tensor_tensor(tok_neg[:, :], tok_neg[:, :], tok_all[:, 0:N_TILES], ALU.add))
            prep.wait()
            vc.tensor_scalar(tok_all[:, 0:N_TILES], tok_neg[:, :], 0.0, float(VOCAB - 1), ALU.max, ALU.min)\
                .then_inc(s_clamped, 1)
            dve.wait_ge(s_consts, 16 * N_LOADS)
            vc.tensor_scalar(cw[:, :, :], cw[:, :, :], 0.5, None, ALU.mult)
            vc.tensor_scalar(cb[:, :], cb[:, :], 0.5, None, ALU.mult)
            vc.tensor_scalar(w_in[:, :, 0:DI], w_in[:, :, 0:DI], 0.5, None, ALU.mult)
            for k in range(KI):
                vc.tensor_scalar(w_out[:, k, :], w_out[:, k, :], nw[:, k:k + 1], None, ALU.mult)
            dve.wait_ge(s_nega, 1)
            prep.mark(vc.tensor_scalar(neg_a[:, :], neg_a[:, :], -1.0, None, ALU.mult))
            prep.wait()

            def embed(p):
                vc.scalar_tensor_tensor(out=flat(x[p][:, :, :]), in0=flat(xg[p][:, :, :]), scalar=float(DM) ** 0.5,
                                        in1=flat(pos[:, :, :]), op0=ALU.mult, op1=ALU.add).then_inc(x_ready[p], 1)

            for sig in (h2_ready, slot_ready, pos_taken):
                dve.sem_inc(sig.sem, sig.credit)
            dve.wait_ge(gathered[0], gathered.credit)
            embed(0)

            def embed_next(r, p):
                q = 1 - p
                dve.wait_ge(gathered[q], gathered.before(r, q) if q == 1 else gathered.now(r, q))
                embed(q)

            def half(p, f, b, t):
                front = Chain(dve, front_chain, FRONT_LINKS, f, p)
                back = Chain(dve, back_chain, BACK_LINKS, b, 1 - p)
                routing = Chain(dve, routing_chain, ROUTING_LINKS, t, p)

                def norm_stats(ch, p, src, st6, mean_var):
                    for c in range(KD):
                        last = ch.mark(vc.bn_stats(st6[:, c, :], src[:, c, :]))
                    hold(dve, ch.sem, ch.value(last))
                    for c in range(KD):
                        last = ch.mark(vc.bn_aggr(mean_var[:, c, :], st6[:, c, :]))
                    ch.wait()

                def query_max(r, p):
                    dve.wait_ge(st_psum[p], st_psum.now(r, p))
                    vc.tensor_reduce(nmax[p][:, :], bank[p][3][:, :].rearrange("p (c q) -> p c q", c=KD), AX.X,
                                     ALU.max, negate=True).then_inc(nmax_ready[p], 1)

                def scale_v(r, p):
                    dve.wait_ge(probs_ready[p], probs_ready.now(r, p))
                    front.mark(vc.reciprocal(rinv[p][:, :], rsum[p][:, :]))
                    front.wait()
                    dve.wait_ge(v_psum[p], v_psum.now(r, p))
                    vc.tensor_tensor(v[p][:, :, :], bank[p][2][:, :].rearrange("p (c d) -> p c d", c=KD),
                                     bc(rinv[p][:, :].unsqueeze(2), [P, KD, DM]), ALU.mult).then_inc(v_ready[p], 1)

                def norm_1(r, p):
                    dve.wait_ge(o_psum[p], o_psum.now(r, p))
                    norm_stats(front, p, bank[p][0][:, :].rearrange("p (c d) -> p c d", c=KD), stats[p], mv[p])
                    vc.tensor_scalar(lnv[p][:, 0, :], mv[p][:, :, 1], EPS, None, ALU.add)
                    vc.tensor_scalar(lnv[p][:, 1, :], mv[p][:, :, 1], 1.0 + EPS, EPS * EPS, ALU.mult, ALU.add)\
                        .then_inc(lnv_ready[p], 1)

                def apply_norm_1(r, p):
                    dve.wait_ge(lnr_ready[p], lnr_ready.now(r, p))
                    for c in range(KD):
                        ins = vc.tensor_scalar(hn[p][:, c, :], bank[p][0][:, c * DM:(c + 1) * DM],
                                               mv[p][:, c, 0:1], lnr[p][:, 1, c:c + 1], ALU.subtract, ALU.mult)
                    ins.then_inc(hn_ready[p], 1)
                    vc.tensor_scalar(hu_s[p][:, :], lnr[p][:, 0, :], 1.0, None, ALU.add)
                    vc.scalar_tensor_tensor(out=hu_b[p][:, :], in0=mv[p][:, :, 0], scalar=-1.0, in1=lnr[p][:, 0, :],
                                            op0=ALU.mult, op1=ALU.mult).then_inc(hu_coef[p], 1)

                def dt_in(r, p):
                    dve.wait_ge(dt_psum[p], dt_psum.now(r, p))
                    front.mark(vc.tensor_tensor(dty[p][:, :, :], bank[p][1][:, 0:KD * NH].rearrange("p (c h) -> p c h", c=KD),
                                             bc(dtb[:, :].unsqueeze(1), [P, KD, NH]), ALU.add))
                    front.wait()
                    vc.scalar_tensor_tensor(out=dtn[p][:, :, :], in0=dty[p][:, :, :], scalar=-1.0, in1=dty[p][:, :, :],
                                            op0=ALU.mult, op1=ALU.min).then_inc(dtn_ready[p], 1)

                def softplus(r, p, n):
                    w, q_, s_, poly = (flat(x_[p][:, :, :]) for x_ in (dtw, dtq, dts, dtp))
                    terms = len(LOG_TERMS)
                    if n == 0:
                        dve.wait_ge(dtw_ready[p], dtw_ready.now(r, p))
                        ins = vc.tensor_scalar(q_, w, 2.0, None, ALU.add)
                    elif n <= terms + 7:
                        front.wait(softplus.last)
                    if n == 1:
                        ins = vc.reciprocal(q_, q_)
                    elif n == 2:
                        ins = vc.tensor_tensor(s_, w, q_, ALU.mult)
                    elif n == 3:
                        ins = vc.tensor_tensor(q_, s_, s_, ALU.mult)
                    elif n == 4:
                        ins = vc.tensor_scalar(poly, q_, LOG_TERMS[0], None, ALU.mult)
                    elif 4 < n < 4 + terms:
                        ins = vc.scalar_tensor_tensor(out=poly, in0=poly, scalar=LOG_TERMS[n - 4], in1=q_,
                                                      op0=ALU.add, op1=ALU.mult)
                    elif n == terms + 4:
                        ins = vc.scalar_tensor_tensor(out=poly, in0=poly, scalar=1.0, in1=s_,
                                                      op0=ALU.add, op1=ALU.mult)
                    elif n == terms + 5:
                        ins = vc.tensor_scalar(poly, poly, 2.0, None, ALU.mult)
                    elif n == terms + 6:
                        ins = vc.scalar_tensor_tensor(out=flat(dt_[p][:, :, :]), in0=flat(dty[p][:, :, :]), scalar=0.0,
                                                      in1=poly, op0=ALU.max, op1=ALU.add)
                    elif n == terms + 7:
                        vc.tensor_tensor(a_[p][:, :, :], dt_[p][:, :, :], bc(neg_a[:, :].unsqueeze(1), [P, KD, NH]),
                                         ALU.mult).then_inc(a_ready[p], 1)
                    if n < terms + 7:
                        softplus.last = front.mark(ins)

                def conv(r, p, i):
                    j = GROUPS[i]
                    dve.wait_ge(tap_ready[p], tap_ready.now(r, p, i + 1))
                    done = [None, None]
                    for back in range(1, TAPS):
                        for h in range(2):
                            m = 2 * j + h
                            if done[h]:
                                front.wait(done[h])
                            ins = vc.scalar_tensor_tensor(
                                out=xc[p][:, m, back:], in0=bank[p][XBC_BANK[i]][:, h * L:(h + 1) * L - back],
                                scalar=cw[:, m, TAPS - 1 - back:TAPS - back], in1=xc[p][:, m, back:],
                                op0=ALU.mult, op1=ALU.add)
                            if back < TAPS - 1:
                                done[h] = front.mark(ins)
                            elif h == 1:
                                ins.then_inc(conv_done[p], 1)
                            softplus(r, p, 3 + 2 * (TAPS - 1) * i + 2 * (back - 1) + h)

                def gate_conv(r, p, i):
                    j = GROUPS[i]
                    dve.wait_ge(th_ready[p], th_ready.now(r, p, i + 1))
                    both = flat(xc[p][:, 2 * j:2 * j + 2, :])
                    vc.scalar_tensor_tensor(out=both, in0=th[p][:, j, :], scalar=1.0, in1=both,
                                            op0=ALU.add, op1=ALU.mult).then_inc(xc_ready[p], 1)

                def gate_z(r, p, c):
                    dve.wait_ge(tz_ready[p], tz_ready.now(r, p, c + 1))
                    vc.scalar_tensor_tensor(out=sz[p][:, c, :], in0=sz[p][:, c, :], scalar=1.0,
                                            in1=bank[p][Z_BANK[c]][:, :], op0=ALU.add, op1=ALU.mult)\
                        .then_inc(sz_ready[p], 1)

                def mask_scores(r, p):
                    dve.wait_ge(bs_ready[p], bs_ready.now(r, p))
                    vc.tensor_tensor(gm[p][:, :, :], bank[p][3][:, P:3 * P].rearrange("p (c l) -> p c l", c=KD),
                                     bc(tri[:, :].unsqueeze(1), [P, KD, P]), ALU.mult).then_inc(gm_ready[p], 1)

                def times_dt(r, p, c):
                    dve.wait_ge(xs_ready[p], xs_ready.now(r, p, c + 1))
                    vc.tensor_tensor(heads(xdt[p][:, c, :]), heads(bank[p][XS_BANK[c]][:, :]),
                                     bc(dt_[p][:, c, :].unsqueeze(2), [P, NH, HD]), ALU.mult).then_inc(xdt_ready[p], 1)

                def decay_scores(r, p, c):
                    dve.wait_ge(decay_ready[p], decay_ready.now(r, p, 2 * c + 2))
                    dve.wait_ge(edec_ready[p], edec_ready.now(r, p))
                    dve.wait_ge(gm_ready[p], gm_ready.now(r, p))
                    vc.tensor_tensor(seg[p][:, c, :, :], seg[p][:, c, :, :], bc(gm[p][:, c, :].unsqueeze(1), [P, NH, P]),
                                     ALU.mult).then_inc(m_ready[p], 1)

                def gated_y(r, p, c):
                    if c == 0:
                        dve.wait_ge(yd_psum[p], yd_psum.now(r, p, 1))
                        dve.wait_ge(skip_ready[p], skip_ready.now(r, p, 1))
                        back.mark(vc.tensor_tensor(y[p][:, 0, :], bank[p][YD_BANK[0]][:, :], xs[p][:, 0, :], ALU.add))
                        back.wait()
                    else:
                        dve.wait_ge(yo_psum[p], yo_psum.now(r, p))
                        back.mark(vc.tensor_tensor(heads(y[p][:, 1, :]), heads(bank[p][2][:, :]),
                                                 bc(ea[p][:, :].unsqueeze(2), [P, NH, HD]), ALU.mult))
                        back.wait()
                        dve.wait_ge(skip_ready[p], skip_ready.now(r, p, 2))
                        back.mark(vc.tensor_tensor(y[p][:, 1, :], y[p][:, 1, :], xs[p][:, 1, :], ALU.add))
                        back.wait()
                        back.mark(vc.tensor_tensor(y[p][:, 1, :], bank[p][YD_BANK[1]][:, :], y[p][:, 1, :], ALU.add))
                        back.wait()
                    vc.tensor_tensor(y[p][:, c, :], y[p][:, c, :], sz[p][:, c, :], ALU.mult).then_inc(y_ready[p], 1)

                def mean_square(r, p):
                    dve.wait_ge(ss_ready[p], ss_ready.now(r, p))
                    vc.tensor_scalar(msq[p][:, :], ss[p][:, :], 1.0 / DI, EPS, ALU.mult, ALU.add)\
                        .then_inc(msq_ready[p], 1)

                def residual(r, p):
                    dve.wait_ge(out_psum[p], out_psum.now(r, p))
                    dve.wait_ge(rms_ready[p], rms_ready.now(r, p))
                    dve.wait_ge(hu_ready[p], hu_ready.now(r, p))
                    for c in range(KD):
                        ins = vc.scalar_tensor_tensor(out=h2[p][:, c, :], in0=bank[p][0][:, c * DM:(c + 1) * DM],
                                                      scalar=rms[p][:, c:c + 1], in1=hu[p][:, c, :],
                                                      op0=ALU.mult, op1=ALU.add)
                    ins.then_inc(h2_ready[p], 1)
                    hold(dve, h2_ready[p], h2_ready.now(r, p))
                    norm_stats(back, p, h2[p], stats2[p], mv2[p])
                    vc.tensor_scalar(lv2[p][:, :], mv2[p][:, :, 1], EPS, None, ALU.add).then_inc(lv2_ready[p], 1)

                def norm_2(t, p):
                    dve.wait_ge(lr2_ready[p], lr2_ready.now(t, p))
                    dve.wait_ge(rows_free[p], rows_free.before(t, p))
                    for c in range(KD):
                        ins = vc.tensor_scalar(rows[p][:, c, 0:DM], h2[p][:, c, :], mv2[p][:, c, 0:1],
                                               lr2[p][:, c:c + 1], ALU.subtract, ALU.mult)
                    ins.then_inc(v2_ready[p], 1)

                def router_in(t, p):
                    dve.wait_ge(logit_psum[p], logit_psum.now(t, p))
                    logits = bank[p][3][:, 0:KD * NE].rearrange("p (c e) -> p c e", c=KD)
                    routing.mark(vc.tensor_reduce(lmax[p][:, :], logits, AX.X, ALU.max, negate=True))
                    routing.wait()
                    vc.tensor_tensor(lg[p][:, :, :], logits, bc(lmax[p][:, :].unsqueeze(2), [P, KD, NE]), ALU.add)\
                        .then_inc(lg_ready[p], 1)

                def router_top(t, p):
                    dve.wait_ge(le_ready[p], le_ready.now(t, p))
                    routing.mark(vc.tensor_reduce(lsum[p][:, :], le[p][:, :, :], AX.X, ALU.add))
                    routing.wait()
                    routing.mark(vc.reciprocal(linv[p][:, :], lsum[p][:, :]))
                    routing.wait()
                    last = routing.mark(vc.tensor_tensor(pr[p][:, :, :], le[p][:, :, :],
                                                    bc(linv[p][:, :].unsqueeze(2), [P, KD, NE]), ALU.mult))
                    hold(dve, routing.sem, routing.value(last))
                    for c in range(KD):
                        last = routing.mark(vc.max(top[p][:, c, :], pr[p][:, c, :]))
                    hold(dve, routing.sem, routing.value(last))
                    for c in range(KD):
                        routing.mark(vc.max_index(topi[p][:, c, :], top[p][:, c, :], pr[p][:, c, :]))
                    routing.wait()
                    routing.mark(vc.tensor_copy(topf[p][:, :, :], topi[p][:, :, 0:2]))
                    routing.wait()
                    routing.mark(vc.tensor_tensor(oh[p][:, :, :, :].rearrange("p c k e -> p (c k) e"),
                                             bc(e_iota[:, :].unsqueeze(1), [P, 2 * KD, NE]),
                                             bc(flat(topf[p][:, :, :]).unsqueeze(2), [P, 2 * KD, NE]), ALU.is_equal))
                    routing.wait()
                    vc.tensor_tensor(ohs[p][:, :, :], oh[p][:, :, 0, :], oh[p][:, :, 1, :], ALU.add)\
                        .then_inc(ohs_ready[p], 1)
                    vc.tensor_copy(rows[p][:, :, C_W0:C_W0 + 2], top[p][:, :, 0:2])
                    vc.tensor_copy(rows[p][:, :, C_E0], topf[p][:, :, 0])
                    routing.mark(vc.tensor_copy(rows[p][:, :, C_TOK].bitcast(I32), tok_iota[:, :]))

                def slots_of(t, p):
                    dve.wait_ge(pos_psum[p], pos_psum.now(t, p))
                    dve.wait_ge(slot_ready[p], slot_ready.before(t, p))
                    vc.tensor_tensor(ohp[p][:, :, :, :], oh[p][:, :, :, :],
                                     bc(bank[p][1][:, 0:KD * NE].rearrange("p (c e) -> p c e", c=KD).unsqueeze(2),
                                        [P, KD, 2, NE]), ALU.mult).then_inc(pos_taken[p], 1)
                    dve.wait_ge(pos_taken[p], pos_taken.now(t, p))
                    routing.mark(vc.tensor_reduce(offs[p][:, :], ohp[p][:, :, :, :].rearrange("p c k e -> p (c k) e"),
                                             AX.X, ALU.add))
                    routing.wait()
                    vc.scalar_tensor_tensor(out=sl[p][:, :], in0=flat(topf[p][:, :, :]), scalar=float(CAP),
                                            in1=offs[p][:, :], op0=ALU.mult, op1=ALU.add)
                    routing.mark(vc.tensor_scalar(valid[p][:, :], offs[p][:, :], float(CAP), None, ALU.is_lt))
                    routing.wait()
                    routing.mark(vc.scalar_tensor_tensor(out=sl[p][:, :], in0=sl[p][:, :], scalar=-float(NSLOT),
                                                    in1=valid[p][:, :], op0=ALU.add, op1=ALU.mult))
                    routing.wait()
                    vc.tensor_scalar(slot[p][:, :], sl[p][:, :], float(NSLOT), None, ALU.add).then_inc(slot_ready[p], 1)

                def count_choices(p):
                    for c in range(KD):
                        routing.mark(vc.tensor_tensor(oh_sum[:, :], oh_sum[:, :], ohs[p][:, c, :], ALU.add))
                        routing.wait()
                    routing.mark(vc.tensor_scalar(tok_iota[:, :], tok_iota[:, :], float(L), None, ALU.add))
                    routing.wait()

                q = 1 - p
                if b:
                    gate_conv(b, q, 1); gate_conv(b, q, 2)
                if t:
                    norm_2(t, p)
                if b:
                    mask_scores(b, q)
                if f:
                    embed_next(f, p)
                if b:
                    gate_z(b, q, 1)
                    times_dt(b, q, 0)
                if f:
                    query_max(f, p)
                if b:
                    decay_scores(b, q, 0)
                if f:
                    scale_v(f, p)
                if b:
                    times_dt(b, q, 1)
                    decay_scores(b, q, 1)
                if f:
                    norm_1(f, p)
                if b:
                    gated_y(b, q, 0)
                if t:
                    router_in(t, p)
                if f:
                    apply_norm_1(f, p)
                if b:
                    gated_y(b, q, 1)
                if f:
                    dt_in(f, p)
                if t:
                    router_top(t, p)
                if b:
                    mean_square(b, q)
                if f:
                    for n in range(3):
                        softplus(f, p, n)
                    conv(f, p, 0)
                    conv(f, p, 1)
                if t:
                    slots_of(t, p)
                    count_choices(p)
                    routing.close()
                if b:
                    residual(b, q)
                    back.close()
                if f:
                    conv(f, p, 2)
                    gate_conv(f, p, 0)
                    gate_z(f, p, 0)
                    front.close()

            run_batches(vc.Fori, half, PAIRS)
            dve.drain().then_inc(part_done, 1)

            dve.wait_ge(part_done, 4)
            dve.sem_inc(xe_split, 1)
            dve.sem_inc(hlo_ready, 2)
            dve.sem_inc(ye_ready, 2)
            prep.mark(vc.memset(e_now[:, :], 0.0))
            prep.wait()
            with vc.Fori(1, NE // 2 + 1) as r:
                ch = Chain(dve, moe_chain_sem, MOE_LINKS, Turn(r), 0, 1)

                def slot_infos(q):
                    dve.wait_ge(xe_loaded[q], xe_loaded.now(Turn(r), q))
                    dve.wait_ge(expert_added, r * 2 + (q - 1))
                    vc.tensor_tensor(wd[q][:, :], xe[q][:, :, C_W0], xe[q][:, :, C_W0 + 1], ALU.subtract)
                    ch.mark(vc.tensor_scalar(is_first[q][:, :], xe[q][:, :, C_E0], e_now[:, :], None, ALU.is_equal))
                    ch.wait()
                    ch.mark(vc.tensor_tensor(wd[q][:, :], wd[q][:, :], is_first[q][:, :], ALU.mult))
                    ch.wait()
                    vc.tensor_tensor(w_slot[q][:, :], wd[q][:, :], xe[q][:, :, C_W0 + 1], ALU.add)
                    vc.tensor_scalar(e_now[:, :], e_now[:, :], 1.0, None, ALU.add)
                    ch.mark(vc.tensor_copy(tok_slot[q][:, :], xe[q][:, :, C_TOK].bitcast(I32)))
                    hold(dve, ch.sem, ch.value(ch.count))
                    dve.sem_inc(slot_info, 1)

                def split_x(g):
                    dve.wait_ge(xeT_psum, r * (2 * NG) + (g + 1 - 2 * NG))
                    for k in range(KD):
                        vc.tensor_copy(xe_hi[g % 2][:, k, :], x_bank[k][:, :]).then_inc(x_half, 1)
                    for k in range(KD):
                        dve.wait_ge(x_half, r * (2 * NG * KD) + (g * KD + k + 1 - 2 * NG * KD))
                        ins = vc.tensor_tensor(xe_lo[g % 2][:, k, :], x_bank[k][:, :], xe_hi[g % 2][:, k, :].bitcast(F32),
                                               ALU.subtract)
                    ins.then_inc(xe_split, 1)

                def split_h(g):
                    for m in range(KF):
                        i = KF * g + m
                        dve.wait_ge(hhi_ready, r * PER_TURN + (H_BANKS + i + 1 - PER_TURN))
                        vc.tensor_tensor(h_lo[:, m, :], hf[m % 2][:, :], h_hi[:, m, :].bitcast(F32), ALU.subtract)\
                            .then_inc(hlo_ready, 1)

                def weigh(g):
                    q, half = g // NG, g % NG
                    for b in range(2):
                        j = 4 * half + 2 * b
                        dve.wait_ge(y_psum, r * (4 * NG) + (Y0 + 2 * g + b + 1 - 4 * NG))
                        vc.tensor_tensor(ye[q][:, j:j + 2, :], y_bank[b][:, :].rearrange("p (j d) -> p j d", j=2),
                                         bc(w_slot[q][:, j:j + 2].unsqueeze(2), [P, 2, DM]), ALU.mult)\
                            .then_inc(ye_ready, 1)

                slot_infos(0)
                split_x(0)
                for g in range(2 * NG):
                    split_h(g)
                    if g + 1 == NG:
                        slot_infos(1)
                    if g + 1 < 2 * NG:
                        split_x(g + 1)
                    weigh(g)
                ch.close()

        @block.tensor
        def _(pe):
            te = nc.tensor

            pe.wait_ge(s_consts, 16 * N_LOADS)
            pe.wait_ge(s_masks, 1)
            for m in range(KD):
                for k in range(KD):
                    ins = te.matmul(bank[0][0][:, m * DM:(m + 1) * DM], wqk_in[:, 0, k, m * P:(m + 1) * P],
                                    wqk_in[:, 1, k, :], start=(k == 0), stop=(k == KD - 1))
            ins.then_inc(s_wqk, 1)
            pe.wait_ge(s_wqk, 2)
            pe.wait_ge(s_prep, 3)

            def transposes(p, b, srcs):
                for n, src in enumerate(srcs):
                    ins = te.transpose(bank[p][b][:, n * P:(n + 1) * P], src, ident[:, :])
                return ins

            def half(p, f, b, t):
                def to_xT(r, p):
                    pe.wait_ge(x_ready[p], x_ready.before(r, p))
                    pe.wait_ge(h2_ready[p], h2_ready.before(r, p))
                    transposes(p, 0, [x[p][:, c, k * P:(k + 1) * P] for k in range(KD) for c in range(KD)])\
                        .then_inc(xT_psum[p], 1)

                def query_side(r, p):
                    pe.wait_ge(xT_ready[p], xT_ready.now(r, p))
                    for m in range(KD):
                        for k in range(KD):
                            ins = te.matmul(bank[p][1][:, m * L:(m + 1) * L], wqk[:, k, m * P:(m + 1) * P],
                                            xT[p][:, k, :], start=(k == 0), stop=(k == KD - 1))
                    ins.then_inc(tT_psum[p], 1)
                    for c in range(KD):
                        for k in range(KD):
                            ins = te.matmul(bank[p][2][:, c * DM:(c + 1) * DM], xT[p][:, k, c * P:(c + 1) * P],
                                            wv[:, k, :], start=(k == 0), stop=(k == KD - 1))
                    ins.then_inc(v_psum[p], 1)

                def scores(r, p):
                    pe.wait_ge(tT_ready[p], tT_ready.now(r, p))
                    for c in range(KD):
                        for k in range(KD):
                            ins = te.matmul(bank[p][3][:, c * L:(c + 1) * L], xT[p][:, k, c * P:(c + 1) * P],
                                            tT[p][:, k, :], start=(k == 0), stop=(k == KD - 1))
                    ins.then_inc(st_psum[p], 1)

                def attend(r, p):
                    pe.wait_ge(v_ready[p], v_ready.now(r, p))
                    if t:
                        pe.wait_ge(v2T_ready[p], v2T_ready.now(t, p))
                    for c in range(KD):
                        for k in range(KD):
                            ins = te.matmul(bank[p][0][:, c * DM:(c + 1) * DM], probs[p][:, k, c * P:(c + 1) * P],
                                            v[p][:, k, :], start=(k == 0), stop=(k == KD - 1))
                    ins.then_inc(o_psum[p], 1)

                def to_hT(r, p):
                    pe.wait_ge(hn_ready[p], hn_ready.now(r, p))
                    transposes(p, 1, [hn[p][:, c, k * P:(k + 1) * P] for k in range(KD) for c in range(KD)])\
                        .then_inc(hnT_psum[p], 1)

                def project_dt(r, p):
                    pe.wait_ge(hT_ready[p], hT_ready.now(r, p))
                    for c in range(KD):
                        for k in range(KD):
                            ins = te.matmul(bank[p][1][:, c * NH:(c + 1) * NH], hT[p][:, k, c * P:(c + 1) * P],
                                            w_in[:, k, DI + CC:DI + CC + NH], start=(k == 0), stop=(k == KD - 1))
                    ins.then_inc(dt_psum[p], 1)

                def project_channels(r, p, i):
                    if i == 1 and t:
                        pe.wait_ge(lg_ready[p], lg_ready.now(t, p))
                    if i == 2:
                        pe.wait_ge(hu_ready[p], hu_ready.now(r, p))
                    for h in range(2):
                        m = 2 * GROUPS[i] + h
                        for k in range(KD):
                            ins = te.matmul(bank[p][XBC_BANK[i]][:, h * L:(h + 1) * L],
                                            w_in[:, k, DI + m * P:DI + (m + 1) * P], hT[p][:, k, :],
                                            start=(k == 0), stop=(k == KD - 1))
                    ins.then_inc(xbc_psum[p], 1)

                def project_z(r, p, c):
                    pe.wait_ge(conv_done[p], conv_done.now(r, p, 1 if c == 0 else 3))
                    for k in range(KD):
                        ins = te.matmul(bank[p][Z_BANK[c]][:, :], hT[p][:, k, c * P:(c + 1) * P], w_in[:, k, 0:DI],
                                        start=(k == 0), stop=(k == KD - 1))
                    ins.then_inc(z_psum[p], 1)

                def state_inputs(r, p):
                    pe.wait_ge(xc_ready[p], xc_ready.now(r, p, 1))
                    pe.wait_ge(conv_done[p], conv_done.now(r, p, 2))
                    pe.wait_ge(a_ready[p], a_ready.now(r, p))
                    te.transpose(bank[p][3][:, 0:P], xc[p][:, KI, 0:P], ident[:, :])
                    for c in range(KD):
                        te.matmul(bank[p][3][:, (c + 1) * P:(c + 2) * P], xc[p][:, KI, c * P:(c + 1) * P],
                                  xc[p][:, KI + 1, c * P:(c + 1) * P], start=True, stop=True)
                    te.matmul(bank[p][3][:, 3 * P:3 * P + NH], tri[:, :], a_[p][:, 1, :], start=True, stop=True)\
                        .then_inc(btg_psum[p], 1)

                def segment_sums(r, p, i):
                    c, half = i // 2, i % 2
                    pe.wait_ge(seg_in[p], seg_in.now(r, p, c + 1))
                    if i == 0:
                        pe.wait_ge(pos_taken[p], pos_taken.before(r, p))
                    if i == 1:
                        pe.wait_ge(bs_ready[p], bs_ready.now(r, p))
                        pe.wait_ge(gm_ready[p], gm_ready.now(r, p))
                    if i == 2:
                        pe.wait_ge(sz_ready[p], sz_ready.now(r, p, 2))
                    if i == 3:
                        pe.wait_ge(xs_ready[p], xs_ready.now(r, p, 1))
                        pe.wait_ge(xdt_ready[p], xdt_ready.now(r, p, 1))
                    te.matmul(bank[p][SEG_BANK[i]][:, :], below[:, :],
                              seg[p][:, c, 4 * half:4 * half + 4, :].rearrange("p h l -> p (h l)"),
                              start=True, stop=True).then_inc(seg_psum[p], 1)

                def x_to_rows(r, p, c):
                    if c == 0:
                        pe.wait_ge(sz_ready[p], sz_ready.now(r, p, 1))
                        pe.wait_ge(xc_ready[p], xc_ready.now(r, p))
                    else:
                        pe.wait_ge(decay_ready[p], decay_ready.now(r, p, 1))
                    transposes(p, XS_BANK[c], [xc[p][:, m, c * P:(c + 1) * P] for m in range(KI)])\
                        .then_inc(xs_psum[p], 1)

                def chunk_state(r, p):
                    pe.wait_ge(decay_ready[p], decay_ready.now(r, p, 2))
                    pe.wait_ge(bs_ready[p], bs_ready.now(r, p))
                    pe.wait_ge(xdec_ready[p], xdec_ready.now(r, p))
                    te.matmul(bank[p][3][:, :], bs[p][:, :], xdec[p][:, :], start=True, stop=True)\
                        .then_inc(state_psum[p], 1)

                def own_chunk(r, p, c):
                    pe.wait_ge(m_ready[p], m_ready.now(r, p, c + 1))
                    if c == 0:
                        pe.wait_ge(xs_ready[p], xs_ready.now(r, p, 2))
                        pe.wait_ge(xdt_ready[p], xdt_ready.now(r, p, 2))
                    for h in range(NH):
                        ins = te.matmul(bank[p][YD_BANK[c]][:, h * HD:(h + 1) * HD], seg[p][:, c, h, :],
                                        xdt[p][:, c, h * HD:(h + 1) * HD], start=True, stop=True)
                    ins.then_inc(yd_psum[p], 1)

                def from_state(r, p):
                    pe.wait_ge(st_ready[p], st_ready.now(r, p))
                    pe.wait_ge(decay_ready[p], decay_ready.now(r, p))
                    te.matmul(bank[p][2][:, :], xc[p][:, KI + 1, P:2 * P], st[p][:, :], start=True, stop=True)\
                        .then_inc(yo_psum[p], 1)

                def to_yT(r, p, c):
                    pe.wait_ge(y_ready[p], y_ready.now(r, p, c + 1))
                    transposes(p, YT_BANK[c], [y[p][:, c, k * P:(k + 1) * P] for k in range(KI)])\
                        .then_inc(yT_psum[p], 1)

                def project_out(r, p):
                    pe.wait_ge(yT_ready[p], yT_ready.now(r, p))
                    for c in range(KD):
                        for k in range(KI):
                            ins = te.matmul(bank[p][0][:, c * DM:(c + 1) * DM], yT[p][:, c, k, :], w_out[:, k, :],
                                            start=(k == 0), stop=(k == KI - 1))
                    ins.then_inc(out_psum[p], 1)

                def to_v2T(t, p):
                    pe.wait_ge(v2_ready[p], v2_ready.now(t, p))
                    transposes(p, 0, [rows[p][:, c, k * P:(k + 1) * P] for k in range(KD) for c in range(KD)])\
                        .then_inc(v2T_psum[p], 1)

                def route(t, p):
                    pe.wait_ge(v2T_ready[p], v2T_ready.now(t, p))
                    for c in range(KD):
                        for k in range(KD):
                            ins = te.matmul(bank[p][3][:, c * NE:(c + 1) * NE], v2T[p][:, k, c * P:(c + 1) * P],
                                            wr[:, k, :], start=(k == 0), stop=(k == KD - 1))
                    ins.then_inc(logit_psum[p], 1)

                def choices_before(t, p):
                    pe.wait_ge(ohs_ready[p], ohs_ready.now(t, p))
                    if f:
                        pe.wait_ge(dtn_ready[p], dtn_ready.now(f, p))
                    for c in range(KD):
                        dst = bank[p][1][:, c * NE:(c + 1) * NE]
                        te.matmul(dst, before_b[:, :], ohs[p][:, c, :], start=True, stop=False)
                        for cc in range(c):
                            te.matmul(dst, ones_b[:, :], ohs[p][:, cc, :], start=False, stop=False)
                        ins = te.matmul(dst, ones_b[:, :], oh_sum[:, :], start=False, stop=True)
                    ins.then_inc(pos_psum[p], 1)

                q = 1 - p
                if f:
                    to_xT(f, p)
                    query_side(f, p)
                if b:
                    state_inputs(b, q)
                    segment_sums(b, q, 0)
                    project_z(b, q, 1)
                    x_to_rows(b, q, 0)
                    segment_sums(b, q, 1)
                if f:
                    scores(f, p)
                if b:
                    x_to_rows(b, q, 1)
                    segment_sums(b, q, 2); segment_sums(b, q, 3)
                if t:
                    to_v2T(t, p)
                if b:
                    chunk_state(b, q)
                if f:
                    attend(f, p)
                if b:
                    own_chunk(b, q, 0)
                if t:
                    route(t, p)
                if b:
                    own_chunk(b, q, 1)
                if f:
                    to_hT(f, p)
                if b:
                    from_state(b, q)
                    to_yT(b, q, 0)
                if f:
                    project_dt(f, p)
                    project_channels(f, p, 0)
                if b:
                    to_yT(b, q, 1)
                if f:
                    project_channels(f, p, 1)
                if t:
                    choices_before(t, p)
                if b:
                    project_out(b, q)
                if f:
                    project_channels(f, p, 2)
                    project_z(f, p, 0)

            run_batches(te.Fori, half, PAIRS)
            pe.drain().then_inc(part_done, 1)

            pe.wait_ge(part_done, 4)
            pe.sem_inc(y_psum, Y0)

            def three(out_, hi, lo, rhi, rlo, first_, last_):
                te.matmul(out_, hi, rhi, start=first_, stop=False)
                te.matmul(out_, hi, rlo, start=False, stop=False)
                return te.matmul(out_, lo, rhi, start=False, stop=last_)

            with te.Fori(1, NE // 2 + 1) as r:
                def turn_x(g):
                    q, half = g // NG, g % NG
                    if half == 0:
                        pe.wait_ge(xe_loaded[q], xe_loaded.now(Turn(r), q))
                    pe.wait_ge(xe_split, r * (2 * NG) + (1 + g - 2 * NG))
                    for k in range(KD):
                        for j in range(4):
                            ins = te.transpose(x_bank[k][:, j * P:(j + 1) * P],
                                               xe[q][:, 4 * half + j, k * P:(k + 1) * P], ident[:, :])
                    ins.then_inc(xeT_psum, 1)

                def first_product(g):
                    q = g // NG
                    pe.wait_ge(w_split, r * 4 + (2 * q - 2))
                    pe.wait_ge(xe_split, r * (2 * NG) + (2 + g - 2 * NG))
                    for m in range(KF):
                        i = KF * g + m
                        pe.wait_ge(hhi_ready, r * PER_TURN + (i + 1 - PER_TURN))
                        for k in range(KD):
                            at = slice(k * FF + m * P, k * FF + (m + 1) * P)
                            ins = three(h_bank[i % H_BANKS][:, :], w_hi[q][:, 0, at], w_lo[q][:, 0, at],
                                        xe_hi[g % 2][:, k, :], xe_lo[g % 2][:, k, :], k == 0, k == KD - 1)
                        ins.then_inc(h_psum, 1)

                def second_product(g):
                    q = g // NG
                    for b in range(2):
                        pe.wait_ge(ye_ready, r * (4 * NG) + (2 * g + b + 1 - 4 * NG))
                        for j in (2 * b, 2 * b + 1):
                            dst = y_bank[b][:, (j % 2) * DM:(j % 2 + 1) * DM]
                            for m in range(KF):
                                if j == 0:
                                    pe.wait_ge(hlo_ready, r * PER_TURN + (2 + KF * g + m + 1 - PER_TURN))
                                at = slice(m * DM, (m + 1) * DM)
                                ins = three(dst, h_hi[:, m, j * P:(j + 1) * P], h_lo[:, m, j * P:(j + 1) * P],
                                            w_hi[q][:, 1, at], w_lo[q][:, 1, at], m == 0, m == KF - 1)
                        ins.then_inc(y_psum, 1)

                turn_x(0)
                for g in range(2 * NG):
                    first_product(g)
                    if g + 1 < 2 * NG:
                        turn_x(g + 1)
                    second_product(g)


def kernel(x, L0_tok_emb, L0_tok_w_q, L0_tok_w_k, L0_tok_w_v, L0_tok_pos_enc, L0_attn_ln_w, L0_attn_ln_b,
           L0_attn_in_proj_w, L0_attn_conv_w, L0_attn_conv_b, L0_attn_dt_bias, L0_attn_A_log, L0_attn_D,
           L0_attn_norm_w, L0_attn_out_proj_w, L0_ffn_w_router, L0_ffn_w1, L0_ffn_w2, L0_ffn_bias):
    import numpy as np
    import concourse.bacc as bacc
    from concourse.bass_utils import run_bass_kernel_spmd

    A = np.asarray
    x = A(x)
    nb, length = x.shape
    tokens = nb * length
    dm = A(L0_tok_emb).shape[1]
    ne, _, ff = A(L0_ffn_w1).shape

    def by_lane(a):
        a = A(a)
        return np.moveaxis(a.reshape(-1, P, *a.shape[1:]), 1, 0)

    laid_out = {
        "tokens": by_lane(x.reshape(-1)),
        "emb": A(L0_tok_emb),
        "w_qT": A(L0_tok_w_q).T, "w_kT": A(L0_tok_w_k).T, "w_v": A(L0_tok_w_v),
        "pos_enc": A(L0_tok_pos_enc)[:length],
        "ln_w": by_lane(L0_attn_ln_w), "ln_b": by_lane(L0_attn_ln_b),
        "in_wT": A(L0_attn_in_proj_w).T,
        "conv_w": by_lane(L0_attn_conv_w), "conv_b": by_lane(L0_attn_conv_b),
        "dt_bias": A(L0_attn_dt_bias)[None], "A_log": A(L0_attn_A_log)[None], "D_skip": A(L0_attn_D)[None],
        "norm_w": by_lane(L0_attn_norm_w),
        "out_wT": A(L0_attn_out_proj_w).T,
        "w_router": by_lane(L0_ffn_w_router),
        "w1": A(L0_ffn_w1).reshape(ne * dm, ff), "w2": A(L0_ffn_w2).reshape(ne * ff, dm),
        "bias": A(L0_ffn_bias).reshape(1, dm),
    }
    nc = bacc.Bacc("TRN2", target_bir_lowering=False, num_devices=1)
    arrays, aps = {}, {}
    for name, a in laid_out.items():
        arrays[name] = np.ascontiguousarray(a)
        aps[name] = nc.dram_tensor(name, a.shape, mybir.dt.from_np(a.dtype), kind="ExternalInput").ap()
    aps["out"] = nc.dram_tensor("out", (tokens + P, dm), F32, kind="ExternalOutput").ap()
    aps["slots_dram"] = nc.dram_tensor("slots_dram", (2 * tokens, dm + 4), F32).ap()
    lm_block(nc, **aps)
    r = run_bass_kernel_spmd(nc, [arrays], core_ids=[0])
    return r.results[0]["out"][:tokens].reshape(nb, length, dm)
```

```python
import concourse.bass as bass
from concourse import mybir
from contextlib import ExitStack

F32 = mybir.dt.float32
F32R = mybir.dt.float32r
BF16 = mybir.dt.bfloat16
I32 = mybir.dt.int32
U32 = mybir.dt.uint32
ALU = mybir.AluOpType
ACT = mybir.ActivationFunctionType
AX = mybir.AxisListType

P = 128
EPS = 1e-5
LOG_TERMS = [1.0 / (2 * n + 1) for n in range(7, 0, -1)]


class Turn:

    def __init__(self, reg, shift=0):
        self.reg, self.shift = reg, shift

    def value(self, factor, rest):
        return self.reg * factor + (self.shift * factor + rest)


class Signal:

    def __init__(self, sem, steps=1, credit=0):
        self.sem, self.steps, self.credit = sem, steps, credit

    def __getitem__(self, p):
        return self.sem

    def now(self, r, p, step=None):
        step = self.steps if step is None else step
        return r.value(2 * self.steps, self.credit - 2 * self.steps + p * self.steps + step)

    def before(self, r, p):
        assert self.credit == 2 * self.steps
        return r.value(2 * self.steps, (p - 1) * self.steps)


class DmaSignal:

    def __init__(self, sems, per_turn, credit=0):
        self.sems, self.per_turn, self.credit = sems, per_turn, credit

    def __getitem__(self, p):
        return self.sems[p]

    def now(self, r, p):
        return r.value(self.per_turn, self.credit)

    def before(self, r, p):
        assert self.credit == self.per_turn
        return r.value(self.per_turn, 0)


class Chain:

    def __init__(self, eng, sem, links, r=None, p=0, times=2):
        self.eng, self.sem, self.links, self.count = eng, sem, links, 0
        self.r, self.p, self.times = r, p, times

    def mark(self, ins):
        self.count += 1
        ins.then_inc(self.sem, 1)
        return self.count

    def wait(self, count=None):
        self.eng.wait_ge(self.sem, self.value(self.count if count is None else count))

    def value(self, count):
        if self.r is None:
            return count
        return self.r.value(self.times * self.links, (self.p - self.times) * self.links + count)

    def close(self):
        assert self.count == self.links, self.count


def hold(eng, sem, value):
    eng.wait_ge(sem, value)
    eng.sem_inc(hold.counts[eng.engine], 1)


def run_batches(loop, half, turns):
    half(0, Turn(1), None, None)
    half(1, Turn(1), Turn(1), None)
    with loop(2, turns + 1) as reg:
        half(0, Turn(reg), Turn(reg, -1), Turn(reg, -1))
        half(1, Turn(reg), Turn(reg), Turn(reg, -1))
    half(0, None, Turn(turns), Turn(turns))
    half(1, None, None, Turn(turns))


def lm_block(nc, tokens, emb, w_qT, w_kT, w_v, pos_enc, ln_w, ln_b, in_wT, conv_w, conv_b, dt_bias, A_log,
             D_skip, norm_w, out_wT, w_router, w1, w2, bias, out, slots_dram):
    N_TILES = tokens.shape[1]
    T = N_TILES * P
    VOCAB, DM = emb.shape
    KD = DM // P
    L = 2 * P
    NB = T // L
    PAIRS = NB // 2
    DI = out_wT.shape[0]
    NH = dt_bias.shape[1]
    HD = DI // NH
    KI = DI // P
    NS = P
    CC = DI + 2 * NS
    MC = CC // P
    TAPS = conv_w.shape[2]
    NE = w_router.shape[2]
    FF = w1.shape[1]
    KF = FF // P
    CAP = 2 * T // NE
    NSLOT = NE * CAP
    JS = CAP // P
    GW = 4 * P
    NG = CAP // GW
    ROW = slots_dram.shape[1]
    C_W0, C_E0, C_TOK = DM, DM + 2, DM + 3
    assert (L, KD, MC, NS, TAPS) == (256, 2, 6, 128, 4) and NH * P == 1024 and NE == 8 and HD * NH == 4 * P

    FRONT_LINKS, BACK_LINKS, RESIDUAL_LINKS, ROUTING_LINKS, MOE_LINKS, N_EARLY, N_LOADS = 34, 4, 4, 17, 3, 4, 12

    with ExitStack() as ctx:
        def sb(name, shape, dt=F32, c=ctx):
            return c.enter_context(nc.sbuf_tensor(name, shape, dt))

        def sem(name):
            return ctx.enter_context(nc.semaphore(name))

        def signal(name, steps=1, credit=0):
            return Signal(sem(name), steps, credit)

        def dma_signal(name, per_turn, credit=0):
            return DmaSignal([sem(f"{name}{p}") for p in range(2)], per_turn, credit)

        ident = sb("ident", [P, P])
        w_raw = sb("w_raw", [P, 2, KD * FF])
        zero_row = sb("zero_row", [P, ROW])
        tok_iota = sb("tok_iota", [P, KD], I32)

        W_IN = KD * in_wT.shape[1]
        staged = w_raw[:, :, :].rearrange("p w n -> p (w n)")
        w_in = staged[:, 0:W_IN].rearrange("p (k n) -> p k n", k=KD)
        wqk_in = staged[:, W_IN:W_IN + 2 * KD * DM].rearrange("p (s k n) -> p s k n", s=2, k=KD)

        first = ExitStack()
        fb = lambda name, shape, dt=F32: sb(name, shape, dt, first)
        tri = fb("tri", [P, P])
        below = fb("below", [P, P])
        before_b = fb("before_b", [P, P], BF16)
        ones_b = fb("ones_b", [P, P], BF16)
        neg_half = fb("neg_half", [P, 4])
        e_iota = fb("e_iota", [P, NE])
        tok_all = fb("tok_all", [P, N_TILES + 4], I32)
        tok_neg = fb("tok_neg", [P, N_TILES], I32)
        below_r = fb("below_r", [P, P], F32R)
        wqk = fb("wqk", [P, KD, DM])
        wv = fb("wv", [P, KD, DM])
        w_in_hi = fb("w_in_hi", [P, KD, in_wT.shape[1]], F32R)
        w_in_lo = fb("w_in_lo", [P, KD, in_wT.shape[1]], F32R)
        w_dt = fb("w_dt", [P, KD, NH])
        w_out = fb("w_out", [P, KI, DM])
        pos = fb("pos", [P, KD, DM])
        lnw = fb("lnw", [P, KD])
        lnb = fb("lnb", [P, KD])
        cw = fb("cw", [P, MC, TAPS])
        cb = fb("cb", [P, MC])
        nw = fb("nw", [P, KI])
        dtb = fb("dtb", [P, NH])
        alog = fb("alog", [P, NH])
        neg_a = fb("neg_a", [P, NH])
        dskip = fb("dskip", [P, NH])
        wr = fb("wr", [P, KD, NE])
        bias_b = fb("bias_b", [P, DM])
        oh_sum = fb("oh_sum", [P, NE], BF16)

        def pair(name, shape, dt=F32):
            return [fb(f"{name}{p}", shape, dt) for p in range(2)]

        idx = pair("idx", [P, KD], I32)
        xg = pair("xg", [P, KD, DM])
        x = pair("x", [P, KD, DM])

        def shared(later, *sooner):
            with ExitStack() as own:
                one = [sb(f"{later[0]}{p}", later[1], later[2], own) for p in range(2)]
            sets = [[fb(f"{name}{p}", shape) for name, shape in sooner] for p in range(2)]
            return [one] + [list(t) for t in zip(*sets)]

        th, xT, tT, probs = shared(("th", [P, 3, 2 * L], F32), ("xT", [P, KD, L]), ("tT", [P, KD, L]),
                                   ("probs", [P, KD, L]))
        v = pair("v", [P, KD, DM])
        hn = pair("hn", [P, KD, DM])
        hT = [t[:, :, :] for t in hn]
        hu = pair("hu", [P, KD, DM])
        hT_hi = pair("hT_hi", [P, KD, L], F32R)
        hT_lo = pair("hT_lo", [P, KD, L], F32R)
        xc = pair("xc", [P, MC, L])
        sz = pair("sz", [P, KD, DI])
        xs = pair("xs", [P, KD, DI])
        xdt = pair("xdt", [P, KD, DI])
        seg_hi, seg = shared(("seg_hi", [P, KD, NH, P], F32R), ("seg", [P, KD, NH, P]))
        seg_lo, y, yT = shared(("seg_lo", [P, KD, NH, P], F32R), ("y", [P, KD, DI]), ("yT", [P, KD, KI, P]))
        gm = pair("gm", [P, KD, P])
        bs = pair("bs", [P, NS])
        xdec = pair("xdec", [P, DI])
        st = pair("st", [P, DI])
        h2 = pair("h2", [P, KD, DM])
        hb = pair("hb", [P, KD, DM])
        rows = pair("rows", [P, KD, ROW])
        v2T = pair("v2T", [P, KD, L])
        nmax = pair("nmax", [P, KD]); rsum = pair("rsum", [P, KD]); rinv = pair("rinv", [P, KD])
        stats = pair("stats", [P, KD, 6]); mv = pair("mv", [P, KD, 2])
        lnv = pair("lnv", [P, 2, KD]); lnr = pair("lnr", [P, 2, KD])
        hu_s = pair("hu_s", [P, KD]); hu_b = pair("hu_b", [P, KD])
        dty = pair("dty", [P, KD, NH]); dtn = pair("dtn", [P, KD, NH]); dtw = pair("dtw", [P, KD, NH])
        dts = pair("dts", [P, KD, NH]); dtq = pair("dtq", [P, KD, NH]); dtp = pair("dtp", [P, KD, NH])
        dt_ = pair("dt_", [P, KD, NH]); a_ = pair("a_", [P, KD, NH])
        a_hi = pair("a_hi", [P, KD, NH], F32R); a_lo = pair("a_lo", [P, KD, NH], F32R)
        ea = pair("ea", [P, NH]); edec = pair("edec", [P, NH])
        ss = pair("ss", [P, KD]); msq = pair("msq", [P, KD]); rms = pair("rms", [P, KD])
        stats2 = pair("stats2", [P, KD, 6]); mv2 = pair("mv2", [P, KD, 2])
        lv2 = pair("lv2", [P, KD]); nm2 = pair("nm2", [P, KD]); lr2 = pair("lr2", [P, KD])
        lmax = pair("lmax", [P, KD]); lg = pair("lg", [P, KD, NE]); le = pair("le", [P, KD, NE])
        lsum = pair("lsum", [P, KD]); linv = pair("linv", [P, KD]); pr = pair("pr", [P, KD, NE])
        top = pair("top", [P, KD, 8]); topi = pair("topi", [P, KD, 8], U32); topf = pair("topf", [P, KD, 2])
        oh = pair("oh", [P, KD, 2, NE]); ohs = pair("ohs", [P, KD, NE], BF16); ohp = pair("ohp", [P, KD, 2, NE])
        offs = pair("offs", [P, 2 * KD]); valid = pair("valid", [P, 2 * KD])
        sl = pair("sl", [P, 2 * KD]); slot = pair("slot", [P, 2 * KD], I32)
        first.close()

        second = ExitStack()
        eb = lambda name, shape, dt=F32: sb(name, shape, dt, second)
        w_hi = [eb(f"w_hi{q}", [P, 2, KD * FF], F32R) for q in range(2)]
        w_lo = [eb(f"w_lo{q}", [P, 2, KD * FF], F32R) for q in range(2)]
        xe = [eb(f"xe{q}", [P, JS, ROW]) for q in range(2)]
        xe_hi = [eb(f"xe_hi{g}", [P, KD, GW], F32R) for g in range(2)]
        xe_lo = [eb(f"xe_lo{g}", [P, KD, GW], F32R) for g in range(2)]
        hf = [eb(f"hf{g}", [P, GW]) for g in range(2)]
        h_hi = eb("h_hi", [P, KF, GW], F32R)
        h_lo = eb("h_lo", [P, KF, GW], F32R)
        ye = [eb(f"ye{q}", [P, JS, DM]) for q in range(2)]
        e_now = eb("e_now", [P, 1])
        is_first = [eb(f"is_first{q}", [P, JS]) for q in range(2)]
        wd = [eb(f"wd{q}", [P, JS]) for q in range(2)]
        w_slot = [eb(f"w_slot{q}", [P, JS]) for q in range(2)]
        tok_slot = [eb(f"tok_slot{q}", [P, JS], I32) for q in range(2)]
        second.close()

        bank = [[ctx.enter_context(nc.psum_tensor(f"bank{p}{i}", [P, 512], F32)) for i in range(4)]
                for p in range(2)]

        s_early = sem("s_early")
        s_consts = sem("s_consts")
        w_in_split = sem("w_in_split")
        s_tok = sem("s_tok")
        hold.counts = {nc.vector.engine: sem("dve_held"), nc.gpsimd.engine: sem("pool_held")}
        s_clamped = sem("s_clamped")
        s_masks = sem("s_masks")
        s_mask0 = sem("s_mask0")
        s_prep = sem("s_prep")
        s_nega = sem("s_nega")
        s_wqk = sem("s_wqk")
        s_template = sem("s_template")
        s_fill = sem("s_fill")
        s_dump = sem("s_dump")
        idx_ready = signal("idx_ready", 1, 2)
        gathered = dma_signal("gathered", 16 * KD, 16 * KD)
        rows_scaled = signal("rows_scaled", 1, 2); x_ready = signal("x_ready", 1, 2)
        xT_psum = signal("xT_psum"); xT_ready = signal("xT_ready")
        tT_psum = signal("tT_psum"); v_psum = signal("v_psum"); tT_ready = signal("tT_ready")
        st_psum = signal("st_psum"); nmax_ready = signal("nmax_ready"); probs_ready = signal("probs_ready")
        v_ready = signal("v_ready"); o_psum = signal("o_psum")
        lnv_ready = signal("lnv_ready"); lnr_ready = signal("lnr_ready")
        hn_ready = signal("hn_ready"); hu_coef = signal("hu_coef"); hu_ready = signal("hu_ready")
        hnT_psum = signal("hnT_psum"); hT_ready = signal("hT_ready"); hT_split = signal("hT_split")
        dt_psum = signal("dt_psum"); xbc_psum = signal("xbc_psum", 3); tap_ready = signal("tap_ready", 3)
        conv_done = signal("conv_done", 3); th_ready = signal("th_ready", 3); xc_ready = signal("xc_ready", 3)
        dtn_ready = signal("dtn_ready"); dtw_ready = signal("dtw_ready"); a_ready = signal("a_ready")
        seg_in = signal("seg_in", 2)
        z_psum = signal("z_psum", 2); tz_ready = signal("tz_ready", 2); sz_ready = signal("sz_ready", 2)
        btg_psum = signal("btg_psum"); bs_ready = signal("bs_ready"); gm_ready = signal("gm_ready")
        xs_psum = signal("xs_psum", 2); xs_ready = signal("xs_ready", 2); xdt_ready = signal("xdt_ready", 2)
        seg_psum = signal("seg_psum", 4); decay_ready = signal("decay_ready", 4)
        edec_ready = signal("edec_ready"); xdec_ready = signal("xdec_ready")
        m_ready = [signal(f"m{c}_ready") for c in range(KD)]; skip_ready = signal("skip_ready", 2)
        state_psum = signal("state_psum"); st_ready = signal("st_ready")
        yd_psum = signal("yd_psum", 2); yo_psum = signal("yo_psum")
        y_ready = signal("y_ready", 2); ss_ready = signal("ss_ready", 1, 2)
        yT_psum = signal("yT_psum", 2); yT_ready = signal("yT_ready", 2)
        msq_ready = signal("msq_ready"); rms_ready = signal("rms_ready")
        out_psum = signal("out_psum"); h2_ready = signal("h2_ready", 1, 2)
        lv2_ready = signal("lv2_ready"); lr2_ready = signal("lr2_ready")
        nm2_ready = signal("nm2_ready"); v2_ready = signal("v2_ready"); hb_ready = signal("hb_ready")
        hb_stored = dma_signal("hb_stored", 16, 16)
        v2T_psum = signal("v2T_psum"); v2T_ready = signal("v2T_ready")
        logit_psum = signal("logit_psum"); lg_ready = signal("lg_ready"); le_ready = signal("le_ready")
        ohs_ready = signal("ohs_ready"); pos_psum = signal("pos_psum"); pos_taken = signal("pos_taken", 1, 2); slot_ready = signal("slot_ready", 1, 2)
        scattered = dma_signal("scattered", 64)
        rows_free = signal("rows_free", 1, 2)
        front_chain = sem("front_chain"); back_chain = sem("back_chain"); routing_chain = sem("routing_chain"); residual_chain = sem("residual_chain")
        moe_chain_sem = sem("dve_moe_chain")
        part_done = sem("part_done")
        w_loaded = sem("w_loaded")
        w_high = sem("w_high")
        w1_split = sem("w1_split")
        w2_split = sem("w2_split")
        xe_loaded = [dma_signal(f"xe{half_}_loaded", 16) for half_ in range(NG)]
        slot_info = sem("slot_info")
        xeT_psum = sem("xeT_psum")
        x_half = sem("x_half")
        xe_split = sem("xe_split")
        h_psum = sem("h_psum")
        hf_ready = sem("hf_ready")
        hhi_ready = sem("hhi_ready")
        hlo_ready = sem("hlo_ready")
        y_psum = sem("y_psum")
        ye_ready = sem("ye_ready")
        added = sem("added")
        expert_added = sem("expert_added")
        H_BANKS, Y0, CHUNKS = 4, 4 * NG, KF
        CHUNK = 2 * KD * FF // CHUNKS

        def run_experts(loop, turn):
            with loop(1, NE // 2) as r:
                turn(r, False)
            turn(NE // 2, True)

        def bc(ap, shape):
            return ap.to_broadcast(shape)

        GROUPS = (2, 0, 1)
        XBC_BANK, Z_BANK, SEG_BANK = (2, 3, 0), (2, 0), (1, 3, 0, 2)
        XS_BANK, YD_BANK, YT_BANK = (2, 1), (1, 0), (3, 1)
        PER_TURN = 2 * NG * KF
        h_bank = bank[0]
        x_bank = bank[1][0:2]
        y_bank = bank[1][2:4]

        block = ctx.enter_context(nc.Block())

        @block.sync
        def _(sp):
            sp.dma_start(tok_all[:, 0:N_TILES], tokens).then_inc(s_tok, 16)
            early = [
                (wqk_in[:, 0, :, :], w_qT.rearrange("(k p) n -> p k n", p=P)),
                (wqk_in[:, 1, :, :], w_kT.rearrange("(k p) n -> p k n", p=P)),
                (pos[:, :, :], pos_enc.rearrange("(k p) n -> p k n", p=P)),
                (wv[:, :, :], w_v.rearrange("(k p) n -> p k n", p=P)),
            ]
            loads = [
                (w_in[:, :, :], in_wT.rearrange("(k p) n -> p k n", p=P)),
                (w_out[:, :, :], out_wT.rearrange("(k p) n -> p k n", p=P)),
                (lnw[:, :], ln_w), (lnb[:, :], ln_b), (cw[:, :, :], conv_w), (cb[:, :], conv_b),
                (nw[:, :], norm_w), (wr[:, :, :], w_router),
                (dtb[:, :], bc(dt_bias, [P, NH])), (alog[:, :], bc(A_log, [P, NH])),
                (dskip[:, :], bc(D_skip, [P, NH])), (bias_b[:, :], bc(bias, [P, DM])),
            ]
            assert (len(early), len(loads)) == (N_EARLY, N_LOADS)
            for dst, src in early:
                sp.dma_start(dst, src).then_inc(s_early, 16)
            for dst, src in loads:
                sp.dma_start(dst, src).then_inc(s_consts, 16)
            sp.wait_ge(s_template, 1)
            sp.dma_start(slots_dram.rearrange("(n p) c -> p n c", p=P),
                         zero_row[:, :].unsqueeze(1).to_broadcast([P, NSLOT // P, ROW])).then_inc(s_fill, 16)
            sp.dma_start(out[T:T + P, :], zero_row[:, 0:DM]).then_inc(s_dump, 16)
            sp.wait_ge(w_in_split, 2)
            sp.wait_ge(s_wqk, 1)
            sp.dma_start(w_raw[:, 0, :].rearrange("p (k f) -> p k f", k=KD),
                         w1[0:DM, :].rearrange("(k p) f -> p k f", p=P)).then_inc(w_loaded, 16)
            sp.dma_start(w_raw[:, 1, :].rearrange("p (k f) -> p k f", k=KF),
                         w2[0:FF, :].rearrange("(k p) f -> p k f", p=P)).then_inc(w_loaded, 16)
            with sp.Fori(1, PAIRS + 1) as reg:
                r = Turn(reg)
                for p in range(2):
                    sp.wait_ge(hb_ready[p], hb_ready.now(r, p))
                    sp.dma_start(out[bass.ds(r.value(2 * L, p * L - 2 * L), L), :]
                                 .rearrange("(k p) n -> p k n", p=P), hb[p][:, :, :]).then_inc(hb_stored[p], 16)
            for p in range(2):
                sp.wait_ge(scattered[p], 64 * PAIRS)
                sp.wait_ge(hb_stored[p], 16 * (PAIRS + 1))
            sp.wait_ge(s_dump, 16)

            sp.wait_ge(part_done, 4)

            def load_weights(e):
                sp.wait_ge(w1_split, e)
                sp.wait_ge(w2_split, e)
                sp.dma_start(w_raw[:, 0, :].rearrange("p (k f) -> p k f", k=KD),
                             w1[bass.ds(e * DM, DM), :].rearrange("(k p) f -> p k f", p=P)).then_inc(w_loaded, 16)
                sp.dma_start(w_raw[:, 1, :].rearrange("p (k f) -> p k f", k=KF),
                             w2[bass.ds(e * FF, FF), :].rearrange("(k p) f -> p k f", p=P)).then_inc(w_loaded, 16)

            def load_slots(e, q):
                for half_ in range(NG):
                    sp.dma_start(xe[q][:, half_ * 4:half_ * 4 + 4, :],
                                 slots_dram[bass.ds(e * CAP + half_ * GW, GW), :]
                                 .rearrange("(j p) c -> p j c", p=P)).then_inc(xe_loaded[half_][q], 16)

            for q in range(2):
                load_slots(q, q)
            with sp.Fori(1, NE // 2) as r:
                for q in range(2):
                    e = r * 2 + (q - 1)
                    load_weights(e)
                    sp.wait_ge(xeT_psum, e * NG)
                    sp.wait_ge(slot_info, e)
                    load_slots(e + 1, q)
            load_weights(NE - 1)
            sp.wait_ge(added, 16 * NE * JS)
            sp.wait_ge(expert_added, 2 + NE)

        @block.gpsimd
        def _(pool):
            g = nc.gpsimd
            g.memset(zero_row[:, :], 0.0)
            for m, val in ((ident, 0.0), (tri, 1.0), (below, 1.0), (before_b, 1.0), (ones_b, 1.0)):
                g.memset(m[:, :], val)
            g.memset(neg_half[:, :], -0.5)
            g.memset(oh_sum[:, :], 0.0)
            g.memset(tok_all[:, N_TILES:], 0).then_inc(s_mask0, 1)
            pool.wait_ge(s_mask0, 1)
            g.affine_select(out=ident[:, :], in_=ident[:, :], compare_op=ALU.not_equal, fill=1.0, base=0,
                            pattern=[[-1, P]], channel_multiplier=1)
            g.affine_select(out=tri[:, :], in_=tri[:, :], compare_op=ALU.is_ge, fill=0.0, base=0,
                            pattern=[[1, P]], channel_multiplier=-1)
            g.affine_select(out=below[:, :], in_=below[:, :], compare_op=ALU.is_gt, fill=0.0, base=0,
                            pattern=[[-1, P]], channel_multiplier=1)
            g.affine_select(out=before_b[:, :], in_=before_b[:, :], compare_op=ALU.is_gt, fill=0.0, base=0,
                            pattern=[[1, P]], channel_multiplier=-1)
            g.iota(e_iota[:, :], pattern=[[1, NE]], base=0, channel_multiplier=0,
                   allow_small_or_imprecise_dtypes=True)
            g.iota(tok_iota[:, :], pattern=[[P, KD]], base=0, channel_multiplier=1).then_inc(s_masks, 1)
            g.iota(zero_row[:, C_TOK:C_TOK + 1].bitcast(I32), pattern=[[0, 1]], base=T,
                   channel_multiplier=1).then_inc(s_template, 1)

            def take_tokens(p, col):
                g.tensor_copy(idx[p][:, :], tok_all[:, bass.ds(col, KD)]).then_inc(idx_ready[p], 1)

            def gather(p):
                for c in range(KD):
                    g.indirect_dma_start(xg[p][:, c, :], None, emb,
                                         bass.IndirectOffsetOnAxis(ap=idx[p][:, c:c + 1], axis=0))\
                        .then_inc(gathered[p], 16)

            pool.wait_ge(s_clamped, 1)
            for p in range(2):
                take_tokens(p, KD * p)
            for p in range(2):
                pool.wait_ge(idx_ready[p], p + 1)
                gather(p)
            for p in range(2):
                pool.sem_inc(hb_stored[p], hb_stored.credit)
            pool.sem_inc(rows_free.sem, rows_free.credit)
            pool.wait_ge(s_early, 16 * N_EARLY)
            pool.wait_ge(rows_scaled[0], 1)
            g.tensor_tensor(x[0][:, :, :], xg[0][:, :, :], pos[:, :, :], ALU.add).then_inc(x_ready[0], 1)
            pool.wait_ge(s_masks, 1)
            pool.wait_ge(s_consts, 16 * N_LOADS)
            def gather_next(r, p):
                hold(pool, x_ready[p], x_ready.before(r, p))
                hold(pool, gathered[p], gathered.before(r, p))
                take_tokens(p, r.value(2 * KD, KD * p))
                hold(pool, idx_ready[p], idx_ready.now(r, p))
                gather(p)

            def embed(q):
                g.tensor_tensor(x[q][:, :, :], xg[q][:, :, :], pos[:, :, :], ALU.add).then_inc(x_ready[q], 1)

            def embed_next(r, p):
                q = 1 - p
                pool.wait_ge(rows_scaled[q], rows_scaled.before(r, q) if q == 1 else rows_scaled.now(r, q))
                embed(q)

            def norm_roots(r, p):
                pool.wait_ge(lnv_ready[p], lnv_ready.now(r, p))
                g.tensor_tensor(lnr[p][:, :, :].rearrange("p a c -> p (a c)"),
                                lnv[p][:, :, :].rearrange("p a c -> p (a c)"),
                                neg_half[:, :], ALU.pow).then_inc(lnr_ready[p], 1)

            def segment_inputs(r, p, c):
                pool.wait_ge(a_ready[p], a_ready.now(r, p))
                for part, a_part in ((seg_hi, a_hi), (seg_lo, a_lo)):
                    ins = g.tensor_tensor(part[p][:, c, :, :], bc(tri[:, :].unsqueeze(1), [P, NH, P]),
                                          bc(a_part[p][:, c, :].unsqueeze(2).bitcast(F32), [P, NH, P]), ALU.mult)
                ins.then_inc(seg_in[p], 1)

            def decayed_x(r, p):
                pool.wait_ge(edec_ready[p], edec_ready.now(r, p))
                pool.wait_ge(xdt_ready[p], xdt_ready.now(r, p, 1))
                g.tensor_tensor(xdec[p][:, :].rearrange("p (h d) -> p h d", h=NH),
                                xdt[p][:, 0, :].rearrange("p (h d) -> p h d", h=NH),
                                bc(edec[p][:, :].unsqueeze(2), [P, NH, HD]), ALU.mult).then_inc(xdec_ready[p], 1)

            def skip_x(r, p, c):
                pool.wait_ge(xs_ready[p], xs_ready.now(r, p, c + 1))
                g.tensor_tensor(xs[p][:, c, :].rearrange("p (h d) -> p h d", h=NH),
                                xs[p][:, c, :].rearrange("p (h d) -> p h d", h=NH),
                                bc(dskip[:, :].unsqueeze(2), [P, NH, HD]), ALU.mult).then_inc(skip_ready[p], 1)

            def decay_scores(r, p):
                pool.wait_ge(decay_ready[p], decay_ready.now(r, p))
                pool.wait_ge(gm_ready[p], gm_ready.now(r, p))
                g.tensor_tensor(seg[p][:, 1, :, :], seg[p][:, 1, :, :], bc(gm[p][:, 1, :].unsqueeze(1), [P, NH, P]),
                                ALU.mult).then_inc(m_ready[1][p], 1)

            def gated_root(r, p):
                pool.wait_ge(msq_ready[p], msq_ready.now(r, p))
                g.tensor_tensor(rms[p][:, :], msq[p][:, :], neg_half[:, 0:KD], ALU.pow).then_inc(rms_ready[p], 1)

            def second_root(r, p):
                pool.wait_ge(lv2_ready[p], lv2_ready.now(r, p))
                g.tensor_tensor(lr2[p][:, :], lv2[p][:, :], neg_half[:, 0:KD], ALU.pow).then_inc(lr2_ready[p], 1)

            def with_bias(r, p):
                pool.wait_ge(hb_stored[p], hb_stored.before(r, p))
                pool.wait_ge(h2_ready[p], h2_ready.now(r, p))
                g.tensor_tensor(hb[p][:, :, :], h2[p][:, :, :], bc(bias_b[:, :].unsqueeze(1), [P, KD, DM]),
                                ALU.add).then_inc(hb_ready[p], 1)

            def scatter_rows(t, p):
                pool.wait_ge(s_fill, 16)
                hold(pool, slot_ready[p], slot_ready.now(t, p))
                for c in range(KD):
                    for k in range(2):
                        g.indirect_dma_start(
                            slots_dram, bass.IndirectOffsetOnAxis(ap=slot[p][:, 2 * c + k:2 * c + k + 1], axis=0),
                            rows[p][:, c, :], None, bounds_check=NSLOT - 1, oob_is_err=False)\
                            .then_inc(scattered[p], 16)

            def free_rows(t, p):
                pool.wait_ge(scattered[p], scattered.now(t, p))
                pool.sem_inc(rows_free[p], 1)

            def half(p, f, b, t):
                q = 1 - p
                if f:
                    norm_roots(f, p)
                if b:
                    decayed_x(b, q)
                    decay_scores(b, q)
                    skip_x(b, q, 0)
                    skip_x(b, q, 1)
                if f:
                    gather_next(f, p)
                if t:
                    with_bias(t, p)
                if f:
                    embed_next(f, p)
                if t:
                    scatter_rows(t, p)
                if b:
                    gated_root(b, q)
                if t:
                    free_rows(t, p)
                if f:
                    segment_inputs(f, p, 0)
                if b:
                    second_root(b, q)
                if f:
                    segment_inputs(f, p, 1)

            run_batches(g.Fori, half, PAIRS)
            for p in range(2):
                pool.wait_ge(gathered[p], gathered.credit * (PAIRS + 1))

            pool.drain().then_inc(part_done, 1)

            pool.wait_ge(part_done, 4)
            pool.sem_inc(expert_added, 2)

            def low_weights(n, q, w, done):
                pool.wait_ge(w_high, n * CHUNKS + (w - 1) * (CHUNKS // 2))
                g.tensor_tensor(w_lo[q][:, w, :], w_raw[:, w, :], w_hi[q][:, w, :].bitcast(F32), ALU.subtract)\
                    .then_inc(done, 1)

            def add_results(n, q):
                for j in range(JS):
                    if j % 2 == 0:
                        hold(pool, ye_ready, n * (JS // 2) + (2 + j // 2 + 1 - JS // 2))
                    g.indirect_dma_start(out, bass.IndirectOffsetOnAxis(ap=tok_slot[q][:, j:j + 1], axis=0),
                                         ye[q][:, j, :], None, compute_op=ALU.add).then_inc(added, 16)
                    hold(pool, added, n * (16 * JS) + (16 * j + 16 - 16 * JS))
                pool.sem_inc(expert_added, 1)

            def experts(r, last):
                for q in range(2):
                    if not (last and q):
                        low_weights(r * 2 + q, 1 - q, 0, w1_split)
                        low_weights(r * 2 + q, 1 - q, 1, w2_split)
                    add_results(r * 2 + (q - 1), q)

            low_weights(1, 0, 1, w2_split)
            run_experts(g.Fori, experts)

        @block.scalar
        def _(act):
            sc = nc.scalar
            act.wait_ge(s_wqk, 1)
            sc.activation(wqk[:, :, :].rearrange("p k n -> p (k n)"), bank[0][0][:, :], ACT.Copy,
                          scale=float(DM) ** -0.5).then_inc(s_wqk, 1)
            act.wait_ge(s_consts, 16 * N_LOADS)
            sc.activation(neg_a[:, :], alog[:, :], ACT.Exp).then_inc(s_nega, 1)

            def copy(dst, src, signal_, func=ACT.Copy, **kw):
                sc.activation(dst, src, func, **kw).then_inc(signal_, 1)

            def flat(t):
                return t.rearrange("p a b -> p (a b)")

            act.sem_inc(ss_ready.sem, ss_ready.credit)
            act.wait_ge(gathered[0], gathered.credit)
            copy(flat(xg[0][:, :, :]), flat(xg[0][:, :, :]), rows_scaled[0], scale=float(DM) ** 0.5)

            def transposed_x(r, p):
                act.wait_ge(ss_ready[p], ss_ready.before(r, p))
                act.wait_ge(xT_psum[p], xT_psum.now(r, p))
                copy(flat(xT[p][:, :, :]), bank[p][3][:, :], xT_ready[p])

            def query_side(r, p):
                act.wait_ge(tT_psum[p], tT_psum.now(r, p))
                copy(flat(tT[p][:, :, :]), bank[p][1][:, :], tT_ready[p])

            def score_exps(r, p):
                act.wait_ge(nmax_ready[p], nmax_ready.now(r, p))
                for c in range(KD):
                    ins = sc.activation(probs[p][:, c, :], bank[p][3][:, c * L:(c + 1) * L], ACT.Exp,
                                        bias=nmax[p][:, c:c + 1], accum_out=rsum[p][:, c:c + 1])
                ins.then_inc(probs_ready[p], 1)

            def scale_rows(r, p):
                q = 1 - p
                act.wait_ge(gathered[q], gathered.before(r, q) if q == 1 else gathered.now(r, q))
                copy(flat(xg[q][:, :, :]), flat(xg[q][:, :, :]), rows_scaled[q], scale=float(DM) ** 0.5)

            def norm_2(t, p):
                act.wait_ge(nm2_ready[p], nm2_ready.now(t, p))
                act.wait_ge(rows_free[p], rows_free.before(t, p))
                for c in range(KD):
                    ins = sc.activation(rows[p][:, c, 0:DM], h2[p][:, c, :], ACT.Identity,
                                        scale=lr2[p][:, c:c + 1], bias=nm2[p][:, c:c + 1])
                ins.then_inc(v2_ready[p], 1)

            def residuals(r, p):
                act.wait_ge(hu_coef[p], hu_coef.now(r, p))
                act.wait_ge(hn_ready[p], hn_ready.now(r, p))
                for c in range(KD):
                    ins = sc.activation(hu[p][:, c, :], bank[p][0][:, c * DM:(c + 1) * DM], ACT.Identity,
                                        scale=hu_s[p][:, c:c + 1], bias=hu_b[p][:, c:c + 1])
                ins.then_inc(hu_ready[p], 1)

            def mixer_input(r, p):
                act.wait_ge(hnT_psum[p], hnT_psum.now(r, p))
                for dst in (hT_hi, hT):
                    for k in range(KD):
                        ins = sc.activation(dst[p][:, k, :], bank[p][1][:, k * L:(k + 1) * L], ACT.Identity,
                                            scale=lnw[:, k:k + 1], bias=lnb[:, k:k + 1])
                ins.then_inc(hT_ready[p], 1)

            def dt_exp(r, p):
                act.wait_ge(dtn_ready[p], dtn_ready.now(r, p))
                copy(flat(dtw[p][:, :, :]), flat(dtn[p][:, :, :]), dtw_ready[p], ACT.Exp)

            def last_tap(r, p, i):
                j = GROUPS[i]
                act.wait_ge(xbc_psum[p], xbc_psum.now(r, p, i + 1))
                for h in range(2):
                    m = 2 * j + h
                    ins = sc.activation(xc[p][:, m, :], bank[p][XBC_BANK[i]][:, h * L:(h + 1) * L], ACT.Identity,
                                        scale=cw[:, m, TAPS - 1:TAPS], bias=cb[:, m:m + 1])
                ins.then_inc(tap_ready[p], 1)

            def tanh_conv(r, p, i):
                j = GROUPS[i]
                act.wait_ge(conv_done[p], conv_done.now(r, p, i + 1))
                copy(th[p][:, j, :], flat(xc[p][:, 2 * j:2 * j + 2, :]), th_ready[p], ACT.Tanh)

            def tanh_z(r, p, c):
                act.wait_ge(z_psum[p], z_psum.now(r, p, c + 1))
                copy(sz[p][:, c, :], bank[p][Z_BANK[c]][:, :], tz_ready[p], ACT.Tanh)

            def state_inputs(r, p):
                act.wait_ge(btg_psum[p], btg_psum.now(r, p))
                sc.activation(bs[p][:, :], bank[p][3][:, 0:NS], ACT.Copy)
                copy(ea[p][:, :], bank[p][3][:, 3 * P:3 * P + NH], bs_ready[p], ACT.Exp)

            def decay(r, p, i):
                act.wait_ge(seg_psum[p], seg_psum.now(r, p, i + 1))
                c, half_ = i // 2, i % 2
                copy(seg[p][:, c, 4 * half_:4 * half_ + 4, :].rearrange("p h l -> p (h l)"),
                     bank[p][SEG_BANK[i]][:, :], decay_ready[p], ACT.Exp)

            def end_decay(r, p):
                act.wait_ge(decay_ready[p], decay_ready.now(r, p, 2))
                copy(edec[p][:, :], seg[p][:, 0, :, P - 1], edec_ready[p])

            def x_rows(r, p, c):
                act.wait_ge(xs_psum[p], xs_psum.now(r, p, c + 1))
                copy(xs[p][:, c, :], bank[p][XS_BANK[c]][:, :], xs_ready[p])

            def state(r, p):
                act.wait_ge(state_psum[p], state_psum.now(r, p))
                copy(st[p][:, :], bank[p][3][:, :], st_ready[p])

            def squares(r, p):
                act.wait_ge(y_ready[p], y_ready.now(r, p))
                for c in range(KD):
                    ins = sc.activation(th[p][:, c, :], y[p][:, c, :], ACT.Square, accum_out=ss[p][:, c:c + 1])
                ins.then_inc(ss_ready[p], 1)

            def transposed_y(r, p, c):
                act.wait_ge(yT_psum[p], yT_psum.now(r, p, c + 1))
                copy(flat(yT[p][:, c, :, :]), bank[p][YT_BANK[c]][:, :], yT_ready[p])

            def transposed_rows(t, p):
                act.wait_ge(v2T_psum[p], v2T_psum.now(t, p))
                copy(flat(v2T[p][:, :, :]), bank[p][2][:, :], v2T_ready[p])

            def router_exp(t, p):
                act.wait_ge(lg_ready[p], lg_ready.now(t, p))
                copy(flat(le[p][:, :, :]), flat(lg[p][:, :, :]), le_ready[p], ACT.Exp)

            def half(p, f, b, t):
                q = 1 - p
                if f:
                    transposed_x(f, p)
                if b:
                    tanh_conv(b, q, 0)
                    tanh_conv(b, q, 1)
                if f:
                    scale_rows(f, p)
                    query_side(f, p)
                if b:
                    tanh_z(b, q, 0)
                    tanh_conv(b, q, 2)
                if f:
                    score_exps(f, p)
                if b:
                    tanh_z(b, q, 1)
                if t:
                    norm_2(t, p)
                if b:
                    state_inputs(b, q)
                    decay(b, q, 0)
                    x_rows(b, q, 0)
                    decay(b, q, 1)
                    end_decay(b, q)
                if t:
                    transposed_rows(t, p)
                if b:
                    decay(b, q, 2)
                    decay(b, q, 3)
                    x_rows(b, q, 1)
                if t:
                    router_exp(t, p)
                if b:
                    state(b, q)
                if f:
                    mixer_input(f, p)
                    dt_exp(f, p)
                    residuals(f, p)
                    last_tap(f, p, 0)
                if b:
                    transposed_y(b, q, 0)
                    transposed_y(b, q, 1)
                if f:
                    last_tap(f, p, 1)
                if b:
                    squares(b, q)
                if f:
                    last_tap(f, p, 2)

            run_batches(sc.Fori, half, PAIRS)
            act.drain().then_inc(part_done, 1)

            act.wait_ge(part_done, 4)
            act.sem_inc(hhi_ready, H_BANKS)

            def high_weights(n, q, m):
                if m == 0:
                    act.wait_ge(w_loaded, n * 32)
                    act.wait_ge(y_psum, n * (2 * NG))
                sc.activation(w_hi[q].rearrange("p w n -> p (w n)")[:, m * CHUNK:(m + 1) * CHUNK],
                              w_raw.rearrange("p w n -> p (w n)")[:, m * CHUNK:(m + 1) * CHUNK], ACT.Copy)\
                    .then_inc(w_high, 1)

            def experts(r, last):
                for g in range(2 * NG):
                    for m in range(KF):
                        i = KF * g + m
                        act.wait_ge(h_psum, r * PER_TURN + (i + 1 - PER_TURN))
                        act.wait_ge(hlo_ready, r * PER_TURN + (i + 1 - PER_TURN))
                        sc.activation(hf[m % 2][:, :], h_bank[i % H_BANKS][:, :], ACT.Gelu_apprx_tanh)\
                            .then_inc(hf_ready, 1)
                        sc.activation(h_hi[:, m, :], h_bank[i % H_BANKS][:, :], ACT.Gelu_apprx_tanh)\
                            .then_inc(hhi_ready, 1)
                        if g % NG == NG - 1 and not (last and g // NG):
                            high_weights(r * 2 + g // NG, 1 - g // NG, m)

            for m in range(CHUNKS):
                high_weights(1, 0, m)
            run_experts(sc.Fori, experts)

        @block.vector
        def _(dve):
            vc = nc.vector

            def flat(t):
                return t.rearrange("p a b -> p (a b)")

            def heads(t):
                return t.rearrange("p (h d) -> p h d", h=NH)

            prep = Chain(dve, s_prep, 0)
            dve.wait_ge(s_tok, 16)
            prep.mark(vc.tensor_scalar(tok_neg[:, :], tok_all[:, 0:N_TILES], 0.0, float(VOCAB), ALU.is_lt, ALU.mult))
            prep.wait()
            prep.mark(vc.tensor_tensor(tok_neg[:, :], tok_neg[:, :], tok_all[:, 0:N_TILES], ALU.add))
            prep.wait()
            vc.tensor_scalar(tok_all[:, 0:N_TILES], tok_neg[:, :], 0.0, float(VOCAB - 1), ALU.max, ALU.min)\
                .then_inc(s_clamped, 1)
            for sig in (h2_ready, slot_ready, pos_taken):
                dve.sem_inc(sig.sem, sig.credit)
            dve.wait_ge(s_consts, 16 * N_LOADS)
            dve.wait_ge(s_masks, 1)
            vc.tensor_scalar(cw[:, :, :], cw[:, :, :], 0.5, None, ALU.mult)
            vc.tensor_scalar(cb[:, :], cb[:, :], 0.5, None, ALU.mult)
            vc.tensor_scalar(w_in[:, :, 0:DI], w_in[:, :, 0:DI], 0.5, None, ALU.mult)
            prep.mark(vc.tensor_copy(below_r[:, :], below[:, :]))
            prep.wait()
            vc.tensor_copy(w_dt[:, :, :], w_in[:, :, DI + CC:])
            vc.tensor_copy(w_in_hi[:, :, :], w_in).then_inc(w_in_split, 1)
            dve.wait_ge(w_in_split, 1)
            for k in range(KI):
                vc.tensor_scalar(w_out[:, k, :], w_out[:, k, :], nw[:, k:k + 1], None, ALU.mult)
            vc.tensor_tensor(w_in_lo[:, :, :], w_in, w_in_hi[:, :, :].bitcast(F32), ALU.subtract)\
                .then_inc(w_in_split, 1)
            dve.wait_ge(s_nega, 1)
            prep.mark(vc.tensor_scalar(neg_a[:, :], neg_a[:, :], -1.0, None, ALU.mult))
            prep.wait()

            def half(p, f, b, t):
                front = Chain(dve, front_chain, FRONT_LINKS, f, p)
                back = Chain(dve, back_chain, BACK_LINKS, b, 1 - p)
                routing = Chain(dve, routing_chain, ROUTING_LINKS, t, p)

                def norm_stats(ch, p, src, st6, mean_var):
                    for c in range(KD):
                        last = ch.mark(vc.bn_stats(st6[:, c, :], src[:, c, :]))
                    hold(dve, ch.sem, ch.value(last))
                    for c in range(KD):
                        last = ch.mark(vc.bn_aggr(mean_var[:, c, :], st6[:, c, :]))
                    ch.wait()

                def query_max(r, p):
                    dve.wait_ge(st_psum[p], st_psum.now(r, p))
                    vc.tensor_reduce(nmax[p][:, :], bank[p][3][:, :].rearrange("p (c q) -> p c q", c=KD), AX.X,
                                     ALU.max, negate=True).then_inc(nmax_ready[p], 1)

                def scale_v(r, p):
                    dve.wait_ge(probs_ready[p], probs_ready.now(r, p))
                    front.mark(vc.reciprocal(rinv[p][:, :], rsum[p][:, :]))
                    front.wait()
                    dve.wait_ge(v_psum[p], v_psum.now(r, p))
                    vc.tensor_tensor(v[p][:, :, :], bank[p][2][:, :].rearrange("p (c d) -> p c d", c=KD),
                                     bc(rinv[p][:, :].unsqueeze(2), [P, KD, DM]), ALU.mult).then_inc(v_ready[p], 1)

                def norm_1(r, p):
                    dve.wait_ge(o_psum[p], o_psum.now(r, p))
                    norm_stats(front, p, bank[p][0][:, :].rearrange("p (c d) -> p c d", c=KD), stats[p], mv[p])
                    vc.tensor_scalar(lnv[p][:, 0, :], mv[p][:, :, 1], EPS, None, ALU.add)
                    vc.tensor_scalar(lnv[p][:, 1, :], mv[p][:, :, 1], 1.0 + EPS, EPS * EPS, ALU.mult, ALU.add)\
                        .then_inc(lnv_ready[p], 1)

                def apply_norm_1(r, p):
                    dve.wait_ge(lnr_ready[p], lnr_ready.now(r, p))
                    for c in range(KD):
                        ins = vc.tensor_scalar(hn[p][:, c, :], bank[p][0][:, c * DM:(c + 1) * DM],
                                               mv[p][:, c, 0:1], lnr[p][:, 1, c:c + 1], ALU.subtract, ALU.mult)
                    ins.then_inc(hn_ready[p], 1)
                    vc.tensor_scalar(hu_s[p][:, :], lnr[p][:, 0, :], 1.0, None, ALU.add)
                    vc.scalar_tensor_tensor(out=hu_b[p][:, :], in0=mv[p][:, :, 0], scalar=-1.0, in1=lnr[p][:, 0, :],
                                            op0=ALU.mult, op1=ALU.mult).then_inc(hu_coef[p], 1)

                def split_hT(r, p):
                    dve.wait_ge(hT_ready[p], hT_ready.now(r, p))
                    vc.tensor_tensor(hT_lo[p][:, :, :], hT[p][:, :, :], hT_hi[p][:, :, :].bitcast(F32), ALU.subtract)\
                        .then_inc(hT_split[p], 1)

                def dt_in(r, p):
                    dve.wait_ge(dt_psum[p], dt_psum.now(r, p))
                    front.mark(vc.tensor_tensor(dty[p][:, :, :], bank[p][1][:, 0:KD * NH].rearrange("p (c h) -> p c h", c=KD),
                                             bc(dtb[:, :].unsqueeze(1), [P, KD, NH]), ALU.add))
                    front.wait()
                    vc.scalar_tensor_tensor(out=dtn[p][:, :, :], in0=dty[p][:, :, :], scalar=-1.0, in1=dty[p][:, :, :],
                                            op0=ALU.mult, op1=ALU.min).then_inc(dtn_ready[p], 1)

                def softplus(r, p, n):
                    w, q_, s_, poly = (flat(x_[p][:, :, :]) for x_ in (dtw, dtq, dts, dtp))
                    terms = len(LOG_TERMS)
                    if n == 0:
                        dve.wait_ge(dtw_ready[p], dtw_ready.now(r, p))
                        ins = vc.tensor_scalar(q_, w, 2.0, None, ALU.add)
                    elif n <= terms + 9:
                        front.wait(softplus.last)
                    if n == 1:
                        ins = vc.reciprocal(q_, q_)
                    elif n == 2:
                        ins = vc.tensor_tensor(s_, w, q_, ALU.mult)
                    elif n == 3:
                        ins = vc.tensor_tensor(q_, s_, s_, ALU.mult)
                    elif n == 4:
                        ins = vc.tensor_scalar(poly, q_, LOG_TERMS[0], None, ALU.mult)
                    elif 4 < n < 4 + terms:
                        ins = vc.scalar_tensor_tensor(out=poly, in0=poly, scalar=LOG_TERMS[n - 4], in1=q_,
                                                      op0=ALU.add, op1=ALU.mult)
                    elif n == terms + 4:
                        ins = vc.scalar_tensor_tensor(out=poly, in0=poly, scalar=1.0, in1=s_,
                                                      op0=ALU.add, op1=ALU.mult)
                    elif n == terms + 5:
                        ins = vc.tensor_scalar(poly, poly, 2.0, None, ALU.mult)
                    elif n == terms + 6:
                        ins = vc.scalar_tensor_tensor(out=flat(dt_[p][:, :, :]), in0=flat(dty[p][:, :, :]), scalar=0.0,
                                                      in1=poly, op0=ALU.max, op1=ALU.add)
                    elif n == terms + 7:
                        ins = vc.tensor_tensor(a_[p][:, :, :], dt_[p][:, :, :], bc(neg_a[:, :].unsqueeze(1), [P, KD, NH]),
                                               ALU.mult)
                    elif n == terms + 8:
                        ins = vc.tensor_copy(a_hi[p][:, :, :], a_[p][:, :, :])
                    elif n == terms + 9:
                        vc.tensor_tensor(a_lo[p][:, :, :], a_[p][:, :, :], a_hi[p][:, :, :].bitcast(F32), ALU.subtract)\
                            .then_inc(a_ready[p], 1)
                    if n < terms + 9:
                        softplus.last = front.mark(ins)

                def conv(r, p, i):
                    j = GROUPS[i]
                    dve.wait_ge(tap_ready[p], tap_ready.now(r, p, i + 1))
                    done = [None, None]
                    for back in range(1, TAPS):
                        for h in range(2):
                            m = 2 * j + h
                            if done[h]:
                                front.wait(done[h])
                            ins = vc.scalar_tensor_tensor(
                                out=xc[p][:, m, back:], in0=bank[p][XBC_BANK[i]][:, h * L:(h + 1) * L - back],
                                scalar=cw[:, m, TAPS - 1 - back:TAPS - back], in1=xc[p][:, m, back:],
                                op0=ALU.mult, op1=ALU.add)
                            if back < TAPS - 1:
                                done[h] = front.mark(ins)
                            elif h == 1:
                                ins.then_inc(conv_done[p], 1)
                            softplus(r, p, 5 + 2 * (TAPS - 1) * i + 2 * (back - 1) + h)

                def gate_conv(r, p, i):
                    j = GROUPS[i]
                    dve.wait_ge(th_ready[p], th_ready.now(r, p, i + 1))
                    both = flat(xc[p][:, 2 * j:2 * j + 2, :])
                    vc.scalar_tensor_tensor(out=both, in0=th[p][:, j, :], scalar=1.0, in1=both,
                                            op0=ALU.add, op1=ALU.mult).then_inc(xc_ready[p], 1)

                def gate_z(r, p, c):
                    dve.wait_ge(tz_ready[p], tz_ready.now(r, p, c + 1))
                    vc.scalar_tensor_tensor(out=sz[p][:, c, :], in0=sz[p][:, c, :], scalar=1.0,
                                            in1=bank[p][Z_BANK[c]][:, :], op0=ALU.add, op1=ALU.mult)\
                        .then_inc(sz_ready[p], 1)

                def mask_scores(r, p):
                    dve.wait_ge(bs_ready[p], bs_ready.now(r, p))
                    vc.tensor_tensor(gm[p][:, :, :], bank[p][3][:, P:3 * P].rearrange("p (c l) -> p c l", c=KD),
                                     bc(tri[:, :].unsqueeze(1), [P, KD, P]), ALU.mult).then_inc(gm_ready[p], 1)

                def times_dt(r, p, c):
                    dve.wait_ge(xs_ready[p], xs_ready.now(r, p, c + 1))
                    vc.tensor_tensor(heads(xdt[p][:, c, :]), heads(bank[p][XS_BANK[c]][:, :]),
                                     bc(dt_[p][:, c, :].unsqueeze(2), [P, NH, HD]), ALU.mult).then_inc(xdt_ready[p], 1)

                def decay_scores(r, p, c):
                    dve.wait_ge(decay_ready[p], decay_ready.now(r, p, 2 * c + 2))
                    dve.wait_ge(edec_ready[p], edec_ready.now(r, p))
                    dve.wait_ge(gm_ready[p], gm_ready.now(r, p))
                    vc.tensor_tensor(seg[p][:, c, :, :], seg[p][:, c, :, :], bc(gm[p][:, c, :].unsqueeze(1), [P, NH, P]),
                                     ALU.mult).then_inc(m_ready[0][p], 1)

                def gated_y(r, p, c):
                    if c == 0:
                        dve.wait_ge(yd_psum[p], yd_psum.now(r, p, 1))
                        dve.wait_ge(skip_ready[p], skip_ready.now(r, p, 1))
                        back.mark(vc.tensor_tensor(y[p][:, 0, :], bank[p][YD_BANK[0]][:, :], xs[p][:, 0, :], ALU.add))
                        back.wait()
                    else:
                        dve.wait_ge(yo_psum[p], yo_psum.now(r, p))
                        back.mark(vc.tensor_tensor(heads(y[p][:, 1, :]), heads(bank[p][2][:, :]),
                                                 bc(ea[p][:, :].unsqueeze(2), [P, NH, HD]), ALU.mult))
                        back.wait()
                        dve.wait_ge(skip_ready[p], skip_ready.now(r, p, 2))
                        back.mark(vc.tensor_tensor(y[p][:, 1, :], y[p][:, 1, :], xs[p][:, 1, :], ALU.add))
                        back.wait()
                        dve.wait_ge(yd_psum[p], yd_psum.now(r, p))
                        back.mark(vc.tensor_tensor(y[p][:, 1, :], bank[p][YD_BANK[1]][:, :], y[p][:, 1, :], ALU.add))
                        back.wait()
                    vc.tensor_tensor(y[p][:, c, :], y[p][:, c, :], sz[p][:, c, :], ALU.mult).then_inc(y_ready[p], 1)

                def mean_square(r, p):
                    dve.wait_ge(ss_ready[p], ss_ready.now(r, p))
                    vc.tensor_scalar(msq[p][:, :], ss[p][:, :], 1.0 / DI, EPS, ALU.mult, ALU.add)\
                        .then_inc(msq_ready[p], 1)

                def residual(r, p):
                    own = Chain(dve, residual_chain, RESIDUAL_LINKS, r, p)
                    dve.wait_ge(out_psum[p], out_psum.now(r, p))
                    dve.wait_ge(rms_ready[p], rms_ready.now(r, p))
                    dve.wait_ge(hu_ready[p], hu_ready.now(r, p))
                    for c in range(KD):
                        ins = vc.scalar_tensor_tensor(out=h2[p][:, c, :], in0=bank[p][0][:, c * DM:(c + 1) * DM],
                                                      scalar=rms[p][:, c:c + 1], in1=hu[p][:, c, :],
                                                      op0=ALU.mult, op1=ALU.add)
                    ins.then_inc(h2_ready[p], 1)
                    hold(dve, h2_ready[p], h2_ready.now(r, p))
                    norm_stats(own, p, h2[p], stats2[p], mv2[p])
                    vc.tensor_scalar(lv2[p][:, :], mv2[p][:, :, 1], EPS, None, ALU.add).then_inc(lv2_ready[p], 1)
                    own.close()

                def norm_2_bias(t, p):
                    dve.wait_ge(lr2_ready[p], lr2_ready.now(t, p))
                    vc.scalar_tensor_tensor(out=nm2[p][:, :], in0=mv2[p][:, :, 0], scalar=-1.0, in1=lr2[p][:, :],
                                            op0=ALU.mult, op1=ALU.mult).then_inc(nm2_ready[p], 1)

                def router_in(t, p):
                    dve.wait_ge(logit_psum[p], logit_psum.now(t, p))
                    logits = bank[p][3][:, 0:KD * NE].rearrange("p (c e) -> p c e", c=KD)
                    routing.mark(vc.tensor_reduce(lmax[p][:, :], logits, AX.X, ALU.max, negate=True))
                    routing.wait()
                    vc.tensor_tensor(lg[p][:, :, :], logits, bc(lmax[p][:, :].unsqueeze(2), [P, KD, NE]), ALU.add)\
                        .then_inc(lg_ready[p], 1)

                def router_top(t, p):
                    dve.wait_ge(le_ready[p], le_ready.now(t, p))
                    routing.mark(vc.tensor_reduce(lsum[p][:, :], le[p][:, :, :], AX.X, ALU.add))
                    routing.wait()
                    routing.mark(vc.reciprocal(linv[p][:, :], lsum[p][:, :]))
                    routing.wait()
                    last = routing.mark(vc.tensor_tensor(pr[p][:, :, :], le[p][:, :, :],
                                                    bc(linv[p][:, :].unsqueeze(2), [P, KD, NE]), ALU.mult))
                    hold(dve, routing.sem, routing.value(last))
                    for c in range(KD):
                        last = routing.mark(vc.max(top[p][:, c, :], pr[p][:, c, :]))
                    hold(dve, routing.sem, routing.value(last))
                    for c in range(KD):
                        routing.mark(vc.max_index(topi[p][:, c, :], top[p][:, c, :], pr[p][:, c, :]))
                    routing.wait()
                    routing.mark(vc.tensor_copy(topf[p][:, :, :], topi[p][:, :, 0:2]))
                    routing.wait()
                    routing.mark(vc.tensor_tensor(oh[p][:, :, :, :].rearrange("p c k e -> p (c k) e"),
                                             bc(e_iota[:, :].unsqueeze(1), [P, 2 * KD, NE]),
                                             bc(flat(topf[p][:, :, :]).unsqueeze(2), [P, 2 * KD, NE]), ALU.is_equal))
                    routing.wait()
                    vc.tensor_tensor(ohs[p][:, :, :], oh[p][:, :, 0, :], oh[p][:, :, 1, :], ALU.add)\
                        .then_inc(ohs_ready[p], 1)
                    vc.tensor_copy(rows[p][:, :, C_W0:C_W0 + 2], top[p][:, :, 0:2])
                    vc.tensor_copy(rows[p][:, :, C_E0], topf[p][:, :, 0])
                    routing.mark(vc.tensor_copy(rows[p][:, :, C_TOK].bitcast(I32), tok_iota[:, :]))

                def slots_of(t, p):
                    dve.wait_ge(pos_psum[p], pos_psum.now(t, p))
                    dve.wait_ge(slot_ready[p], slot_ready.before(t, p))
                    vc.tensor_tensor(ohp[p][:, :, :, :], oh[p][:, :, :, :],
                                     bc(bank[p][1][:, 0:KD * NE].rearrange("p (c e) -> p c e", c=KD).unsqueeze(2),
                                        [P, KD, 2, NE]), ALU.mult).then_inc(pos_taken[p], 1)
                    dve.wait_ge(pos_taken[p], pos_taken.now(t, p))
                    routing.mark(vc.tensor_reduce(offs[p][:, :], ohp[p][:, :, :, :].rearrange("p c k e -> p (c k) e"),
                                             AX.X, ALU.add))
                    routing.wait()
                    vc.scalar_tensor_tensor(out=sl[p][:, :], in0=flat(topf[p][:, :, :]), scalar=float(CAP),
                                            in1=offs[p][:, :], op0=ALU.mult, op1=ALU.add)
                    routing.mark(vc.tensor_scalar(valid[p][:, :], offs[p][:, :], float(CAP), None, ALU.is_lt))
                    routing.wait()
                    routing.mark(vc.scalar_tensor_tensor(out=sl[p][:, :], in0=sl[p][:, :], scalar=-float(NSLOT),
                                                    in1=valid[p][:, :], op0=ALU.add, op1=ALU.mult))
                    routing.wait()
                    vc.tensor_scalar(slot[p][:, :], sl[p][:, :], float(NSLOT), None, ALU.add).then_inc(slot_ready[p], 1)

                def count_choices(p):
                    for c in range(KD):
                        routing.mark(vc.tensor_tensor(oh_sum[:, :], oh_sum[:, :], ohs[p][:, c, :], ALU.add))
                        routing.wait()
                    routing.mark(vc.tensor_scalar(tok_iota[:, :], tok_iota[:, :], float(L), None, ALU.add))
                    routing.wait()

                q = 1 - p
                if f:
                    query_max(f, p)
                if b:
                    gate_conv(b, q, 0)
                if t:
                    norm_2_bias(t, p)
                if b:
                    gate_conv(b, q, 1)
                if f:
                    scale_v(f, p)
                if b:
                    gate_conv(b, q, 2)
                    gate_z(b, q, 0)
                    mask_scores(b, q)
                    gate_z(b, q, 1)
                if f:
                    norm_1(f, p)
                if b:
                    times_dt(b, q, 0)
                    decay_scores(b, q, 0)
                if f:
                    apply_norm_1(f, p)
                if t:
                    router_in(t, p)
                if b:
                    times_dt(b, q, 1)
                if t:
                    router_top(t, p)
                if b:
                    gated_y(b, q, 0)
                if f:
                    dt_in(f, p)
                    split_hT(f, p)
                    for n in range(5):
                        softplus(f, p, n)
                if b:
                    gated_y(b, q, 1)
                if t:
                    slots_of(t, p)
                    count_choices(p)
                if f:
                    conv(f, p, 0)
                if b:
                    mean_square(b, q)
                if f:
                    conv(f, p, 1)
                    conv(f, p, 2)
                if b:
                    residual(b, q)
                if f:
                    front.close()
                if b:
                    back.close()
                if t:
                    routing.close()

            run_batches(vc.Fori, half, PAIRS)
            dve.drain().then_inc(part_done, 1)

            dve.wait_ge(part_done, 4)
            dve.sem_inc(xe_split, 1)
            dve.sem_inc(hlo_ready, 2)
            dve.sem_inc(ye_ready, 2)
            prep.mark(vc.memset(e_now[:, :], 0.0))
            prep.wait()
            for m in range(CHUNKS // 2):
                dve.wait_ge(w_high, m + 1)
                at = slice(m * CHUNK, (m + 1) * CHUNK)
                ins = vc.tensor_tensor(w_lo[0][:, 0, at], w_raw[:, 0, at], w_hi[0][:, 0, at].bitcast(F32), ALU.subtract)
            ins.then_inc(w1_split, 1)

            def experts(r, last):
                def slot_infos(e, q):
                    ch = Chain(dve, moe_chain_sem, MOE_LINKS, e, q)
                    for loaded in xe_loaded:
                        dve.wait_ge(loaded[q], loaded.now(e, q))
                    dve.wait_ge(expert_added, e.value(2, q - 1))
                    vc.tensor_tensor(wd[q][:, :], xe[q][:, :, C_W0], xe[q][:, :, C_W0 + 1], ALU.subtract)
                    ch.mark(vc.tensor_scalar(is_first[q][:, :], xe[q][:, :, C_E0], e_now[:, :], None, ALU.is_equal))
                    ch.wait()
                    ch.mark(vc.tensor_tensor(wd[q][:, :], wd[q][:, :], is_first[q][:, :], ALU.mult))
                    ch.wait()
                    vc.tensor_tensor(w_slot[q][:, :], wd[q][:, :], xe[q][:, :, C_W0 + 1], ALU.add)
                    vc.tensor_scalar(e_now[:, :], e_now[:, :], 1.0, None, ALU.add)
                    ch.mark(vc.tensor_copy(tok_slot[q][:, :], xe[q][:, :, C_TOK].bitcast(I32)))
                    hold(dve, ch.sem, ch.value(ch.count))
                    dve.sem_inc(slot_info, 1)
                    ch.close()

                def split_x(g):
                    dve.wait_ge(xeT_psum, r * (2 * NG) + (g + 1 - 2 * NG))
                    for k in range(KD):
                        vc.tensor_copy(xe_hi[g % 2][:, k, :], x_bank[k][:, :]).then_inc(x_half, 1)
                    for k in range(KD):
                        dve.wait_ge(x_half, r * (2 * NG * KD) + (g * KD + k + 1 - 2 * NG * KD))
                        ins = vc.tensor_tensor(xe_lo[g % 2][:, k, :], x_bank[k][:, :], xe_hi[g % 2][:, k, :].bitcast(F32),
                                               ALU.subtract)
                    ins.then_inc(xe_split, 1)

                def split_h(g):
                    for m in range(KF):
                        i = KF * g + m
                        dve.wait_ge(hhi_ready, r * PER_TURN + (H_BANKS + i + 1 - PER_TURN))
                        vc.tensor_tensor(h_lo[:, m, :], hf[m % 2][:, :], h_hi[:, m, :].bitcast(F32), ALU.subtract)\
                            .then_inc(hlo_ready, 1)

                def weigh(g):
                    q, half = g // NG, g % NG
                    for b in range(2):
                        j = 4 * half + 2 * b
                        dve.wait_ge(y_psum, r * (4 * NG) + (Y0 + 2 * g + b + 1 - 4 * NG))
                        vc.tensor_tensor(ye[q][:, j:j + 2, :], y_bank[b][:, :].rearrange("p (j d) -> p j d", j=2),
                                         bc(w_slot[q][:, j:j + 2].unsqueeze(2), [P, 2, DM]), ALU.mult)\
                            .then_inc(ye_ready, 1)

                if last is None:
                    split_x(0)
                    slot_infos(Turn(1), 0)
                    return
                for g in range(2 * NG):
                    split_h(g)
                    if not (last and g + 1 == 2 * NG):
                        split_x(g + 1)
                    weigh(g)
                    if g + 1 == NG:
                        slot_infos(Turn(r), 1)
                    if g + 1 == 2 * NG and not last:
                        slot_infos(Turn(r, 1), 0)

            experts(1, None)
            run_experts(vc.Fori, experts)

        @block.tensor
        def _(pe):
            te = nc.tensor

            pe.wait_ge(s_early, 16 * N_EARLY)
            pe.wait_ge(s_masks, 1)
            for m in range(KD):
                for k in range(KD):
                    ins = te.matmul(bank[0][0][:, m * DM:(m + 1) * DM], wqk_in[:, 0, k, m * P:(m + 1) * P],
                                    wqk_in[:, 1, k, :], start=(k == 0), stop=(k == KD - 1))
            ins.then_inc(s_wqk, 1)
            pe.wait_ge(s_wqk, 2)

            def transposes(p, b, srcs):
                for n, src in enumerate(srcs):
                    ins = te.transpose(bank[p][b][:, n * P:(n + 1) * P], src, ident[:, :])
                return ins

            def half(p, f, b, t):
                def to_xT(r, p):
                    pe.wait_ge(x_ready[p], x_ready.before(r, p))
                    transposes(p, 3, [x[p][:, c, k * P:(k + 1) * P] for k in range(KD) for c in range(KD)])\
                        .then_inc(xT_psum[p], 1)

                def query_side(r, p):
                    pe.wait_ge(xT_ready[p], xT_ready.now(r, p))
                    for m in range(KD):
                        for k in range(KD):
                            ins = te.matmul(bank[p][1][:, m * L:(m + 1) * L], wqk[:, k, m * P:(m + 1) * P],
                                            xT[p][:, k, :], start=(k == 0), stop=(k == KD - 1))
                    ins.then_inc(tT_psum[p], 1)

                def values(r, p):
                    for c in range(KD):
                        for k in range(KD):
                            ins = te.matmul(bank[p][2][:, c * DM:(c + 1) * DM], xT[p][:, k, c * P:(c + 1) * P],
                                            wv[:, k, :], start=(k == 0), stop=(k == KD - 1))
                    ins.then_inc(v_psum[p], 1)

                def scores(r, p):
                    pe.wait_ge(tT_ready[p], tT_ready.now(r, p))
                    for c in range(KD):
                        for k in range(KD):
                            ins = te.matmul(bank[p][3][:, c * L:(c + 1) * L], xT[p][:, k, c * P:(c + 1) * P],
                                            tT[p][:, k, :], start=(k == 0), stop=(k == KD - 1))
                    ins.then_inc(st_psum[p], 1)

                def attend(r, p):
                    pe.wait_ge(v_ready[p], v_ready.now(r, p))
                    pe.wait_ge(h2_ready[p], h2_ready.before(r, p))
                    for c in range(KD):
                        for k in range(KD):
                            ins = te.matmul(bank[p][0][:, c * DM:(c + 1) * DM], probs[p][:, k, c * P:(c + 1) * P],
                                            v[p][:, k, :], start=(k == 0), stop=(k == KD - 1))
                    ins.then_inc(o_psum[p], 1)

                def to_hT(r, p):
                    pe.wait_ge(hn_ready[p], hn_ready.now(r, p))
                    transposes(p, 1, [hn[p][:, c, k * P:(k + 1) * P] for k in range(KD) for c in range(KD)])\
                        .then_inc(hnT_psum[p], 1)

                def project(p, dst, transposed, k, tokens_, columns, first_, last_):
                    h_hi_, h_lo_ = (t[:, k, tokens_] for t in (hT_hi[p], hT_lo[p]))
                    w_hi_, w_lo_ = (t[:, k, columns] for t in (w_in_hi, w_in_lo))
                    pairs_ = ((h_hi_, w_hi_), (h_hi_, w_lo_), (h_lo_, w_hi_))
                    for n, (h_, w_) in enumerate(pairs_):
                        ins = te.matmul(dst, *((w_, h_) if transposed else (h_, w_)), start=first_ and n == 0,
                                        stop=last_ and n == 2)
                    return ins

                def project_dt(r, p):
                    pe.wait_ge(w_in_split, 2)
                    pe.wait_ge(hT_ready[p], hT_ready.now(r, p))
                    for c in range(KD):
                        for k in range(KD):
                            ins = te.matmul(bank[p][1][:, c * NH:(c + 1) * NH], hT[p][:, k, c * P:(c + 1) * P],
                                            w_dt[:, k, :], start=(k == 0), stop=(k == KD - 1))
                    ins.then_inc(dt_psum[p], 1)

                def project_channels(r, p, i):
                    if i == 0:
                        pe.wait_ge(hT_split[p], hT_split.now(r, p))
                    if i == 0 and t:
                        pe.wait_ge(v2T_ready[p], v2T_ready.now(t, p))
                    if i == 1 and t:
                        pe.wait_ge(lg_ready[p], lg_ready.now(t, p))
                    if i == 2:
                        pe.wait_ge(hu_ready[p], hu_ready.now(r, p))
                    for h in range(2):
                        m = 2 * GROUPS[i] + h
                        for k in range(KD):
                            ins = project(p, bank[p][XBC_BANK[i]][:, h * L:(h + 1) * L], True, k, slice(0, L),
                                          slice(DI + m * P, DI + (m + 1) * P), k == 0, k == KD - 1)
                    ins.then_inc(xbc_psum[p], 1)

                def project_z(r, p, c):
                    pe.wait_ge(conv_done[p], conv_done.now(r, p, 1 if c == 0 else 3))
                    for k in range(KD):
                        ins = project(p, bank[p][Z_BANK[c]][:, :], False, k, slice(c * P, (c + 1) * P), slice(0, DI),
                                      k == 0, k == KD - 1)
                    ins.then_inc(z_psum[p], 1)

                def state_inputs(r, p):
                    pe.wait_ge(xc_ready[p], xc_ready.now(r, p, 1))
                    pe.wait_ge(conv_done[p], conv_done.now(r, p, 2))
                    pe.wait_ge(a_ready[p], a_ready.now(r, p))
                    te.transpose(bank[p][3][:, 0:P], xc[p][:, KI, 0:P], ident[:, :])
                    for c in range(KD):
                        te.matmul(bank[p][3][:, (c + 1) * P:(c + 2) * P], xc[p][:, KI, c * P:(c + 1) * P],
                                  xc[p][:, KI + 1, c * P:(c + 1) * P], start=True, stop=True)
                    te.matmul(bank[p][3][:, 3 * P:3 * P + NH], tri[:, :], a_[p][:, 1, :], start=True, stop=True)\
                        .then_inc(btg_psum[p], 1)

                def segment_sums(r, p, i):
                    c, half = i // 2, i % 2
                    pe.wait_ge(seg_in[p], seg_in.now(r, p, c + 1))
                    if i == 0:
                        pe.wait_ge(pos_taken[p], pos_taken.before(r, p))
                    if i == 1:
                        pe.wait_ge(bs_ready[p], bs_ready.now(r, p))
                        pe.wait_ge(gm_ready[p], gm_ready.now(r, p))
                    if i == 2:
                        pe.wait_ge(sz_ready[p], sz_ready.now(r, p, 2))
                    if i == 3:
                        pe.wait_ge(xs_ready[p], xs_ready.now(r, p, 1))
                        pe.wait_ge(xdt_ready[p], xdt_ready.now(r, p, 1))
                    for part in (seg_hi, seg_lo):
                        ins = te.matmul(bank[p][SEG_BANK[i]][:, :], below_r[:, :],
                                        part[p][:, c, 4 * half:4 * half + 4, :].rearrange("p h l -> p (h l)"),
                                        start=part is seg_hi, stop=part is seg_lo)
                    ins.then_inc(seg_psum[p], 1)

                def x_to_rows(r, p, c):
                    if c == 0:
                        pe.wait_ge(sz_ready[p], sz_ready.now(r, p, 1))
                        pe.wait_ge(xc_ready[p], xc_ready.now(r, p))
                    else:
                        pe.wait_ge(decay_ready[p], decay_ready.now(r, p, 1))
                    transposes(p, XS_BANK[c], [xc[p][:, m, c * P:(c + 1) * P] for m in range(KI)])\
                        .then_inc(xs_psum[p], 1)

                def chunk_state(r, p):
                    pe.wait_ge(decay_ready[p], decay_ready.now(r, p, 2))
                    pe.wait_ge(bs_ready[p], bs_ready.now(r, p))
                    pe.wait_ge(xdec_ready[p], xdec_ready.now(r, p))
                    te.matmul(bank[p][3][:, :], bs[p][:, :], xdec[p][:, :], start=True, stop=True)\
                        .then_inc(state_psum[p], 1)

                def own_chunk(r, p, c):
                    pe.wait_ge(m_ready[c][p], m_ready[c].now(r, p))
                    if c == 0:
                        pe.wait_ge(xs_ready[p], xs_ready.now(r, p, 2))
                        pe.wait_ge(xdt_ready[p], xdt_ready.now(r, p, 2))
                    for h in range(NH):
                        ins = te.matmul(bank[p][YD_BANK[c]][:, h * HD:(h + 1) * HD], seg[p][:, c, h, :],
                                        xdt[p][:, c, h * HD:(h + 1) * HD], start=True, stop=True)
                    ins.then_inc(yd_psum[p], 1)

                def from_state(r, p):
                    pe.wait_ge(st_ready[p], st_ready.now(r, p))
                    pe.wait_ge(decay_ready[p], decay_ready.now(r, p))
                    te.matmul(bank[p][2][:, :], xc[p][:, KI + 1, P:2 * P], st[p][:, :], start=True, stop=True)\
                        .then_inc(yo_psum[p], 1)

                def to_yT(r, p, c):
                    pe.wait_ge(y_ready[p], y_ready.now(r, p, c + 1))
                    transposes(p, YT_BANK[c], [y[p][:, c, k * P:(k + 1) * P] for k in range(KI)])\
                        .then_inc(yT_psum[p], 1)

                def project_out(r, p):
                    pe.wait_ge(yT_ready[p], yT_ready.now(r, p))
                    for c in range(KD):
                        for k in range(KI):
                            ins = te.matmul(bank[p][0][:, c * DM:(c + 1) * DM], yT[p][:, c, k, :], w_out[:, k, :],
                                            start=(k == 0), stop=(k == KI - 1))
                    ins.then_inc(out_psum[p], 1)

                def to_v2T(t, p):
                    pe.wait_ge(v2_ready[p], v2_ready.now(t, p))
                    if f:
                        pe.wait_ge(v_ready[p], v_ready.now(f, p))
                    transposes(p, 2, [rows[p][:, c, k * P:(k + 1) * P] for k in range(KD) for c in range(KD)])\
                        .then_inc(v2T_psum[p], 1)

                def route(t, p):
                    pe.wait_ge(v2T_ready[p], v2T_ready.now(t, p))
                    for c in range(KD):
                        for k in range(KD):
                            ins = te.matmul(bank[p][3][:, c * NE:(c + 1) * NE], v2T[p][:, k, c * P:(c + 1) * P],
                                            wr[:, k, :], start=(k == 0), stop=(k == KD - 1))
                    ins.then_inc(logit_psum[p], 1)

                def choices_before(t, p):
                    pe.wait_ge(ohs_ready[p], ohs_ready.now(t, p))
                    if f:
                        pe.wait_ge(dtn_ready[p], dtn_ready.now(f, p))
                    for c in range(KD):
                        dst = bank[p][1][:, c * NE:(c + 1) * NE]
                        te.matmul(dst, before_b[:, :], ohs[p][:, c, :], start=True, stop=False)
                        for cc in range(c):
                            te.matmul(dst, ones_b[:, :], ohs[p][:, cc, :], start=False, stop=False)
                        ins = te.matmul(dst, ones_b[:, :], oh_sum[:, :], start=False, stop=True)
                    ins.then_inc(pos_psum[p], 1)

                q = 1 - p
                if f:
                    to_xT(f, p)
                if b:
                    project_z(b, q, 0)
                if f:
                    query_side(f, p)
                    values(f, p)
                    scores(f, p)
                if b:
                    project_z(b, q, 1)
                    segment_sums(b, q, 0)
                    state_inputs(b, q)
                if f:
                    attend(f, p)
                if b:
                    x_to_rows(b, q, 0)
                    segment_sums(b, q, 1)
                    segment_sums(b, q, 2)
                if t:
                    to_v2T(t, p)
                if b:
                    segment_sums(b, q, 3)
                    x_to_rows(b, q, 1)
                if t:
                    route(t, p)
                if b:
                    chunk_state(b, q)
                if f:
                    to_hT(f, p)
                if b:
                    own_chunk(b, q, 0)
                    from_state(b, q)
                if f:
                    project_dt(f, p)
                if b:
                    own_chunk(b, q, 1)
                if f:
                    project_channels(f, p, 0)
                if b:
                    to_yT(b, q, 0)
                if t:
                    choices_before(t, p)
                if f:
                    project_channels(f, p, 1)
                if b:
                    to_yT(b, q, 1)
                if f:
                    project_channels(f, p, 2)
                if b:
                    project_out(b, q)

            run_batches(te.Fori, half, PAIRS)
            pe.drain().then_inc(part_done, 1)

            pe.wait_ge(part_done, 4)
            pe.sem_inc(y_psum, Y0)

            def three(out_, hi, lo, rhi, rlo, first_, last_):
                te.matmul(out_, hi, rhi, start=first_, stop=False)
                te.matmul(out_, hi, rlo, start=False, stop=False)
                return te.matmul(out_, lo, rhi, start=False, stop=last_)

            def experts(r, last):
                def turn_x(g):
                    q, half_ = g // NG % 2, g % NG
                    loaded = xe_loaded[half_]
                    pe.wait_ge(loaded[q], loaded.now(Turn(r, g // (2 * NG)), q))
                    pe.wait_ge(xe_split, r * (2 * NG) + (1 + g - 2 * NG))
                    for k in range(KD):
                        for j in range(4):
                            ins = te.transpose(x_bank[k][:, j * P:(j + 1) * P],
                                               xe[q][:, 4 * half_ + j, k * P:(k + 1) * P], ident[:, :])
                    ins.then_inc(xeT_psum, 1)

                def first_product(g):
                    q = g // NG
                    pe.wait_ge(w1_split, r * 2 + (q - 1))
                    pe.wait_ge(xe_split, r * (2 * NG) + (2 + g - 2 * NG))
                    for m in range(KF):
                        i = KF * g + m
                        pe.wait_ge(hhi_ready, r * PER_TURN + (i + 1 - PER_TURN))
                        for k in range(KD):
                            at = slice(k * FF + m * P, k * FF + (m + 1) * P)
                            ins = three(h_bank[i % H_BANKS][:, :], w_hi[q][:, 0, at], w_lo[q][:, 0, at],
                                        xe_hi[g % 2][:, k, :], xe_lo[g % 2][:, k, :], k == 0, k == KD - 1)
                        ins.then_inc(h_psum, 1)

                def second_product(g):
                    q = g // NG
                    pe.wait_ge(w2_split, r * 2 + (q - 1))
                    for b in range(2):
                        pe.wait_ge(ye_ready, r * (4 * NG) + (2 * g + b + 1 - 4 * NG))
                        for j in (2 * b, 2 * b + 1):
                            dst = y_bank[b][:, (j % 2) * DM:(j % 2 + 1) * DM]
                            for m in range(KF):
                                if j == 0:
                                    pe.wait_ge(hlo_ready, r * PER_TURN + (2 + KF * g + m + 1 - PER_TURN))
                                at = slice(m * DM, (m + 1) * DM)
                                ins = three(dst, h_hi[:, m, j * P:(j + 1) * P], h_lo[:, m, j * P:(j + 1) * P],
                                            w_hi[q][:, 1, at], w_lo[q][:, 1, at], m == 0, m == KF - 1)
                        ins.then_inc(y_psum, 1)

                if last is None:
                    turn_x(0)
                    return
                for g in range(2 * NG):
                    first_product(g)
                    if not (last and g + 1 == 2 * NG):
                        turn_x(g + 1)
                    second_product(g)

            experts(1, None)
            run_experts(te.Fori, experts)


def kernel(x, L0_tok_emb, L0_tok_w_q, L0_tok_w_k, L0_tok_w_v, L0_tok_pos_enc, L0_attn_ln_w, L0_attn_ln_b,
           L0_attn_in_proj_w, L0_attn_conv_w, L0_attn_conv_b, L0_attn_dt_bias, L0_attn_A_log, L0_attn_D,
           L0_attn_norm_w, L0_attn_out_proj_w, L0_ffn_w_router, L0_ffn_w1, L0_ffn_w2, L0_ffn_bias):
    import numpy as np
    import concourse.bacc as bacc
    from concourse.bass_utils import run_bass_kernel_spmd

    A = np.asarray
    x = A(x)
    nb, length = x.shape
    tokens = nb * length
    dm = A(L0_tok_emb).shape[1]
    ne, _, ff = A(L0_ffn_w1).shape

    def by_lane(a):
        a = A(a)
        return np.moveaxis(a.reshape(-1, P, *a.shape[1:]), 1, 0)

    laid_out = {
        "tokens": by_lane(x.reshape(-1)),
        "emb": A(L0_tok_emb),
        "w_qT": A(L0_tok_w_q).T, "w_kT": A(L0_tok_w_k).T, "w_v": A(L0_tok_w_v),
        "pos_enc": A(L0_tok_pos_enc)[:length],
        "ln_w": by_lane(L0_attn_ln_w), "ln_b": by_lane(L0_attn_ln_b),
        "in_wT": A(L0_attn_in_proj_w).T,
        "conv_w": by_lane(L0_attn_conv_w), "conv_b": by_lane(L0_attn_conv_b),
        "dt_bias": A(L0_attn_dt_bias)[None], "A_log": A(L0_attn_A_log)[None], "D_skip": A(L0_attn_D)[None],
        "norm_w": by_lane(L0_attn_norm_w),
        "out_wT": A(L0_attn_out_proj_w).T,
        "w_router": by_lane(L0_ffn_w_router),
        "w1": A(L0_ffn_w1).reshape(ne * dm, ff), "w2": A(L0_ffn_w2).reshape(ne * ff, dm),
        "bias": A(L0_ffn_bias).reshape(1, dm),
    }
    nc = bacc.Bacc("TRN2", target_bir_lowering=False, num_devices=1)
    arrays, aps = {}, {}
    for name, a in laid_out.items():
        arrays[name] = np.ascontiguousarray(a)
        aps[name] = nc.dram_tensor(name, a.shape, mybir.dt.from_np(a.dtype), kind="ExternalInput").ap()
    aps["out"] = nc.dram_tensor("out", (tokens + P, dm), F32, kind="ExternalOutput").ap()
    aps["slots_dram"] = nc.dram_tensor("slots_dram", (2 * tokens, dm + 4), F32).ap()
    lm_block(nc, **aps)
    r = run_bass_kernel_spmd(nc, [arrays], core_ids=[0])
    return r.results[0]["out"][:tokens].reshape(nb, length, dm)
```
